# Optimizing a Trainium2 kernel written in Bass

```python
import numpy as np
import jax
import jax.numpy as jnp

def _softmax(x, axis=-1):
    return jax.nn.softmax(x, axis=axis)

def _gelu(x):
    return jax.nn.gelu(x, approximate=True)

def _silu(x):
    return jax.nn.silu(x)

def _sigmoid(x):
    return jax.nn.sigmoid(x)

def _layernorm(x, axis=-1, eps=1e-05):
    m = jnp.mean(x, axis=axis, keepdims=True)
    v = jnp.var(x, axis=axis, keepdims=True)
    return (x - m) / jnp.sqrt(v + eps)

def _scatter_add(tgt, idx, src, axis=0):
    return tgt.at[idx].add(src)

def _segment_sum(src, seg, n):
    return jax.ops.segment_sum(src, seg, n)
kernel_name = 'mk_early_fusion_d2_tok_img768_r4_d95af8'

def setup_inputs(seed: int=0):
    np.random.seed(seed)
    _w = jnp.asarray

    def _rec_inputs():
        import jax
        import jax.numpy as jnp
        _rk = jax.random.key(seed)
        x = -0.00016672 + 0.999947 * jax.random.normal(jax.random.fold_in(_rk, 1), (8, 3, 96, 96), jnp.float32)
        txt = 0.000200627 + 0.144369 * jax.random.normal(jax.random.fold_in(_rk, 2), (8, 128, 192), jnp.float32)
        return (x, txt)
    x, txt = _rec_inputs()

    def _L0_tok_setup():
        import jax, jax.numpy as jnp
        import numpy as np
        P = 16
        EPS = 1e-05
        key = jax.random.key(seed)
        ks = jax.random.split(key, 6)
        B, C, H = (64, 3, 96)
        E = 192
        L = (H // P) ** 2
        patch_dim = C * P * P
        return {'x': jax.random.normal(ks[0], (B, C, H, H), dtype=jnp.float32), 'ln_w': jnp.ones((C, H, H), dtype=jnp.float32), 'ln_b': jnp.zeros((C, H, H), dtype=jnp.float32), 'conv_w': jax.random.normal(ks[1], (C, C, 1, 1), dtype=jnp.float32) * 0.1, 'conv_b': jax.random.normal(ks[2], (C,), dtype=jnp.float32) * 0.1, 'proj_w': jax.random.normal(ks[3], (E, patch_dim), dtype=jnp.float32) * 0.02, 'proj_b': jax.random.normal(ks[4], (E,), dtype=jnp.float32) * 0.02, 'pos_emb': jax.random.normal(ks[5], (1, L, E), dtype=jnp.float32) * 0.02}
    _L0_tok_all = _L0_tok_setup()
    _L0_tok_in = {k: v for k, v in _L0_tok_all.items() if k in ('ln_w', 'ln_b', 'conv_w', 'conv_b', 'proj_w', 'proj_b', 'pos_emb')}
    del _L0_tok_all

    def _L0_attn_setup():
        import jax, jax.numpy as jnp
        import numpy as np
        DIM = 192
        HEADS = 12
        key = jax.random.key(seed)
        k_x, k_qw, k_qb, k_pw, k_pb = jax.random.split(key, 5)
        x = jax.random.normal(k_x, (4, 512, DIM), dtype=jnp.float32)
        s = 1.0 / np.sqrt(DIM)
        qkv_w = jax.random.uniform(k_qw, (3 * DIM, DIM), jnp.float32, -s, s)
        qkv_b = jax.random.uniform(k_qb, (3 * DIM,), jnp.float32, -s, s)
        proj_w = jax.random.uniform(k_pw, (DIM, DIM), jnp.float32, -s, s)
        proj_b = jax.random.uniform(k_pb, (DIM,), jnp.float32, -s, s)
        return {'x': x, 'qkv_w': qkv_w, 'qkv_b': qkv_b, 'proj_w': proj_w, 'proj_b': proj_b}
    _L0_attn_all = _L0_attn_setup()
    _L0_attn_in = {k: v for k, v in _L0_attn_all.items() if k in ('qkv_w', 'qkv_b', 'proj_w', 'proj_b')}
    del _L0_attn_all

    def _L0_ffn_setup():
        import jax, jax.numpy as jnp
        import numpy as np
        DIM = 192
        MOE_INTER = 512
        N_EXPERTS = 16
        TOP_K = 2
        SHARED_INTER = 2 * 512
        ROUTE_SCALE = 1.0
        B, S = (8, 196)
        key = jax.random.key(seed)
        ks = jax.random.split(key, 8)
        sc = 0.02
        return {'x': jax.random.normal(ks[0], (B, S, DIM), jnp.float32), 'gate_w': jax.random.normal(ks[1], (N_EXPERTS, DIM), jnp.float32) * sc, 'w1': jax.random.normal(ks[2], (N_EXPERTS, MOE_INTER, DIM), jnp.float32) * sc, 'w2': jax.random.normal(ks[3], (N_EXPERTS, DIM, MOE_INTER), jnp.float32) * sc, 'w3': jax.random.normal(ks[4], (N_EXPERTS, MOE_INTER, DIM), jnp.float32) * sc, 'sw1': jax.random.normal(ks[5], (SHARED_INTER, DIM), jnp.float32) * sc, 'sw2': jax.random.normal(ks[6], (DIM, SHARED_INTER), jnp.float32) * sc, 'sw3': jax.random.normal(ks[7], (SHARED_INTER, DIM), jnp.float32) * sc}
    _L0_ffn_all = _L0_ffn_setup()
    _L0_ffn_in = {k: v for k, v in _L0_ffn_all.items() if k in ('gate_w', 'w1', 'w2', 'w3', 'sw1', 'sw2', 'sw3')}
    del _L0_ffn_all

    def _L1_attn_setup():
        import jax, jax.numpy as jnp
        import numpy as np
        INIT_RANGE = 0.02
        key = jax.random.key(seed)
        ks = jax.random.split(key, 5)
        B, S, D, H, Dh = (4, 512, 192, 12, 64)
        residual = jax.random.normal(ks[0], (B, S, D), dtype=jnp.float32)
        W_Q = jax.random.normal(ks[1], (H, D, Dh), dtype=jnp.float32) * INIT_RANGE
        W_K = jax.random.normal(ks[2], (H, D, Dh), dtype=jnp.float32) * INIT_RANGE
        W_V = jax.random.normal(ks[3], (H, D, Dh), dtype=jnp.float32) * INIT_RANGE
        W_O = jax.random.normal(ks[4], (H, Dh, D), dtype=jnp.float32) * INIT_RANGE
        b_Q = jnp.zeros((H, Dh), dtype=jnp.float32)
        b_K = jnp.zeros((H, Dh), dtype=jnp.float32)
        b_V = jnp.zeros((H, Dh), dtype=jnp.float32)
        b_O = jnp.zeros((D,), dtype=jnp.float32)
        return {'residual': residual, 'W_Q': W_Q, 'W_K': W_K, 'W_V': W_V, 'W_O': W_O, 'b_Q': b_Q, 'b_K': b_K, 'b_V': b_V, 'b_O': b_O}
    _L1_attn_all = _L1_attn_setup()
    _L1_attn_in = {k: v for k, v in _L1_attn_all.items() if k in ('W_Q', 'W_K', 'W_V', 'W_O', 'b_Q', 'b_K', 'b_V', 'b_O')}
    del _L1_attn_all

    def _L1_ffn_setup():
        import jax, jax.numpy as jnp
        import numpy as np
        B, S, D = (4, 256, 192)
        E = 8
        H = 192
        HS = 768
        TOPK_ROUTED = 2
        key = jax.random.key(seed)
        ks = jax.random.split(key, 10)
        w = lambda k, shape: jax.random.normal(k, shape, dtype=jnp.float32) * 0.02
        return {'x': jax.random.normal(ks[0], (B, S, D), dtype=jnp.float32), 'router_w': w(ks[1], (D, E)), 'w_gate': w(ks[2], (E, D, H)), 'w_up': w(ks[3], (E, D, H)), 'w_down': w(ks[4], (E, H, D)), 'ws_gate': w(ks[5], (D, HS)), 'ws_up': w(ks[6], (D, HS)), 'ws_down': w(ks[7], (HS, D)), 'sg_w': w(ks[8], (D, 1)), 'sg_b': jnp.zeros((1,), jnp.float32)}
    _L1_ffn_all = _L1_ffn_setup()
    _L1_ffn_in = {k: v for k, v in _L1_ffn_all.items() if k in ('router_w', 'w_gate', 'w_up', 'w_down', 'ws_gate', 'ws_up', 'ws_down', 'sg_w', 'sg_b')}
    del _L1_ffn_all
    return {'x': x, 'txt': txt, 'L0_tok_ln_w': _L0_tok_in['ln_w'], 'L0_tok_ln_b': _L0_tok_in['ln_b'], 'L0_tok_conv_w': _L0_tok_in['conv_w'], 'L0_tok_conv_b': _L0_tok_in['conv_b'], 'L0_tok_proj_w': _L0_tok_in['proj_w'], 'L0_tok_proj_b': _L0_tok_in['proj_b'], 'L0_tok_pos_emb': _L0_tok_in['pos_emb'], 'L0_attn_qkv_w': _L0_attn_in['qkv_w'], 'L0_attn_qkv_b': _L0_attn_in['qkv_b'], 'L0_attn_proj_w': _L0_attn_in['proj_w'], 'L0_attn_proj_b': _L0_attn_in['proj_b'], 'L0_ffn_gate_w': _L0_ffn_in['gate_w'], 'L0_ffn_w1': _L0_ffn_in['w1'], 'L0_ffn_w2': _L0_ffn_in['w2'], 'L0_ffn_w3': _L0_ffn_in['w3'], 'L0_ffn_sw1': _L0_ffn_in['sw1'], 'L0_ffn_sw2': _L0_ffn_in['sw2'], 'L0_ffn_sw3': _L0_ffn_in['sw3'], 'L1_attn_W_Q': _L1_attn_in['W_Q'], 'L1_attn_W_K': _L1_attn_in['W_K'], 'L1_attn_W_V': _L1_attn_in['W_V'], 'L1_attn_W_O': _L1_attn_in['W_O'], 'L1_attn_b_Q': _L1_attn_in['b_Q'], 'L1_attn_b_K': _L1_attn_in['b_K'], 'L1_attn_b_V': _L1_attn_in['b_V'], 'L1_attn_b_O': _L1_attn_in['b_O'], 'L1_ffn_router_w': _L1_ffn_in['router_w'], 'L1_ffn_w_gate': _L1_ffn_in['w_gate'], 'L1_ffn_w_up': _L1_ffn_in['w_up'], 'L1_ffn_w_down': _L1_ffn_in['w_down'], 'L1_ffn_ws_gate': _L1_ffn_in['ws_gate'], 'L1_ffn_ws_up': _L1_ffn_in['ws_up'], 'L1_ffn_ws_down': _L1_ffn_in['ws_down'], 'L1_ffn_sg_w': _L1_ffn_in['sg_w'], 'L1_ffn_sg_b': _L1_ffn_in['sg_b']}

def reference(x, txt, L0_tok_ln_w, L0_tok_ln_b, L0_tok_conv_w, L0_tok_conv_b, L0_tok_proj_w, L0_tok_proj_b, L0_tok_pos_emb, L0_attn_qkv_w, L0_attn_qkv_b, L0_attn_proj_w, L0_attn_proj_b, L0_ffn_gate_w, L0_ffn_w1, L0_ffn_w2, L0_ffn_w3, L0_ffn_sw1, L0_ffn_sw2, L0_ffn_sw3, L1_attn_W_Q, L1_attn_W_K, L1_attn_W_V, L1_attn_W_O, L1_attn_b_Q, L1_attn_b_K, L1_attn_b_V, L1_attn_b_O, L1_ffn_router_w, L1_ffn_w_gate, L1_ffn_w_up, L1_ffn_w_down, L1_ffn_ws_gate, L1_ffn_ws_up, L1_ffn_ws_down, L1_ffn_sg_w, L1_ffn_sg_b):
    import jax
    import jax.numpy as jnp

    def _L0_tok_ref(x, ln_w, ln_b, conv_w, conv_b, proj_w, proj_b, pos_emb):
        import jax, jax.numpy as jnp
        import numpy as np
        P = 16
        EPS = 1e-05
        B, C, H, W = x.shape
        mu = jnp.mean(x, axis=(1, 2, 3), keepdims=True)
        var = jnp.var(x, axis=(1, 2, 3), keepdims=True)
        xn = (x - mu) * jax.lax.rsqrt(var + EPS) * ln_w + ln_b
        w = conv_w[:, :, 0, 0]
        xc = jnp.einsum('bchw,oc->bohw', xn, w) + conv_b[None, :, None, None]
        hp, wp = (H // P, W // P)
        patches = xc.reshape(B, C, hp, P, wp, P)
        patches = patches.transpose(0, 2, 4, 1, 3, 5).reshape(B, hp * wp, C * P * P)
        tokens = jnp.einsum('bld,ed->ble', patches, proj_w) + proj_b
        return tokens + pos_emb

    def _L0_attn_ref(x, qkv_w, qkv_b, proj_w, proj_b):
        import jax, jax.numpy as jnp
        import numpy as np
        DIM = 192
        HEADS = 12
        B, N, C = x.shape
        H = HEADS
        D = C // H
        scale = D ** (-0.5)
        qkv = x @ qkv_w.T + qkv_b
        qkv = qkv.reshape(B, N, 3, H, D).transpose(2, 0, 3, 1, 4)
        q, k, v = (qkv[0], qkv[1], qkv[2])
        attn = jnp.einsum('bhnd,bhmd->bhnm', q, k) * scale
        attn = jax.nn.softmax(attn, axis=-1)
        out = jnp.einsum('bhnm,bhmd->bhnd', attn, v)
        out = out.transpose(0, 2, 1, 3).reshape(B, N, C)
        return out @ proj_w.T + proj_b

    def _L0_ffn_ref(x, gate_w, w1, w2, w3, sw1, sw2, sw3):
        import jax, jax.numpy as jnp
        import numpy as np
        DIM = 192
        MOE_INTER = 512
        N_EXPERTS = 16
        TOP_K = 2
        SHARED_INTER = 2 * 512
        ROUTE_SCALE = 1.0
        B, S = (8, 196)
        Bb, Ss, D = x.shape
        xf = x.reshape(-1, D)
        T = xf.shape[0]
        scores = jax.nn.softmax(xf @ gate_w.T, axis=-1)
        topw, topi = jax.lax.top_k(scores, TOP_K)
        topw = topw * ROUTE_SCALE
        comb = jnp.zeros((T, N_EXPERTS), xf.dtype).at[jnp.arange(T)[:, None], topi].set(topw)
        h = jax.nn.silu(jnp.einsum('td,eid->tei', xf, w1)) * jnp.einsum('td,eid->tei', xf, w3)
        h = h * comb[:, :, None]
        y = jnp.einsum('tei,edi->td', h, w2)
        z = jax.nn.silu(xf @ sw1.T) * (xf @ sw3.T) @ sw2.T
        return (y + z).reshape(Bb, Ss, D)

    def _L1_attn_ref(residual, W_Q, W_K, W_V, W_O, b_Q, b_K, b_V, b_O):
        import jax, jax.numpy as jnp
        import numpy as np
        INIT_RANGE = 0.02
        d_head = W_Q.shape[-1]
        q = jnp.einsum('bsd,hde->bshe', residual, W_Q) + b_Q
        k = jnp.einsum('bsd,hde->bshe', residual, W_K) + b_K
        v = jnp.einsum('bsd,hde->bshe', residual, W_V) + b_V
        scores = jnp.einsum('bqhe,bkhe->bhqk', q, k) / jnp.sqrt(jnp.float32(d_head))
        S = residual.shape[1]
        causal = jnp.tril(jnp.ones((S, S), dtype=bool))
        scores = jnp.where(causal, scores, -jnp.inf)
        pattern = jax.nn.softmax(scores, axis=-1)
        z = jnp.einsum('bkhe,bhqk->bqhe', v, pattern)
        attn_out = jnp.einsum('bqhe,hed->bqd', z, W_O) + b_O
        return attn_out

    def _L1_ffn_ref(x, router_w, w_gate, w_up, w_down, ws_gate, ws_up, ws_down, sg_w, sg_b):
        import jax, jax.numpy as jnp
        import numpy as np
        B, S, D = (4, 256, 192)
        E = 8
        H = 192
        HS = 768
        TOPK_ROUTED = 2
        probs = jax.nn.softmax(x @ router_w, axis=-1)
        gates, idx = jax.lax.top_k(probs, TOPK_ROUTED)
        gates = gates / jnp.sum(gates, axis=-1, keepdims=True)
        n_exp = router_w.shape[1]
        dense_g = jnp.sum(jax.nn.one_hot(idx, n_exp, dtype=x.dtype) * gates[..., None], axis=-2)
        g = jax.nn.silu(jnp.einsum('bsd,edh->bseh', x, w_gate))
        u = jnp.einsum('bsd,edh->bseh', x, w_up)
        expert_out = jnp.einsum('bseh,ehd->bsed', g * u, w_down)
        routed = jnp.einsum('bse,bsed->bsd', dense_g, expert_out)
        shared = jax.nn.silu(x @ ws_gate) * (x @ ws_up) @ ws_down
        alpha = jax.nn.sigmoid(x @ sg_w + sg_b)
        return alpha * shared + (1.0 - alpha) * routed
    h = _L0_tok_ref(x, L0_tok_ln_w, L0_tok_ln_b, L0_tok_conv_w, L0_tok_conv_b, L0_tok_proj_w, L0_tok_proj_b, L0_tok_pos_emb)
    h = jnp.concatenate([h, txt], axis=1)
    h = h + _L0_attn_ref(_layernorm(h, axis=-1), L0_attn_qkv_w, L0_attn_qkv_b, L0_attn_proj_w, L0_attn_proj_b)
    h = h + _L0_ffn_ref(_layernorm(h, axis=-1), L0_ffn_gate_w, L0_ffn_w1, L0_ffn_w2, L0_ffn_w3, L0_ffn_sw1, L0_ffn_sw2, L0_ffn_sw3)
    h = h + _L1_attn_ref(_layernorm(h, axis=-1), L1_attn_W_Q, L1_attn_W_K, L1_attn_W_V, L1_attn_W_O, L1_attn_b_Q, L1_attn_b_K, L1_attn_b_V, L1_attn_b_O)
    h = h + _L1_ffn_ref(_layernorm(h, axis=-1), L1_ffn_router_w, L1_ffn_w_gate, L1_ffn_w_up, L1_ffn_w_down, L1_ffn_ws_gate, L1_ffn_ws_up, L1_ffn_ws_down, L1_ffn_sg_w, L1_ffn_sg_b)
    return h

_drawn_inputs = setup_inputs


def setup_inputs(seed=0):
    import zlib

    import numpy as np

    out = dict(_drawn_inputs(seed))
    spreads = {'L0_tok_ln_w': (1.0, 0.2),
     'L0_tok_ln_b': (0.0, 0.271),
     'L1_attn_b_Q': (0.0, 0.8),
     'L1_attn_b_K': (0.0, 2.0),
     'L1_attn_b_V': (0.0, 0.1),
     'L1_attn_b_O': (0.0, 0.1)}
    factors = {'L0_ffn_gate_w': 5.018,
     'L0_ffn_w1': 5.066,
     'L0_ffn_w2': 4.96,
     'L0_ffn_w3': 5.003,
     'L1_attn_W_Q': 8.0,
     'L1_attn_W_K': 7.807,
     'L1_ffn_router_w': 3.63,
     'L1_ffn_w_gate': 3.301,
     'L1_ffn_w_up': 3.38,
     'L1_ffn_w_down': 3.328,
     'L1_ffn_sg_w': 8.0,
     'L1_ffn_ws_gate': 5.139,
     'L1_ffn_ws_up': 5.071,
     'L1_ffn_ws_down': 5.081}
    for name, (base, spread) in spreads.items():
        noise = np.random.default_rng([zlib.crc32(name.encode()), seed]).standard_normal(out[name].shape)
        drawn = base * np.exp(spread * noise) if base else spread * noise
        out[name] = jnp.asarray(drawn.astype(out[name].dtype))
    for name, factor in factors.items():
        out[name] = (out[name] * factor).astype(out[name].dtype)
    return out
```

```python
from contextlib import ExitStack

import concourse.bass as bass
from concourse import mybir

ALU = mybir.AluOpType
ACT = mybir.ActivationFunctionType
AX = mybir.AxisListType
F32 = mybir.dt.float32
BF16 = mybir.dt.bfloat16
I32 = mybir.dt.int32
U32 = mybir.dt.uint32
ds = bass.ds

B = 8
D = 192
KC = 96
NP = 36
TXT = 128
N = NP + TXT
P = N // 2
T = 2 * B
HEADS = 12
EPS = 1e-5
G = 3
PAIRS = HEADS // G
SLOTS = 128
ACCROSS = 11


class Shapes:
    pass


class Signals:
    pass


def layer_shapes(layer):
    s = Shapes()
    s.dh = (16, 64)[layer]
    s.stride = (32, 64)[layer]
    s.chunks = (3, 6)[layer]
    s.causal = (False, True)[layer]
    s.scale = s.dh ** -0.5
    s.e = (16, 8)[layer]
    s.hidden = (512, 192)[layer]
    s.mc = (128, 96)[layer]
    s.shared = (1024, 768)[layer]
    s.gate = (False, True)[layer]
    s.width = s.stride * HEADS
    s.vwidth = s.dh * HEADS
    s.per_chunk = 128 // s.stride
    s.qk_jobs = 2 * s.chunks // 3
    s.v_parts = (1, 2)[layer]
    s.v_cols = s.vwidth // s.v_parts
    s.proj_jobs = s.qk_jobs + 2 * s.v_parts
    s.jobs = s.proj_jobs + 2 * PAIRS
    s.o_banks = s.chunks // 3
    s.ew = s.e + (1 if s.gate else 0)
    if layer == 0:
        s.order = [g + 4 * n for g in range(PAIRS) for n in range(G)]
    else:
        s.order = [6 * (g // 2) + g % 2 + 2 * n for g in range(PAIRS) for n in range(G)]
    s.nch = s.hidden // s.mc
    s.sch = s.shared // 128
    s.s_jobs = s.sch // 2
    s.nt = (2 * B * N + s.e * (SLOTS - 1)) // SLOTS
    assert s.jobs % 4 == 0 and s.nt % 2 == 0
    return s


C_ID = 0
C_TRI = C_ID + 128
C_M0 = C_TRI + P
C_M1 = C_M0 + P
C_STEP = C_M1 + N
C_TILE = C_STEP + ACCROSS
C_DESC = [C_TILE + 36, C_TILE + 36 + 16]
C_BEF = [C_DESC[1] + 8, C_DESC[1] + 8 + 256]
C_ALL = C_BEF[1] + 64


def build(nc, a, out):
    L = [layer_shapes(0), layer_shapes(1)]
    with ExitStack() as ctx:
        def sb(name, shape, dt=F32):
            return ctx.enter_context(nc.sbuf_tensor(name, shape, dt))

        def sem(name):
            return ctx.enter_context(nc.semaphore(name))

        ps = ctx.enter_context(nc.psum_tensor("ps", [128, 8, 512], F32))
        RING, PSE, PSO, PSA = 0, 4, 6, 7

        H = sb("H", [P, T, D])
        XN = sb("XN", [P, T, D])
        XT = sb("XT", [KC, 2, B * N])
        consts = sb("consts", [128, C_ALL])
        ident = consts[:, C_ID:C_ID + 128]
        ident_b = sb("ident_b", [P, P], BF16)
        mask_b = [sb("mask0_b", [P, G, P], BF16), sb("mask1_b", [P, G, N], BF16)]
        ones = sb("ones", [128, 128])
        zeros = sb("zeros", [128, 6 * D])
        half = sb("half", [128, 16])
        eps2 = sb("eps2", [P, 2])
        carrier = sb("carrier", [P, 2])
        wqk = sb("wqk", [KC + 1, 2, 2 * 768])
        wv = sb("wv", [KC + 1, 2, 768])
        wo = sb("wo", [128, 6, D])
        bo = sb("bo", [1, D])
        wr = sb("wr", [KC + 1, 2, 16])
        stats = sb("stats", [P, 2, 6])
        mv = sb("mv", [P, 2, 2])
        ve = sb("ve", [P, 2])
        rstd = sb("rstd", [P, 2])
        xn = sb("xn", [P, 2, D])
        xT = sb("xT", [KC + 1, 2, N])
        stats2 = sb("stats2", [P, 2, 6])
        mv2 = sb("mv2", [P, 2, 2])
        ve2 = sb("ve2", [P, 2])
        rstd2 = sb("rstd2", [P, 2])
        xn2 = sb("xn2", [P, 2, D])
        xT2 = sb("xT2", [KC + 1, 2, N])
        qT = sb("qT", [128, HEADS, N])
        kT = sb("kT", [128, 6, N])
        V = [sb(f"V{u}", [P, 2, 768]) for u in range(2)]
        top = sb("top", [P, 4, G])
        nb = sb("nb", [P, 4, G])
        sums = sb("sums", [P, 2, 2 * G])
        rsum = sb("rsum", [P, 2, 2 * G])
        Ex = [sb(f"Ex{i}", [P, 2, G, N]) for i in range(2)]
        ET = [sb(f"ET{i}", [P, 2, N]) for i in range(2)]
        OT = sb("OT", [128, 6, N])
        LG = sb("LG", [P, T, 17])
        wg = sb("wg", [KC, 2, 1024])
        wu = sb("wu", [KC, 2, 1024])
        wd = sb("wd", [128, 8, D])
        sg = [sb(f"sg{i}", [128, 512]) for i in range(2)]
        gT = [sb(f"gT{i}", [128, 8, N]) for i in range(2)]
        w13_whole = [sb(f"w13_{i}", [128, 2, 1024]) for i in range(2)]
        w13 = [x[0:KC, :, :] for x in w13_whole]
        w2 = [sb(f"w2_{i}", [128, 4, D]) for i in range(2)]
        xs = [sb(f"xs{i}", [SLOTS, D]) for i in range(2)]
        xsT = [sb(f"xsT{i}", [KC, 2, SLOTS]) for i in range(2)]
        hg = [sb(f"hg{i}", [128, 4, SLOTS]) for i in range(2)]
        ys = [sb(f"ys{i}", [SLOTS, D]) for i in range(2)]
        yg = [sb(f"yg{i}", [P, 2, D]) for i in range(4)]
        E16 = 16
        r_mx = sb("r_mx", [P, T])
        r_p = sb("r_p", [P, T, E16])
        r_q = sb("r_q", [P, T, E16])
        r_sm = sb("r_sm", [P, T])
        r_eq = sb("r_eq", [P, T, E16])
        r_v = sb("r_v", [P, T, E16])
        r_vm = sb("r_vm", [P, T])
        onehot = [sb(f"onehot{i}", [P, T, E16]) for i in range(2)]
        chosen = sb("chosen", [P, T, E16])
        gate = [sb(f"gate{i}", [P, T]) for i in range(2)]
        scan = [sb(f"scan{i}", [P, 9 + T, E16]) for i in range(2)]
        count = sb("count", [P, E16])
        r_cmp = sb("r_cmp", [P, E16, ACCROSS])
        tiles = sb("tiles", [P, E16])
        r_bef = sb("r_bef", [P, E16, E16])
        base = sb("base", [P, E16])
        last = sb("last", [P, E16])
        r_id = sb("r_id", [1, 36, E16])
        idf = sb("idf", [1, 36])
        expert = [sb(f"expert{i}", [1, 36], I32) for i in range(2)]
        pos = sb("pos", [P, T, E16])
        slotf = sb("slotf", [P, T])
        slot = [sb(f"slot{i}", [P, T], U32) for i in range(2)]
        alpha = sb("alpha", [P, T])
        first, second = (x[:, :, :].rearrange("p k n -> p (k n)") for x in w13_whole)
        xp = first[:, 0:B * 6 * NP].rearrange("p (b n) -> p b n", b=B)
        pf = second[:, 0:6 * D].rearrange("p (j d) -> p j d", j=6)
        at = 6 * D
        lnw, lnb, junk = (second[:, at + n * 6 * NP:at + (n + 1) * 6 * NP] for n in range(3))
        at += 3 * 6 * NP
        cbr = second[:, at:at + 3 * NP].rearrange("p (o n) -> p o n", o=3)
        pw = wd[:, 0:6, :]
        cw = sb("cw", [128, 9])
        cb = sb("cb", [128, 3])
        pos_emb = sb("pos_emb", [NP, D])
        pb = sb("pb", [NP, D])
        psum1 = sb("psum1", [128, B])
        mean = sb("mean", [128, B])
        sq = sb("sq", [128, B])
        vt = sb("vt", [128, B])
        rs = sb("rs", [128, B])
        cmat = sb("cmat", [NP, D])

        Xs = [nc.dram_tensor(f"sorted_rows{i}", (L[i].nt * SLOTS, D), F32, kind="Internal").ap() for i in range(2)]
        Ys = [nc.dram_tensor(f"expert_out{i}", (L[i].nt * SLOTS, D), F32, kind="Internal").ap() for i in range(2)]

        ld_x = sem("ld_x"); ld_tok = sem("ld_tok"); ld_txt = sem("ld_txt"); ld_const = sem("ld_const")
        const_made = sem("const_made")
        tk = sem("tk"); tk_sum = sem("tk_sum"); tk_tot = sem("tk_tot"); tk_sq = sem("tk_sq")
        tk_rs = sem("tk_rs"); tk_fold = sem("tk_fold"); tk_mm = sem("tk_mm"); tk_done = sem("tk_done")
        zero_fill = sem("zero_fill")
        stored = sem("stored")

        def layer_signals(i):
            m = Signals()
            m.ld_att = sem(f"ld_att_L{i}")
            m.ld_shared = sem(f"ld_shared_L{i}")
            m.st = sem(f"st_L{i}")
            m.mvr = sem(f"mvr_L{i}")
            m.ve_c = sem(f"ve_c_L{i}")
            m.rs = sem(f"rs_L{i}")
            m.xn = sem(f"xn_L{i}")
            m.xnT = sem(f"xnT_L{i}")
            m.xT = sem(f"xT_L{i}")
            m.ring_full = sem(f"ring_full_L{i}")
            m.proj_used = sem(f"proj_used_L{i}")
            m.scores_used = sem(f"scores_used_L{i}")
            m.cleared = sem(f"cleared_L{i}")
            m.nbc = sem(f"nbc_L{i}")
            m.nb = sem(f"nb_L{i}")
            m.rsc = sem(f"rsc_L{i}")
            m.e_norm = sem(f"e_norm_L{i}")
            m.eT_full = sem(f"eT_full_L{i}")
            m.eT_copied = sem(f"eT_copied_L{i}")
            m.pv = sem(f"pv_L{i}")
            m.o_copied = sem(f"o_copied_L{i}")
            m.outp = sem(f"outp_L{i}")
            m.resid = sem(f"resid_L{i}")
            m.st2 = sem(f"st2_L{i}")
            m.mv2r = sem(f"mv2r_L{i}")
            m.ve2_c = sem(f"ve2_c_L{i}")
            m.rs2 = sem(f"rs2_L{i}")
            m.xn2 = sem(f"xn2_L{i}")
            m.xn2T = sem(f"xn2T_L{i}")
            m.xT2 = sem(f"xT2_L{i}")
            m.router = sem(f"router_L{i}")
            m.logits = sem(f"logits_L{i}")
            m.xn_saved = sem(f"xn_saved_L{i}")
            m.xT_saved = sem(f"xT_saved_L{i}")
            m.r = sem(f"r_L{i}")
            m.r_exp = sem(f"r_exp_L{i}")
            m.oh_made = sem(f"oh_made_L{i}")
            m.rank = sem(f"rank_L{i}")
            m.slots = sem(f"slots_L{i}")
            m.tile_ids = sem(f"tile_ids_L{i}")
            m.scat = sem(f"scat_L{i}")
            m.gu_full = sem(f"gu_full_L{i}")
            m.silu = sem(f"silu_L{i}")
            m.gu_used = sem(f"gu_used_L{i}")
            m.d_full = sem(f"d_full_L{i}")
            m.d_used = sem(f"d_used_L{i}")
            m.xs0 = sem(f"xs0_L{i}")
            m.xs1 = sem(f"xs1_L{i}")
            m.w13_0 = sem(f"w13_0_L{i}")
            m.w13_1 = sem(f"w13_1_L{i}")
            m.w2_0 = sem(f"w2_0_L{i}")
            m.w2_1 = sem(f"w2_1_L{i}")
            m.xs_T = sem(f"xs_T_L{i}")
            m.xsT_made = sem(f"xsT_made_L{i}")
            m.h_full = sem(f"h_full_L{i}")
            m.silu2 = sem(f"silu2_L{i}")
            m.hg_made = sem(f"hg_made_L{i}")
            m.y_full = sem(f"y_full_L{i}")
            m.y_copied = sem(f"y_copied_L{i}")
            m.y_st0 = sem(f"y_st0_L{i}")
            m.y_st1 = sem(f"y_st1_L{i}")
            m.gath0 = sem(f"gath0_L{i}")
            m.gath1 = sem(f"gath1_L{i}")
            m.gath2 = sem(f"gath2_L{i}")
            m.gath3 = sem(f"gath3_L{i}")
            m.comb = sem(f"comb_L{i}")
            return m

        S = [layer_signals(0), layer_signals(1)]
        block = ctx.enter_context(nc.Block())

        def klen(c, s):
            return P if c.causal and s == 0 else N

        @block.sync
        def _(sp):
            sp.dma_start(xp, a["xp"]).then_inc(ld_x, 16)
            sp.dma_start(consts[:], a["consts"]).then_inc(ld_const, 16)
            for dst, name in ((pw, "proj_t"), (cw[:], "conv_w"), (cb[:], "conv_b"), (lnw, "ln_w"),
                              (lnb, "ln_b"), (pos_emb[:], "pos_emb"), (pb[:], "proj_b")):
                sp.dma_start(dst, a[name]).then_inc(ld_tok, 16)
            head_rows = P - NP
            sp.dma_start(H[NP:P, 0:T:2, :], a["txt"][:, 0:head_rows, :].rearrange("b p d -> p b d")).then_inc(ld_txt, 16)
            sp.dma_start(H[:, 1:T:2, :], a["txt"][:, head_rows:TXT, :].rearrange("b p d -> p b d")).then_inc(ld_txt, 16)

            def load_attention(i):
                c, m = L[i], S[i]
                for dst, name in ((wqk[:, :, 0:2 * c.width], "wqk"), (wv[:, :, 0:c.vwidth], "wv"),
                                  (wo[:, 0:c.chunks, :], "wo"), (bo[:], "bo"), (wr[:, :, 0:c.ew], "wr")):
                    sp.dma_start(dst, a[f"{name}{i}"]).then_inc(m.ld_att, 16)

            def load_shared(i):
                c, m = L[i], S[i]
                for dst, name in ((wg[:, :, 0:c.shared], "wg"), (wu[:, :, 0:c.shared], "wu"), (wd[:, 0:c.sch, :], "wd")):
                    sp.dma_start(dst, a[f"{name}{i}"]).then_inc(m.ld_shared, 16)

            def load_experts(i):
                c, m = L[i], S[i]
                sp.wait_ge(m.tile_ids, 1)

                def weights(j, u, first):
                    if not first:
                        sp.wait_ge(m.h_full, j - 1)
                    e = sp.value_load(expert[i][0:1, ds(j, 1)], min_val=0, max_val=c.e - 1)
                    sp.dma_start(w13[u][:, :, 0:2 * c.hidden], a[f"w13_{i}"][ds(e, 1)].rearrange("e p k n -> p (e k) n")).then_inc((m.w13_0, m.w13_1)[u], 16)
                    if not first:
                        sp.wait_ge(m.y_full, j - 1)
                    sp.dma_start(w2[u][0:c.mc, 0:c.nch, :], a[f"w2_{i}"][ds(e, 1)].rearrange("e p k n -> p (e k) n")).then_inc((m.w2_0, m.w2_1)[u], 16)

                def rows(j, u, first):
                    if not first:
                        sp.wait_ge(m.xs_T, j - 1)
                    sp.dma_start(xs[u][:], Xs[i][ds(j * SLOTS, SLOTS), :]).then_inc((m.xs0, m.xs1)[u], 16)

                for u in range(2):
                    weights(u, u, True)
                sp.wait_ge(m.scat, 16 * 2 * T)
                for u in range(2):
                    rows(u, u, True)
                with sp.Fori(1, c.nt // 2) as k:
                    for u in range(2):
                        rows(2 * k + u, u, False)
                        weights(2 * k + u, u, False)

            load_attention(0)
            sp.wait_ge(tk_mm, 1)
            sp.wait_ge(tk, 1 + B + 9)
            load_shared(0)
            sp.wait_ge(const_made, 3)
            for i in range(2):
                flat = Xs[i].rearrange("(p n) d -> p (n d)", p=128)
                w = flat.shape[1]
                step = 6 * D
                for o in range(0, w, step):
                    n = min(step, w - o)
                    sp.dma_start(flat[:, o:o + n], zeros[:, 0:n]).then_inc(zero_fill, 16)
            sp.wait_ge(S[0].router, B)
            load_attention(1)
            load_experts(0)
            sp.wait_ge(S[0].d_full, T)
            load_shared(1)
            load_experts(1)
            for t in range(T):
                sp.wait_ge(S[1].comb, 2 * t + 2)
                b, s = divmod(t, 2)
                sp.dma_start(out[b, s * P:(s + 1) * P, :], H[:, t, :]).then_inc(stored, 16)
            sp.wait_ge(stored, 16 * T)

        @block.tensor
        def _(pe):
            def mm(o, l, r, start=True, stop=True):
                return nc.tensor.matmul(o, l, r, start=start, stop=stop, skip_group_check=True)

            pe.wait_ge(const_made, 1)
            pe.wait_ge(tk_sum, 1)
            mm(ps[:, 0, 0:B], ones[:, :], psum1[:, :]).then_inc(tk_tot, 1)
            pe.wait_ge(tk_sq, B)
            mm(ps[:, 0, 16:16 + B], ones[:, :], sq[:, :]).then_inc(tk_tot, 1)
            pe.wait_ge(tk_fold, 1)
            for j in range(6):
                last_c = mm(ps[0:NP, 1, 0:D], cbr[:, j // 2, :], pw[:, j, :], start=(j == 0), stop=(j == 5))
            last_c.then_inc(tk_mm, 1)
            pe.wait_ge(tk_fold, 2)
            for b in range(B):
                for j in range(6):
                    last_c = mm(ps[0:NP, 2 + b // 2, (b % 2) * D:(b % 2 + 1) * D],
                                xp[:, b, j * NP:(j + 1) * NP], pf[:, j, :], start=(j == 0), stop=(j == 5))
                last_c.then_inc(tk_mm, 1)

            def attention(i):
                c, m = L[i], S[i]
                pq = c.per_chunk

                def turn_x(b):
                    pe.wait_ge(m.xn, 2 * b + 2)
                    for s in range(2):
                        for k in range(2):
                            t_ = nc.tensor.transpose(ps[0:KC, PSA, k * N + s * P:k * N + (s + 1) * P],
                                                     xn[:, s, k * KC:(k + 1) * KC], ident[0:P, 0:P])
                    t_.then_inc(m.xnT, 1)

                def ring(b, first, job):
                    if job < 4:
                        if not first:
                            pe.wait_ge(m.scores_used, 2 * PAIRS * b + job - 3)
                    elif job < c.proj_jobs + 4:
                        pe.wait_ge(m.proj_used, c.proj_jobs * b + job - 3)
                    else:
                        pe.wait_ge(m.scores_used, 2 * PAIRS * b + job - c.proj_jobs - 3)
                    return ps[:, RING + job % 4, :]

                def project(b, first):
                    pe.wait_ge(m.xT, b + 1)
                    for j in range(c.qk_jobs):
                        bank = ring(b, first, j)
                        for n in range(3):
                            col = (3 * j + n) * 128
                            mm(bank[:, n * N:(n + 1) * N], wqk[0:KC, 0, col:col + 128], xT[0:KC, 0, :], True, False)
                            x_ = mm(bank[:, n * N:(n + 1) * N], wqk[:, 1, col:col + 128], xT[:, 1, :], False, True)
                        x_.then_inc(m.ring_full, 1)
                    for s in range(2):
                        for q in range(c.v_parts):
                            bank = ring(b, first, c.qk_jobs + s * c.v_parts + q)
                            vw = c.v_cols
                            mm(bank[0:P, 0:vw], xT[0:KC, 0, s * P:(s + 1) * P], wv[0:KC, 0, q * vw:(q + 1) * vw], True, False)
                            mm(bank[0:P, 0:vw], xT[:, 1, s * P:(s + 1) * P], wv[:, 1, q * vw:(q + 1) * vw], False, True).then_inc(m.ring_full, 1)

                def scores(b, g, s, first):
                    if g == 0:
                        pe.wait_ge(m.proj_used, c.proj_jobs * (b + 1))
                    bank = ring(b, first, c.proj_jobs + 2 * g + s)
                    kl = klen(c, s)
                    if c.causal:
                        mm(bank[0:P, 0:G * kl], ident_b[:, :], mask_b[s][:, :, :], True, False)
                    for n in range(G):
                        q = c.order[G * g + n] // pq
                        x_ = mm(bank[0:P, n * kl:(n + 1) * kl], qT[:, G * g + n, s * P:(s + 1) * P],
                                kT[:, q, 0:kl], not c.causal, True)
                    x_.then_inc(m.ring_full, 1)

                def values(b, x, first, u):
                    pe.wait_ge(m.eT_copied, HEADS * b + x + 1)
                    per_bank = HEADS // c.o_banks
                    if x % per_bank == 0 and not (first and x == 0):
                        pe.wait_ge(m.o_copied, c.o_banks * b + x // per_bank)
                    h = c.order[x]
                    r, q = c.stride * (h % pq), (h // pq) % 3
                    o_ = ps[r:r + c.stride, PSO, q * N:(q + 1) * N]
                    mm(o_, V[u][:, 0, h * c.dh:h * c.dh + c.stride], ET[x % 2][:, 0, :], True, False)
                    if c.causal:
                        x_ = mm(o_[:, P:N], V[u][:, 1, h * c.dh:h * c.dh + c.stride], ET[x % 2][:, 1, 0:P], False, True)
                    else:
                        x_ = mm(o_, V[u][:, 1, h * c.dh:h * c.dh + c.stride], ET[x % 2][:, 1, :], False, True)
                    x_.then_inc(m.pv, 1)

                def turn_head(b, x, first):
                    g, n = x // G, x % G
                    if n == 0:
                        pe.wait_ge(m.e_norm, PAIRS * b + g + 1)
                    if not (first and x < 2):
                        pe.wait_ge(m.eT_copied, HEADS * b + x - 1)
                    bank = ps[0:P, PSE + x % 2, :]
                    for kc in range(2):
                        for s in range(2):
                            if c.causal and kc > s:
                                continue
                            at = kc * N + (0 if c.causal and kc else s * P)
                            x_ = nc.tensor.transpose(bank[:, at:at + P], Ex[g % 2][:, s, n, kc * P:(kc + 1) * P], ident[0:P, 0:P])
                    x_.then_inc(m.eT_full, 1)

                def pair(b, g, first, u, b_scores, g_scores, first_scores):
                    x = G * g
                    turn_head(b, x, first)
                    turn_head(b, x + 1, first)
                    if g_scores is not None:
                        scores(b_scores, g_scores, 0, first_scores)
                    values(b, x, first, u)
                    turn_head(b, x + 2, first)
                    values(b, x + 1, first, u)
                    if g_scores is not None:
                        scores(b_scores, g_scores, 1, first_scores)
                    values(b, x + 2, first, u)

                def out_project(b):
                    pe.wait_ge(m.o_copied, c.o_banks * (b + 1))
                    for s in range(2):
                        o_ = ps[0:P, PSA, s * D:(s + 1) * D]
                        mm(o_, ones[0:1, 0:P], bo[:, :], True, False)
                        for q in range(c.chunks):
                            x_ = mm(o_, OT[:, q, s * P:(s + 1) * P], wo[:, q, :], False, q == c.chunks - 1)
                    x_.then_inc(m.outp, 1)

                def turn_x2(b):
                    pe.wait_ge(m.xn2, 2 * b + 2)
                    for s in range(2):
                        for k in range(2):
                            t_ = nc.tensor.transpose(ps[0:KC, PSA, k * N + s * P:k * N + (s + 1) * P],
                                                     xn2[:, s, k * KC:(k + 1) * KC], ident[0:P, 0:P])
                    t_.then_inc(m.xn2T, 1)

                def route(b):
                    pe.wait_ge(m.xT2, b + 1)
                    for s in range(2):
                        o_ = ps[0:P, PSA, s * c.ew:(s + 1) * c.ew]
                        mm(o_, xT2[0:KC, 0, s * P:(s + 1) * P], wr[0:KC, 0, 0:c.ew], True, False)
                        x_ = mm(o_, xT2[:, 1, s * P:(s + 1) * P], wr[:, 1, 0:c.ew], False, True)
                    x_.then_inc(m.router, 1)

                def body(b, u, first, is_last):
                    if first:
                        for g in range(2):
                            for s in range(2):
                                scores(b, g, s, True)
                        turn_x(b + 1)
                    else:
                        pair(b - 1, 2, False, 1 - u, b, 0, False)
                        if not is_last:
                            turn_x(b + 1)
                        pair(b - 1, 3, False, 1 - u, b, 1, False)
                        out_project(b - 1)
                    pair(b, 0, first, u, b, 2, first)
                    pair(b, 1, first, u, b, 3, first)
                    if not first:
                        turn_x2(b - 1)
                    if not is_last:
                        project(b + 1, False)
                    if not first:
                        route(b - 1)

                pe.wait_ge(m.ld_att, 16 * 5)
                turn_x(0)
                project(0, True)
                body(0, 0, True, False)
                with pe.Fori(0, (B - 2) // 2) as k:
                    body(2 * k + 1, 1, False, False)
                    body(2 * k + 2, 0, False, False)
                body(B - 1, 1, False, True)
                pair(B - 1, 2, False, 1, None, None, False)
                pair(B - 1, 3, False, 1, None, None, False)
                out_project(B - 1)
                turn_x2(B - 1)
                route(B - 1)

            def shared(i):
                c, m = L[i], S[i]

                def up(b, u, first):
                    for j in range(c.s_jobs):
                        if not (first and j < 2):
                            pe.wait_ge(m.gu_used, c.s_jobs * b + j - 1)
                        p = (u * c.s_jobs + j) % 2
                        for w, bank in ((wg, p), (wu, 2 + p)):
                            for n in range(2):
                                col = (2 * j + n) * 128
                                for k in range(2):
                                    x_ = mm(ps[:, bank, n * N:(n + 1) * N], w[:, k, col:col + 128],
                                            XT[:, k, ds(b * N, N)], k == 0, k == 1)
                        x_.then_inc(m.gu_full, 1)

                def down(b, u, first):
                    pe.wait_ge(m.gu_used, c.s_jobs * (b + 1))
                    for s in range(2):
                        if not first:
                            pe.wait_ge(m.d_used, 2 * b + s - 1)
                        for q in range(c.sch):
                            x_ = mm(ps[0:P, 4 + s, 0:D], gT[u][:, q, s * P:(s + 1) * P], wd[:, q, :], q == 0, q == c.sch - 1)
                        x_.then_inc(m.d_full, 1)

                pe.wait_ge(m.ld_shared, 16 * 3)
                pe.wait_ge(m.xT_saved, B)
                pe.wait_ge(m.logits, B)
                up(0, 0, True)
                pe.wait_ge(m.oh_made, 1)
                mm(ps[0:P, 6, 0:T * c.e], consts[0:P, C_TRI:C_TRI + P], chosen[:, :, 0:c.e])
                mm(ps[0:P, 7, 0:T * c.e], ones[0:P, 0:P], chosen[:, :, 0:c.e]).then_inc(m.rank, 1)
                up(1, 1, False)
                down(0, 0, True)
                with pe.Fori(1, B // 2) as k:
                    up(2 * k, 0, False)
                    down(2 * k - 1, 1, False)
                    up(2 * k + 1, 1, False)
                    down(2 * k, 0, False)
                down(B - 1, 1, False)

            def experts(i):
                c, m = L[i], S[i]

                def turn(j, u, k, first):
                    pe.wait_ge((m.xs0, m.xs1)[u], 16 * (k + 1))
                    if not first:
                        pe.wait_ge(m.xsT_made, j)
                    for n in range(2):
                        x_ = nc.tensor.transpose(ps[0:KC, 0, n * SLOTS:(n + 1) * SLOTS], xs[u][:, n * KC:(n + 1) * KC], ident)
                    x_.then_inc(m.xs_T, 1)

                def up(j, u, k, first):
                    pe.wait_ge((m.w13_0, m.w13_1)[u], 16 * (k + 1))
                    pe.wait_ge(m.xsT_made, j + 1)
                    if not first:
                        pe.wait_ge(m.hg_made, j - 1)
                    for w in range(2):
                        for n in range(c.nch):
                            col = w * c.hidden + n * c.mc
                            for q in range(2):
                                x_ = mm(ps[0:c.mc, 1 + 2 * w + u, n * SLOTS:(n + 1) * SLOTS], w13[u][:, q, col:col + c.mc],
                                        xsT[u][:, q, :], q == 0, q == 1)
                    x_.then_inc(m.h_full, 1)

                def down(j, u, k, first):
                    pe.wait_ge((m.w2_0, m.w2_1)[u], 16 * (k + 1))
                    pe.wait_ge(m.hg_made, j + 1)
                    if not first:
                        pe.wait_ge(m.y_copied, j - 1)
                    for n in range(c.nch):
                        x_ = mm(ps[:, 5 + u, 0:D], hg[u][0:c.mc, n, :], w2[u][0:c.mc, n, :], n == 0, n == c.nch - 1)
                    x_.then_inc(m.y_full, 1)

                pe.wait_ge(m.gu_used, c.s_jobs * B)
                pe.wait_ge(m.d_used, T)
                turn(0, 0, 0, True)
                up(0, 0, 0, True)
                turn(1, 1, 0, False)
                up(1, 1, 0, True)
                down(0, 0, 0, True)
                with pe.Fori(1, c.nt // 2) as k:
                    turn(2 * k, 0, k, False)
                    up(2 * k, 0, k, False)
                    down(2 * k - 1, 1, k - 1, False)
                    turn(2 * k + 1, 1, k, False)
                    up(2 * k + 1, 1, k, False)
                    down(2 * k, 0, k, False)
                down(c.nt - 1, 1, c.nt // 2 - 1, False)

            for i in range(2):
                if i:
                    pe.wait_ge(S[0].y_copied, L[0].nt)
                else:
                    pe.wait_ge(tk_done, 4)
                attention(i)
                shared(i)
                experts(i)

        @block.scalar
        def _(act):
            act.wait_ge(tk, 1 + B)
            for b in range(B):
                if b:
                    act.wait_ge(tk_sq, b)
                nc.scalar.activation(junk[:, :], xp[:, b, :], ACT.Square, accum_out=sq[:, b:b + 1]).then_inc(tk_sq, 1)

            def attention(i):
                c, m = L[i], S[i]

                def copy_xT(b):
                    act.wait_ge(m.xnT, b + 1)
                    nc.scalar.copy(xT[0:KC, :, :], ps[0:KC, PSA, 0:2 * N].rearrange("p (k n) -> p k n", k=2)).then_inc(m.xT, 1)

                def exps(b, g, halves=(0, 1)):
                    for s in halves:
                        j = c.proj_jobs + 2 * g + s
                        kl = klen(c, s)
                        act.wait_ge(m.nb, 2 * PAIRS * b + 2 * g + s + 1)
                        for n in range(G):
                            x_ = nc.scalar.activation(Ex[g % 2][:, s, n, 0:kl], ps[0:P, RING + j % 4, n * kl:(n + 1) * kl], ACT.Exp,
                                                      bias=nb[:, (2 * g + s) % 4, n:n + 1], scale=c.scale,
                                                      accum_out=sums[:, g % 2, s * G + n:s * G + n + 1])
                        x_.then_inc(m.scores_used, 1)

                def copy_head(b, h, first):
                    w = N + P if c.causal else 2 * N
                    act.wait_ge(m.eT_full, HEADS * b + h + 1)
                    if not (first and h < 2):
                        act.wait_ge(m.pv, HEADS * b + h - 1)
                    nc.scalar.copy(ET[h % 2][:, :, :].rearrange("p k n -> p (k n)")[:, 0:w], ps[0:P, PSE + h % 2, 0:w]).then_inc(m.eT_copied, 1)

                def copy_eT(b, g, first):
                    for n in range(G):
                        copy_head(b, G * g + n, first)

                def copy_eT_2(b, first):
                    copy_head(b, 6, False)
                    if c.o_banks == 2:
                        copy_out(b, 0, first)
                    copy_head(b, 7, False)
                    copy_head(b, 8, False)

                def copy_out(b, k, first):
                    act.wait_ge(m.pv, HEADS * b + (k + 1) * (HEADS // c.o_banks))
                    if not first:
                        act.wait_ge(m.outp, b)
                    nc.scalar.copy(OT[:, 3 * k:3 * k + 3, :], ps[:, PSO, 0:3 * N].rearrange("p (k n) -> p k n", k=3)).then_inc(m.o_copied, 1)

                def copy_xT2(b, first):
                    act.wait_ge(m.xn2T, b + 1)
                    if not first:
                        act.wait_ge(m.xT_saved, b)
                    nc.scalar.copy(xT2[0:KC, :, :], ps[0:KC, PSA, 0:2 * N].rearrange("p (k n) -> p k n", k=2)).then_inc(m.xT2, 1)

                def copy_logits(b):
                    act.wait_ge(m.router, b + 1)
                    nc.scalar.copy(LG[:, ds(2 * b, 2), 0:c.ew], ps[0:P, PSA, 0:2 * c.ew].rearrange("p (s e) -> p s e", s=2)).then_inc(m.logits, 1)

                def body(b, u, first, second, is_last):
                    if not first:
                        copy_eT_2(b - 1, second)
                    if not is_last:
                        copy_xT(b + 1)
                    if not first:
                        copy_eT(b - 1, 3, False)
                        copy_out(b - 1, c.o_banks - 1, second)
                    exps(b, 0)
                    exps(b, 1)
                    copy_eT(b, 0, first)
                    exps(b, 2)
                    copy_eT(b, 1, first)
                    if not first:
                        copy_xT2(b - 1, second)
                    exps(b, 3)
                    if not first:
                        copy_logits(b - 1)

                copy_xT(0)
                body(0, 0, True, False, False)
                body(1, 1, False, True, False)
                with act.Fori(1, B // 2 - 1) as k:
                    body(2 * k, 0, False, False, False)
                    body(2 * k + 1, 1, False, False, False)
                body(B - 2, 0, False, False, False)
                body(B - 1, 1, False, False, True)
                copy_eT_2(B - 1, False)
                copy_eT(B - 1, 3, False)
                copy_out(B - 1, c.o_banks - 1, False)
                copy_xT2(B - 1, False)
                copy_logits(B - 1)

            def route(i):
                c, m = L[i], S[i]
                act.wait_ge(m.r, 2)
                nc.scalar.activation(r_p[:, :, 0:c.e], r_q[:, :, 0:c.e], ACT.Exp).then_inc(m.r_exp, 1)
                if c.gate:
                    nc.scalar.activation(alpha[:, :], LG[:, :, c.e], ACT.Exp, scale=-1.0).then_inc(m.r_exp, 1)

            def shared(i):
                c, m = L[i], S[i]

                def body(b, u):
                    for j in range(c.s_jobs):
                        p = (u * c.s_jobs + j) % 2
                        act.wait_ge(m.gu_full, c.s_jobs * b + j + 1)
                        nc.scalar.activation(sg[p][:, 0:2 * N], ps[:, p, 0:2 * N], ACT.Silu).then_inc(m.silu, 1)

                with act.Fori(0, B // 2) as k:
                    body(2 * k, 0)
                    body(2 * k + 1, 1)

            def experts(i):
                c, m = L[i], S[i]
                w = c.nch * SLOTS

                def copy_x(j, u):
                    act.wait_ge(m.xs_T, j + 1)
                    nc.scalar.copy(xsT[u][:, :, :], ps[0:KC, 0, 0:2 * SLOTS].rearrange("p (k n) -> p k n", k=2)).then_inc(m.xsT_made, 1)

                def silu(j, u):
                    act.wait_ge(m.h_full, j + 1)
                    nc.scalar.activation(sg[u][0:c.mc, 0:w], ps[0:c.mc, 1 + u, 0:w], ACT.Silu).then_inc(m.silu2, 1)

                def copy_y(j, u, k, first):
                    act.wait_ge(m.y_full, j + 1)
                    if not first:
                        act.wait_ge((m.y_st0, m.y_st1)[u], 16 * k)
                    nc.scalar.copy(ys[u][:, :], ps[:, 5 + u, 0:D]).then_inc(m.y_copied, 1)
                    act.wait_ge(m.y_copied, j + 1)
                    act.dma_start(Ys[i][ds(j * SLOTS, SLOTS), :], ys[u][:, :]).then_inc((m.y_st0, m.y_st1)[u], 16)

                copy_x(0, 0)
                copy_x(1, 1)
                silu(0, 0)
                silu(1, 1)
                copy_y(0, 0, 0, True)
                copy_x(2, 0)
                silu(2, 0)
                copy_y(1, 1, 0, True)
                copy_x(3, 1)
                silu(3, 1)
                copy_y(2, 0, 1, False)
                with act.Fori(2, c.nt // 2) as k:
                    copy_x(2 * k, 0)
                    silu(2 * k, 0)
                    copy_y(2 * k - 1, 1, k - 1, False)
                    copy_x(2 * k + 1, 1)
                    silu(2 * k + 1, 1)
                    copy_y(2 * k, 0, k, False)
                copy_y(c.nt - 1, 1, c.nt // 2 - 1, False)

            for i in range(2):
                attention(i)
                route(i)
                shared(i)
                experts(i)

        @block.vector
        def _(dve):
            nc.vector.memset(ones[:, :], 1.0).then_inc(const_made, 1)
            nc.vector.memset(half[:, :], -0.5).then_inc(const_made, 1)
            nc.vector.memset(zeros[:, :], 0.0).then_inc(const_made, 1)
            nc.vector.memset(carrier[:, :], 0.0).then_inc(const_made, 1)
            nc.vector.memset(eps2[:, :], EPS).then_inc(const_made, 1)
            for t_ in (xT, xT2):
                nc.vector.memset(t_[KC:KC + 1, :, :], 1.0).then_inc(const_made, 1)
            for t_ in scan:
                nc.vector.memset(t_[:, :, :], 0.0).then_inc(const_made, 1)

            n_img = 6 * 128 * NP
            dve.wait_ge(ld_x, 16)
            nc.vector.tensor_reduce(psum1[:, :], xp[:, :, :], AX.X, ALU.add).then_inc(tk_sum, 1)
            dve.wait_ge(tk_tot, 1)
            nc.vector.tensor_scalar(mean[:, :], ps[:, 0, 0:B], 1.0 / n_img, None, ALU.mult).then_inc(tk, 1)
            dve.wait_ge(tk, 1)
            for b in range(B):
                nc.vector.tensor_scalar(xp[:, b, :], xp[:, b, :], mean[:, b:b + 1], None, ALU.subtract).then_inc(tk, 1)
            dve.wait_ge(ld_tok, 16 * 7)
            for o in range(3):
                nc.vector.tensor_scalar(cbr[:, o, :], ones[:, 0:NP], cb[:, o:o + 1], None, ALU.mult)
            nc.vector.memset(cmat[:, :], 0.0).then_inc(tk_fold, 1)
            for o in range(3):
                for ci in range(3):
                    dst = pf[:, 2 * ci:2 * ci + 2, :]
                    src = pw[:, 2 * o:2 * o + 2, :]
                    if o == 0:
                        nc.vector.tensor_scalar(dst, src, cw[:, 3 * o + ci:3 * o + ci + 1], None, ALU.mult).then_inc(tk, 1)
                    else:
                        dve.wait_ge(tk, 1 + B + 3 * (o - 1) + ci + 1)
                        nc.vector.scalar_tensor_tensor(out=dst, in0=src, scalar=cw[:, 3 * o + ci:3 * o + ci + 1], in1=dst,
                                                       op0=ALU.mult, op1=ALU.add).then_inc(tk, 1)
            dve.wait_ge(tk_tot, 2)
            nc.vector.tensor_scalar(vt[:, :], ps[:, 0, 16:16 + B], 1.0 / n_img, EPS, ALU.mult, ALU.add).then_inc(tk_rs, 1)
            dve.wait_ge(tk_rs, 2)
            for b in range(B):
                nc.vector.scalar_tensor_tensor(out=xp[:, b, :], in0=xp[:, b, :], scalar=rs[:, b:b + 1], in1=lnw[:, :],
                                               op0=ALU.mult, op1=ALU.mult).then_inc(tk, 1)
            for b in range(B):
                dve.wait_ge(tk, 1 + B + 9 + b + 1)
                x_ = nc.vector.tensor_tensor(xp[:, b, :], xp[:, b, :], lnb[:, :], ALU.add)
            x_.then_inc(tk_fold, 1)
            dve.wait_ge(tk_mm, 1)
            nc.vector.tensor_tensor(cmat[:, :], ps[0:NP, 1, 0:D], pos_emb[:, :], ALU.add).then_inc(tk, 1)
            dve.wait_ge(tk, 1 + 2 * B + 9 + 1)
            nc.vector.tensor_tensor(cmat[:, :], cmat[:, :], pb[:, :], ALU.add).then_inc(tk, 1)
            dve.wait_ge(tk, 1 + 2 * B + 9 + 2)
            for q in range(4):
                dve.wait_ge(tk_mm, 1 + 2 * (q + 1))
                nc.vector.tensor_tensor(H[0:NP, 4 * q:4 * q + 4:2, :], ps[0:NP, 2 + q, 0:2 * D].rearrange("p (b d) -> p b d", b=2),
                                        cmat[:, :].unsqueeze(1).to_broadcast([NP, 2, D]), ALU.add).then_inc(tk_done, 1)
            dve.wait_ge(ld_const, 16)
            nc.vector.tensor_copy(ident_b[:, :], ident[0:P, 0:P]).then_inc(const_made, 1)
            for s, (col, w) in enumerate(((C_M0, P), (C_M1, N))):
                nc.vector.tensor_copy(mask_b[s][:, :, :], consts[0:P, col:col + w].unsqueeze(1).to_broadcast([P, G, w])).then_inc(const_made, 1)
            dve.wait_ge(ld_txt, 32)
            dve.wait_ge(tk_done, 4)

            def carry_wait():
                nc.vector.tensor_copy(carrier[:, 1:2], carrier[:, 0:1])

            def attention(i):
                c, m = L[i], S[i]

                def norm_stats(b):
                    for s in range(2):
                        nc.vector.bn_stats(stats[:, s, :], H[:, ds(2 * b + s, 1), :].rearrange("p o d -> p (o d)")).then_inc(m.st, 1)
                    dve.wait_ge(m.st, 2 * b + 2)
                    carry_wait()
                    for s in range(2):
                        nc.vector.bn_aggr(mv[:, s, :], stats[:, s, :]).then_inc(m.mvr, 1)

                def norm_apply(b, first):
                    dve.wait_ge(m.rs, b + 1)
                    if not first:
                        dve.wait_ge(m.xnT, b)
                    for s in range(2):
                        nc.vector.tensor_scalar(xn[:, s, :], H[:, ds(2 * b + s, 1), :].rearrange("p o d -> p (o d)"), mv[:, s, 0:1], rstd[:, s:s + 1],
                                                ALU.subtract, ALU.mult).then_inc(m.xn, 1)

                def copy_proj(b, u):
                    half_ = c.qk_jobs // 2
                    def bank(j):
                        dve.wait_ge(m.ring_full, b * c.jobs + j + 1)
                        return ps[:, RING + j % 4, :]
                    for j in range(half_):
                        k_ = bank(j)
                        for r in range(c.per_chunk):
                            rows = slice(c.stride * r, c.stride * (r + 1))
                            g = 2 * j + r
                            x_ = nc.vector.tensor_copy(qT[rows, G * g:G * g + G, :], k_[rows, 0:3 * N].rearrange("p (k n) -> p k n", k=3))
                        x_.then_inc(m.proj_used, 1)
                    for j in range(half_):
                        nc.vector.tensor_copy(kT[:, 3 * j:3 * j + 3, :], bank(half_ + j)[:, 0:3 * N].rearrange("p (k n) -> p k n", k=3)).then_inc(m.proj_used, 1)
                    for s in range(2):
                        for q in range(c.v_parts):
                            nc.vector.tensor_copy(V[u][:, s, q * c.v_cols:(q + 1) * c.v_cols],
                                                  bank(c.qk_jobs + s * c.v_parts + q)[0:P, 0:c.v_cols]).then_inc(m.proj_used, 1)

                def maxima(b, g):
                    for s in range(2):
                        j = c.proj_jobs + 2 * g + s
                        r = (2 * g + s) % 4
                        kl = klen(c, s)
                        done = 2 * PAIRS * b + 2 * g + s + 1
                        dve.wait_ge(m.ring_full, b * c.jobs + j + 1)
                        nc.vector.tensor_reduce(top[:, r, :], ps[0:P, RING + j % 4, 0:G * kl].rearrange("p (h k) -> p h k", h=G), AX.X, ALU.max).then_inc(m.nbc, 1)
                        dve.wait_ge(m.nbc, done)
                        nc.vector.tensor_scalar(nb[:, r, :], top[:, r, :], -c.scale, None, ALU.mult).then_inc(m.nb, 1)

                def normalise(b, g):
                    dve.wait_ge(m.scores_used, 2 * PAIRS * b + 2 * g + 2)
                    nc.vector.reciprocal(rsum[:, g % 2, :], sums[:, g % 2, :]).then_inc(m.rsc, 1)
                    dve.wait_ge(m.rsc, PAIRS * b + g + 1)
                    if c.causal:
                        for s in range(2):
                            kl = klen(c, s)
                            e_ = Ex[g % 2][:, s, :, 0:kl]
                            x_ = nc.vector.tensor_tensor(e_, e_, rsum[:, g % 2, s * G:(s + 1) * G].unsqueeze(2).to_broadcast([P, G, kl]), ALU.mult)
                    else:
                        e_ = Ex[g % 2][:, :, :, :].rearrange("p s h k -> p (s h) k")
                        x_ = nc.vector.tensor_tensor(e_, e_, rsum[:, g % 2, :].unsqueeze(2).to_broadcast([P, 2 * G, N]), ALU.mult)
                    x_.then_inc(m.e_norm, 1)

                def residual(b):
                    dve.wait_ge(m.outp, b + 1)
                    h_ = H[:, ds(2 * b, 2), :]
                    nc.vector.tensor_tensor(h_, h_, ps[0:P, PSA, 0:2 * D].rearrange("p (s d) -> p s d", s=2), ALU.add).then_inc(m.resid, 1)
                    dve.wait_ge(m.resid, b + 1)
                    carry_wait()
                    for s in range(2):
                        nc.vector.bn_stats(stats2[:, s, :], H[:, ds(2 * b + s, 1), :].rearrange("p o d -> p (o d)")).then_inc(m.st2, 1)
                    dve.wait_ge(m.st2, 2 * b + 2)
                    carry_wait()
                    for s in range(2):
                        nc.vector.bn_aggr(mv2[:, s, :], stats2[:, s, :]).then_inc(m.mv2r, 1)

                def norm_apply2(b, first):
                    dve.wait_ge(m.rs2, b + 1)
                    if not first:
                        dve.wait_ge(m.xn2T, b)
                        dve.wait_ge(m.xn_saved, b)
                    for s in range(2):
                        nc.vector.tensor_scalar(xn2[:, s, :], H[:, ds(2 * b + s, 1), :].rearrange("p o d -> p (o d)"), mv2[:, s, 0:1], rstd2[:, s:s + 1],
                                                ALU.subtract, ALU.mult).then_inc(m.xn2, 1)

                def body(b, u, first, second, is_last, is_last2):
                    if not first:
                        normalise(b - 1, 3)
                    if not is_last:
                        norm_apply(b + 1, False)
                    maxima(b, 0)
                    maxima(b, 1)
                    normalise(b, 0)
                    if not first:
                        residual(b - 1)
                    maxima(b, 2)
                    normalise(b, 1)
                    if not first:
                        norm_apply2(b - 1, second)
                    if not is_last2:
                        norm_stats(b + 2)
                    maxima(b, 3)
                    normalise(b, 2)
                    if not is_last:
                        copy_proj(b + 1, 1 - u)

                norm_stats(0)
                norm_apply(0, True)
                norm_stats(1)
                nc.vector.memset(qT[:, :, :], 0.0).then_inc(m.cleared, 1)
                if c.dh < c.stride:
                    for v_ in V:
                        nc.vector.memset(v_[:, :, c.vwidth:c.vwidth + c.dh], 0.0).then_inc(m.cleared, 1)
                dve.wait_ge(m.cleared, 3 if c.dh < c.stride else 1)
                copy_proj(0, 0)
                body(0, 0, True, False, False, False)
                body(1, 1, False, True, False, False)
                with dve.Fori(1, B // 2 - 1) as k:
                    body(2 * k, 0, False, False, False, False)
                    body(2 * k + 1, 1, False, False, False, False)
                body(B - 2, 0, False, False, False, True)
                body(B - 1, 1, False, False, True, True)
                normalise(B - 1, 3)
                residual(B - 1)
                norm_apply2(B - 1, False)

            def route(i):
                c, m = L[i], S[i]
                E = c.e
                n = [0]

                def step(ins):
                    n[0] += 1
                    ins.then_inc(m.r, 1)

                def after():
                    dve.wait_ge(m.r, n[0])

                def over_e(x):
                    return x.unsqueeze(2).to_broadcast([P, T, E])

                dve.wait_ge(m.logits, B)
                lg = LG[:, :, 0:E]
                p, q = r_p[:, :, 0:E], r_q[:, :, 0:E]
                eq, v = r_eq[:, :, 0:E], r_v[:, :, 0:E]
                oh = [x[:, :, 0:E] for x in onehot]
                step(nc.vector.tensor_reduce(r_mx[:, :], lg, AX.X, ALU.max))
                after()
                step(nc.vector.tensor_tensor(q, lg, over_e(r_mx[:, :]), ALU.subtract))
                dve.wait_ge(m.r_exp, 2 if c.gate else 1)
                step(nc.vector.tensor_reduce(r_sm[:, :], p, AX.X, ALU.add))
                after()
                step(nc.vector.reciprocal(r_sm[:, :], r_sm[:, :]))
                after()
                step(nc.vector.tensor_tensor(p, p, over_e(r_sm[:, :]), ALU.mult))
                after()
                desc = consts[0:P, C_DESC[i]:C_DESC[i] + E].unsqueeze(1).to_broadcast([P, T, E])
                for k in range(2):
                    step(nc.vector.tensor_reduce(gate[k][:, :], p, AX.X, ALU.max))
                    after()
                    step(nc.vector.tensor_tensor(eq, p, over_e(gate[k][:, :]), ALU.is_equal))
                    after()
                    step(nc.vector.tensor_tensor(v, eq, desc, ALU.mult))
                    after()
                    step(nc.vector.tensor_reduce(r_vm[:, :], v, AX.X, ALU.max))
                    after()
                    step(nc.vector.tensor_tensor(oh[k], v, over_e(r_vm[:, :]), ALU.is_equal))
                    after()
                    if k == 0:
                        step(nc.vector.scalar_tensor_tensor(out=p, in0=oh[0], scalar=-2.0, in1=p, op0=ALU.mult, op1=ALU.add))
                        after()
                nc.vector.tensor_tensor(chosen[:, :, 0:E], oh[0], oh[1], ALU.add).then_inc(m.oh_made, 1)
                if c.gate:
                    step(nc.vector.tensor_scalar(alpha[:, :], alpha[:, :], 1.0, None, ALU.add))
                    after()
                    step(nc.vector.reciprocal(alpha[:, :], alpha[:, :]))
                    step(nc.vector.tensor_tensor(r_sm[:, :], gate[0][:, :], gate[1][:, :], ALU.add))
                    after()
                    step(nc.vector.reciprocal(r_sm[:, :], r_sm[:, :]))
                    step(nc.vector.tensor_scalar(r_vm[:, :], alpha[:, :], -1.0, 1.0, ALU.mult, ALU.add))
                    after()
                    step(nc.vector.tensor_tensor(r_sm[:, :], r_sm[:, :], r_vm[:, :], ALU.mult))
                    after()
                    for k in range(2):
                        step(nc.vector.tensor_tensor(gate[k][:, :], gate[k][:, :], r_sm[:, :], ALU.mult))
                    after()

                def assign_slots():
                    dve.wait_ge(m.rank, 1)
                    rank = ps[0:P, 6, 0:T * E].rearrange("p (t e) -> p t e", t=T)
                    total = ps[0:P, 7, 0:T * E].rearrange("p (t e) -> p t e", t=T)
                    z = 8
                    step(nc.vector.tensor_copy(scan[0][:, z + 1:z + 1 + T, 0:E], total))
                    after()
                    for k, sh in enumerate((1, 2, 4, 8)):
                        x, y = scan[k % 2], scan[(k + 1) % 2]
                        step(nc.vector.tensor_tensor(y[:, z:z + 1 + T, 0:E], x[:, z:z + 1 + T, 0:E], x[:, z - sh:z + 1 + T - sh, 0:E], ALU.add))
                        after()
                    before = scan[0]
                    step(nc.vector.tensor_tensor(r_cmp[:, 0:E, :], before[:, z + T, 0:E].unsqueeze(2).to_broadcast([P, E, ACCROSS]),
                                                 consts[0:P, C_STEP:C_STEP + ACCROSS].unsqueeze(1).to_broadcast([P, E, ACCROSS]), ALU.is_gt))
                    after()
                    step(nc.vector.tensor_reduce(tiles[:, 0:E], r_cmp[:, 0:E, :], AX.X, ALU.add))
                    after()
                    bef = r_bef[:, :, :].rearrange("p a b -> p (a b)")[:, 0:E * E].rearrange("p (a b) -> p a b", a=E)
                    step(nc.vector.tensor_tensor(bef, tiles[:, 0:E].unsqueeze(1).to_broadcast([P, E, E]),
                                                 consts[0:P, C_BEF[i]:C_BEF[i] + E * E].rearrange("p (a b) -> p a b", a=E), ALU.mult))
                    after()
                    step(nc.vector.tensor_reduce(base[:, 0:E], bef, AX.X, ALU.add))
                    after()
                    step(nc.vector.tensor_tensor(last[:, 0:E], base[:, 0:E], tiles[:, 0:E], ALU.add))
                    after()
                    step(nc.vector.tensor_tensor(r_id[:, 0:c.nt, 0:E], last[0:1, 0:E].unsqueeze(1).to_broadcast([1, c.nt, E]),
                                                 consts[0:1, C_TILE:C_TILE + c.nt].unsqueeze(2).to_broadcast([1, c.nt, E]), ALU.is_le))
                    after()
                    step(nc.vector.tensor_reduce(idf[:, 0:c.nt], r_id[:, 0:c.nt, 0:E], AX.X, ALU.add))
                    after()
                    nc.vector.tensor_scalar(expert[i][:, 0:c.nt], idf[:, 0:c.nt], float(E - 1), None, ALU.min).then_inc(m.tile_ids, 1)
                    step(nc.vector.tensor_scalar(base[:, 0:E], base[:, 0:E], float(SLOTS), None, ALU.mult))
                    ps_, pf_ = pos[:, :, 0:E], before[:, z:z + T, 0:E]
                    step(nc.vector.tensor_tensor(ps_, rank, pf_, ALU.add))
                    after()
                    step(nc.vector.tensor_tensor(ps_, ps_, base[:, 0:E].unsqueeze(1).to_broadcast([P, T, E]), ALU.add))
                    after()
                    for k in range(2):
                        step(nc.vector.tensor_tensor(r_v[:, :, 0:E], ps_, oh[k], ALU.mult))
                        after()
                        step(nc.vector.tensor_reduce(slotf[:, :], r_v[:, :, 0:E], AX.X, ALU.add))
                        after()
                        nc.vector.tensor_copy(slot[k][:, :], slotf[:, :]).then_inc(m.slots, 1)

                return assign_slots

            def shared(i, assign_slots):
                c, m = L[i], S[i]

                def products(b, u):
                    for j in range(c.s_jobs):
                        p = (u * c.s_jobs + j) % 2
                        dve.wait_ge(m.silu, c.s_jobs * b + j + 1)
                        nc.vector.tensor_tensor(gT[u][:, 2 * j:2 * j + 2, :], sg[p][:, 0:2 * N].rearrange("p (c n) -> p c n", c=2),
                                                ps[:, 2 + p, 0:2 * N].rearrange("p (c n) -> p c n", c=2), ALU.mult).then_inc(m.gu_used, 1)

                def add(b):
                    for s in range(2):
                        dve.wait_ge(m.d_full, 2 * b + s + 1)
                        h_ = H[:, ds(2 * b + s, 1), :].rearrange("p o d -> p (o d)")
                        if c.gate:
                            nc.vector.scalar_tensor_tensor(out=h_, in0=ps[0:P, 4 + s, 0:D], scalar=alpha[:, ds(2 * b + s, 1)], in1=h_,
                                                           op0=ALU.mult, op1=ALU.add).then_inc(m.d_used, 1)
                        else:
                            nc.vector.tensor_tensor(h_, ps[0:P, 4 + s, 0:D], h_, ALU.add).then_inc(m.d_used, 1)

                products(0, 0)
                assign_slots()
                products(1, 1)
                add(0)
                with dve.Fori(1, B // 2) as k:
                    products(2 * k, 0)
                    add(2 * k - 1)
                    products(2 * k + 1, 1)
                    add(2 * k)
                add(B - 1)

            def experts(i):
                c, m = L[i], S[i]
                w = c.nch * SLOTS

                def product(j, u):
                    dve.wait_ge(m.silu2, j + 1)
                    nc.vector.tensor_tensor(hg[u][0:c.mc, 0:c.nch, :], sg[u][0:c.mc, 0:w].rearrange("p (c n) -> p c n", c=c.nch),
                                            ps[0:c.mc, 3 + u, 0:w].rearrange("p (c n) -> p c n", c=c.nch), ALU.mult).then_inc(m.hg_made, 1)

                with dve.Fori(0, c.nt // 2) as k:
                    product(2 * k, 0)
                    product(2 * k + 1, 1)

            def combine(i):
                c, m = L[i], S[i]
                dve.wait_ge(m.d_used, T)
                for t in range(T):
                    dve.wait_ge((m.gath0, m.gath1, m.gath2, m.gath3)[t % 4], 32 * (t // 4 + 1))
                    for k in range(2):
                        if k:
                            dve.wait_ge(m.comb, 2 * t + 1)
                        nc.vector.scalar_tensor_tensor(out=H[:, t, :], in0=yg[t % 4][:, k, :], scalar=gate[k][:, t:t + 1], in1=H[:, t, :],
                                                       op0=ALU.mult, op1=ALU.add).then_inc(m.comb, 1)
                dve.wait_ge(m.comb, 2 * T)

            for i in range(2):
                attention(i)
                shared(i, route(i))
                experts(i)
                combine(i)

        @block.gpsimd
        def _(pool):
            pool.wait_ge(const_made, 5)
            pool.wait_ge(tk_rs, 1)
            nc.gpsimd.tensor_tensor(rs[:, :], vt[:, :], half[:, 0:B], ALU.pow).then_inc(tk_rs, 1)

            def attention(i):
                c, m = L[i], S[i]

                def power(b, mv_, ve_, rstd_, ready, chain, done):
                    pool.wait_ge(ready, 2 * b + 2)
                    nc.gpsimd.tensor_tensor(ve_[:, :], mv_[:, :, 1], eps2[:, :], ALU.add).then_inc(chain, 1)
                    pool.wait_ge(chain, b + 1)
                    nc.gpsimd.tensor_tensor(rstd_[:, :], ve_[:, :], half[0:P, 0:2], ALU.pow).then_inc(done, 1)

                def save(b):
                    pool.wait_ge(m.xn2, 2 * b + 2)
                    nc.gpsimd.tensor_copy(XN[:, ds(2 * b, 2), :], xn2[:, :, :]).then_inc(m.xn_saved, 1)
                    pool.wait_ge(m.xT2, b + 1)
                    nc.gpsimd.tensor_copy(XT[:, :, ds(b * N, N)], xT2[0:KC, :, :]).then_inc(m.xT_saved, 1)

                power(0, mv, ve, rstd, m.mvr, m.ve_c, m.rs)
                power(1, mv, ve, rstd, m.mvr, m.ve_c, m.rs)
                with pool.Fori(0, B - 2) as b:
                    power(b + 2, mv, ve, rstd, m.mvr, m.ve_c, m.rs)
                    power(b, mv2, ve2, rstd2, m.mv2r, m.ve2_c, m.rs2)
                    save(b)
                for b in (B - 2, B - 1):
                    power(b, mv2, ve2, rstd2, m.mv2r, m.ve2_c, m.rs2)
                    save(b)

            def scatter(i):
                m = S[i]
                pool.wait_ge(zero_fill, 16 * ((L[0].nt + 5) // 6 + (L[1].nt + 5) // 6))
                pool.wait_ge(m.slots, 2)
                pool.wait_ge(m.xn_saved, B)
                for t in range(T):
                    for k in range(2):
                        nc.gpsimd.indirect_dma_start(out=Xs[i], out_offset=bass.IndirectOffsetOnAxis(ap=slot[k][:, t:t + 1], axis=0),
                                                     in_=XN[:, t, :], in_offset=None).then_inc(m.scat, 16)

            def gather(i):
                c, m = L[i], S[i]
                pool.wait_ge(m.y_st0, 16 * (c.nt // 2))
                pool.wait_ge(m.y_st1, 16 * (c.nt // 2))
                for t in range(T):
                    if t >= 4:
                        pool.wait_ge(m.comb, 2 * (t - 3))
                    for k in range(2):
                        nc.gpsimd.indirect_dma_start(out=yg[t % 4][:, k, :], out_offset=None, in_=Ys[i],
                                                     in_offset=bass.IndirectOffsetOnAxis(ap=slot[k][:, t:t + 1], axis=0)).then_inc(
                                                         (m.gath0, m.gath1, m.gath2, m.gath3)[t % 4], 16)

            for i in range(2):
                attention(i)
                scatter(i)
                gather(i)


def _layouts(np, z):
    f = np.float32
    out = {}
    out["xp"] = z["x"].reshape(B, 3, 6, 16, 6, 16).transpose(1, 3, 5, 0, 2, 4).reshape(6, 128, B, NP).transpose(1, 2, 0, 3).reshape(128, B, 6 * NP)
    for n, k in (("ln_w", "L0_tok_ln_w"), ("ln_b", "L0_tok_ln_b")):
        out[n] = z[k].reshape(3, 6, 16, 6, 16).transpose(0, 2, 4, 1, 3).reshape(6, 128, NP).transpose(1, 0, 2).reshape(128, 6 * NP)
    out["proj_t"] = z["L0_tok_proj_w"].T.reshape(6, 128, D).transpose(1, 0, 2)
    out["conv_w"] = np.broadcast_to(z["L0_tok_conv_w"].reshape(1, 9), (128, 9))
    out["conv_b"] = np.broadcast_to(z["L0_tok_conv_b"].reshape(1, 3), (128, 3))
    out["pos_emb"] = z["L0_tok_pos_emb"].reshape(NP, D)
    out["proj_b"] = np.broadcast_to(z["L0_tok_proj_b"].reshape(1, D), (NP, D))
    out["txt"] = z["txt"]

    def halves(w, bias):
        n = w.shape[1]
        r = np.zeros((KC + 1, 2, n), f)
        r[0:KC] = w.reshape(2, KC, n).transpose(1, 0, 2)
        r[KC, 1] = bias
        return r

    def spread(w):
        r = np.zeros((w.shape[0], HEADS, 32), f)
        r[:, :, 0:16] = w.reshape(w.shape[0], HEADS, 16)
        return r.reshape(w.shape[0], 384)

    w, bias = z["L0_attn_qkv_w"], z["L0_attn_qkv_b"]
    q, k = (halves(spread(w[n * D:(n + 1) * D].T), spread(bias[n * D:(n + 1) * D].reshape(1, D))[0]) for n in range(2))
    out["wqk0"] = np.concatenate([q, k], axis=2)
    out["wv0"] = halves(w[2 * D:].T, bias[2 * D:])
    out["wo0"] = spread(z["L0_attn_proj_w"]).T.reshape(3, 128, D).transpose(1, 0, 2)
    out["bo0"] = z["L0_attn_proj_b"].reshape(1, D)
    out["wr0"] = halves(z["L0_ffn_gate_w"].T, np.zeros(16, f))
    flat = lambda n: z[n].transpose(1, 0, 2).reshape(D, 768)
    out["wqk1"] = np.concatenate([halves(flat("L1_attn_W_Q"), z["L1_attn_b_Q"].reshape(768)), halves(flat("L1_attn_W_K"), z["L1_attn_b_K"].reshape(768))], axis=2)
    out["wv1"] = halves(flat("L1_attn_W_V"), z["L1_attn_b_V"].reshape(768))
    out["wo1"] = z["L1_attn_W_O"].reshape(6, 128, D).transpose(1, 0, 2)
    out["bo1"] = z["L1_attn_b_O"].reshape(1, D)
    out["wr1"] = np.concatenate([halves(z["L1_ffn_router_w"], np.zeros(8, f)), halves(z["L1_ffn_sg_w"], z["L1_ffn_sg_b"])], axis=2)
    rows = lambda w: w.reshape(2, KC, w.shape[1]).transpose(1, 0, 2)
    out["wg0"], out["wu0"] = rows(z["L0_ffn_sw1"].T), rows(z["L0_ffn_sw3"].T)
    out["wd0"] = z["L0_ffn_sw2"].T.reshape(8, 128, D).transpose(1, 0, 2)
    out["wg1"], out["wu1"] = rows(z["L1_ffn_ws_gate"]), rows(z["L1_ffn_ws_up"])
    out["wd1"] = z["L1_ffn_ws_down"].reshape(6, 128, D).transpose(1, 0, 2)
    both = np.concatenate([z["L0_ffn_w1"].transpose(0, 2, 1), z["L0_ffn_w3"].transpose(0, 2, 1)], axis=2)
    out["w13_0"] = both.reshape(16, 2, KC, 1024).transpose(0, 2, 1, 3)
    out["w2_0"] = z["L0_ffn_w2"].transpose(0, 2, 1).reshape(16, 4, 128, D).transpose(0, 2, 1, 3)
    both = np.concatenate([z["L1_ffn_w_gate"], z["L1_ffn_w_up"]], axis=2)
    out["w13_1"] = both.reshape(8, 2, KC, 384).transpose(0, 2, 1, 3)
    out["w2_1"] = z["L1_ffn_w_down"].reshape(8, 2, KC, D).transpose(0, 2, 1, 3)

    c = np.zeros((128, C_ALL), f)
    c[:, C_ID:C_ID + 128] = np.eye(128)
    c[0:P, C_TRI:C_TRI + P] = np.triu(np.ones((P, P)), 1)
    hidden = np.triu(np.ones((P, P)), 1) * -1e38
    c[0:P, C_M0:C_M0 + P] = hidden
    c[0:P, C_M1 + P:C_M1 + N] = hidden
    c[:, C_STEP:C_STEP + ACCROSS] = np.arange(ACCROSS) * SLOTS
    c[:, C_TILE:C_TILE + 36] = np.arange(36)
    for i, e in enumerate((16, 8)):
        c[:, C_DESC[i]:C_DESC[i] + e] = e - np.arange(e)
        c[:, C_BEF[i]:C_BEF[i] + e * e] = (np.arange(e)[:, None] > np.arange(e)[None, :]).reshape(e * e)
    out["consts"] = c
    return out


def kernel(**inputs):
    import numpy as _np
    import concourse.bacc as _bacc
    from concourse import mybir as _mybir
    from concourse.bass_utils import run_bass_kernel_spmd as _run

    nc = _bacc.Bacc("TRN2", target_bir_lowering=False, num_devices=1)
    arrays, args = {}, {}
    for name, v in _layouts(_np, {k: _np.asarray(v) for k, v in inputs.items()}).items():
        v = _np.ascontiguousarray(v)
        arrays[f"in_{name}"] = v
        args[name] = nc.dram_tensor(f"in_{name}", v.shape, _mybir.dt.from_np(v.dtype), kind="ExternalInput").ap()
    out = nc.dram_tensor("out_0_dram", (B, N, D), F32, kind="ExternalOutput").ap()
    build(nc, args, out)
    r = _run(nc, [arrays], core_ids=[0])
    return r.results[0]["out_0_dram"]
```

```python
from contextlib import ExitStack

import concourse.bass as bass
from concourse import mybir

ALU = mybir.AluOpType
ACT = mybir.ActivationFunctionType
AX = mybir.AxisListType
F32 = mybir.dt.float32
BF16 = mybir.dt.bfloat16
I32 = mybir.dt.int32
U32 = mybir.dt.uint32
ds = bass.ds

B = 8
D = 192
KC = 96
NP = 36
TXT = 128
N = NP + TXT
P = N // 2
T = 2 * B
HEADS = 12
EPS = 1e-5
G = 3
PAIRS = HEADS // G
SLOTS = 128
ACCROSS = 11


class Shapes:
    pass


class Signals:
    pass


def layer_shapes(layer):
    s = Shapes()
    s.dh = (16, 64)[layer]
    s.stride = (32, 64)[layer]
    s.chunks = (3, 6)[layer]
    s.causal = (False, True)[layer]
    s.scale = s.dh ** -0.5
    s.e = (16, 8)[layer]
    s.hidden = (512, 192)[layer]
    s.mc = (128, 96)[layer]
    s.shared = (1024, 768)[layer]
    s.gate = (False, True)[layer]
    s.width = s.stride * HEADS
    s.vwidth = s.dh * HEADS
    s.per_chunk = 128 // s.stride
    s.qk_jobs = 2 * s.chunks // 3
    s.v_parts = (1, 2)[layer]
    s.v_cols = s.vwidth // s.v_parts
    s.proj_jobs = s.qk_jobs + 2 * s.v_parts
    s.jobs = s.proj_jobs + 2 * PAIRS
    s.o_banks = s.chunks // 3
    s.ew = s.e + (1 if s.gate else 0)
    if layer == 0:
        s.order = [g + 4 * n for g in range(PAIRS) for n in range(G)]
    else:
        s.order = [6 * (g // 2) + g % 2 + 2 * n for g in range(PAIRS) for n in range(G)]
    s.nch = s.hidden // s.mc
    s.sch = s.shared // 128
    s.s_jobs = s.sch // 2
    s.nt = (2 * B * N + s.e * (SLOTS - 1)) // SLOTS
    s.least_pairs = (2 * B * N + 2 * SLOTS - 1) // (2 * SLOTS)
    assert s.jobs % 4 == 0 and s.nt % 2 == 0
    return s


C_ID = 0
C_TRI = C_ID + 128
C_M0 = C_TRI + P
C_M1 = C_M0 + P
C_STEP = C_M1 + N
C_TILE = C_STEP + ACCROSS
C_DESC = [C_TILE + 36, C_TILE + 36 + 16]
C_BEF = [C_DESC[1] + 8, C_DESC[1] + 8 + 256]
C_ALL = C_BEF[1] + 64


def build(nc, a, out):
    L = [layer_shapes(0), layer_shapes(1)]
    with ExitStack() as ctx:
        def sb(name, shape, dt=F32):
            return ctx.enter_context(nc.sbuf_tensor(name, shape, dt))

        def sem(name):
            return ctx.enter_context(nc.semaphore(name))

        ps = ctx.enter_context(nc.psum_tensor("ps", [128, 8, 512], F32))
        RING, PSE, PSO, PSA = 0, 4, 6, 7

        H = sb("H", [P, T, D])
        XN = sb("XN", [P, T, D])
        XT = sb("XT", [KC, 2, B * N])
        consts = sb("consts", [128, C_ALL])
        ident = consts[:, C_ID:C_ID + 128]
        ident_b = sb("ident_b", [P, P], BF16)
        mask_b = [sb("mask0_b", [P, G, P], BF16), sb("mask1_b", [P, G, N], BF16)]
        ones = sb("ones", [128, 128])
        zeros = sb("zeros", [128, 6 * D])
        half = sb("half", [128, 16])
        eps2 = sb("eps2", [P, 2])
        carrier = sb("carrier", [P, 2])
        carrier2 = sb("carrier2", [P, 2])
        wqk = sb("wqk", [KC + 1, 2, 2 * 768])
        wv = sb("wv", [KC + 1, 2, 768])
        wo = sb("wo", [128, 6, D])
        bo = sb("bo", [1, D])
        wr = sb("wr", [KC + 1, 2, 16])
        stats = sb("stats", [P, 2, 6])
        mv = sb("mv", [P, 2, 2])
        ve = sb("ve", [P, 2])
        rstd = sb("rstd", [P, 2])
        xn = sb("xn", [P, 2, D])
        xT = sb("xT", [KC + 1, 2, N])
        stats2 = sb("stats2", [P, 2, 6])
        mv2 = sb("mv2", [P, 2, 2])
        ve2 = sb("ve2", [P, 2])
        rstd2 = sb("rstd2", [P, 2])
        xn2 = sb("xn2", [P, 2, D])
        xT2 = sb("xT2", [KC + 1, 2, N])
        qT = sb("qT", [128, HEADS, N])
        kT = sb("kT", [128, 6, N])
        V = [sb(f"V{u}", [P, 2, 768]) for u in range(2)]
        top = sb("top", [P, 4, G])
        nb = sb("nb", [P, 4, G])
        sums = sb("sums", [P, 2, 2 * G])
        rsum = sb("rsum", [P, 2, 2 * G])
        Ex = [sb(f"Ex{i}", [P, 2, G, N]) for i in range(2)]
        ET = [sb(f"ET{i}", [P, 2, N]) for i in range(2)]
        OT = sb("OT", [128, 6, N])
        LG = sb("LG", [P, T, 17])
        wg = sb("wg", [KC, 2, 1024])
        wu = sb("wu", [KC, 2, 1024])
        wd = sb("wd", [128, 8, D])
        sg = [sb(f"sg{i}", [128, 512]) for i in range(2)]
        gT = [sb(f"gT{i}", [128, 8, N]) for i in range(2)]
        w13_whole = [sb(f"w13_{i}", [128, 2, 2, 512]) for i in range(2)]
        w13 = [x[0:KC, :, :, :] for x in w13_whole]
        w2 = [sb(f"w2_{i}", [128, 4, D]) for i in range(2)]
        xs = [sb(f"xs{i}", [SLOTS, D]) for i in range(2)]
        xsT = [sb(f"xsT{i}", [KC, 2, SLOTS]) for i in range(2)]
        hg = [sb(f"hg{i}", [128, 4, SLOTS]) for i in range(2)]
        ys = [sb(f"ys{i}", [SLOTS, D]) for i in range(2)]
        yg = [sb(f"yg{i}", [P, 2, D]) for i in range(4)]
        for v_ in V:
            yg += [v_[:, :, :].rearrange("p s n -> p (s n)")[:, 2 * D * n:2 * D * (n + 1)].rearrange("p (k d) -> p k d", k=2) for n in range(4)]
        for e_ in Ex:
            yg += [e_[:, :, :, :].rearrange("p s h n -> p (s h n)")[:, 2 * D * n:2 * D * (n + 1)].rearrange("p (k d) -> p k d", k=2) for n in range(2)]
        E16 = 16
        r_mx = sb("r_mx", [P, T])
        r_p = sb("r_p", [P, T, E16])
        r_q = sb("r_q", [P, T, E16])
        r_sm = sb("r_sm", [P, T])
        r_eq = sb("r_eq", [P, T, E16])
        r_v = sb("r_v", [P, T, E16])
        r_vm = sb("r_vm", [P, T])
        onehot = [sb(f"onehot{i}", [P, T, E16]) for i in range(2)]
        chosen = sb("chosen", [P, T, E16])
        gate = [sb(f"gate{i}", [P, T]) for i in range(2)]
        scan = [sb(f"scan{i}", [P, 9 + T, E16]) for i in range(2)]
        count = sb("count", [P, E16])
        r_cmp = sb("r_cmp", [P, E16, ACCROSS])
        tiles = sb("tiles", [P, E16])
        r_bef = sb("r_bef", [P, E16, E16])
        base = sb("base", [P, E16])
        last = sb("last", [P, E16])
        r_id = sb("r_id", [1, 36, E16])
        idf = sb("idf", [1, 36])
        expert = [sb(f"expert{i}", [1, 36], I32) for i in range(2)]
        r_np = sb("r_np", [1, 18])
        npf = sb("npf", [1, 1])
        more_pairs = [sb(f"more_pairs{i}", [1, 1], I32) for i in range(2)]
        pos = sb("pos", [P, T, E16])
        slotf = sb("slotf", [P, T])
        slot = [sb(f"slot{i}", [P, T], U32) for i in range(2)]
        alpha = sb("alpha", [P, T])
        first, second = (x[:, :, :, :].rearrange("p w k n -> p (w k n)") for x in w13_whole)
        xp = first[:, 0:B * 6 * NP].rearrange("p (b n) -> p b n", b=B)
        pf = second[:, 0:6 * D].rearrange("p (j d) -> p j d", j=6)
        at = 6 * D
        lnw, lnb, junk = (second[:, at + n * 6 * NP:at + (n + 1) * 6 * NP] for n in range(3))
        at += 3 * 6 * NP
        cbr = second[:, at:at + 3 * NP].rearrange("p (o n) -> p o n", o=3)
        pw = wd[:, 0:6, :]
        cw = sb("cw", [128, 9])
        cb = sb("cb", [128, 3])
        pos_emb = sb("pos_emb", [NP, D])
        pb = sb("pb", [NP, D])
        psum1 = sb("psum1", [128, B])
        mean = sb("mean", [128, B])
        sq = sb("sq", [128, B])
        vt = sb("vt", [128, B])
        rs = sb("rs", [128, B])
        cmat = sb("cmat", [NP, D])

        Xs = [nc.dram_tensor(f"sorted_rows{i}", (L[i].nt * SLOTS, D), F32, kind="Internal").ap() for i in range(2)]
        Ys = [nc.dram_tensor(f"expert_out{i}", (L[i].nt * SLOTS, D), F32, kind="Internal").ap() for i in range(2)]

        ld_x = sem("ld_x"); ld_tok = sem("ld_tok"); ld_txt = sem("ld_txt"); ld_const = sem("ld_const")
        const_made = sem("const_made")
        tk = sem("tk"); tk_sum = sem("tk_sum"); tk_tot = sem("tk_tot"); tk_sq = sem("tk_sq")
        tk_rs = sem("tk_rs"); tk_fold = sem("tk_fold"); tk_mm = sem("tk_mm"); tk_done = sem("tk_done")
        zero_fill = sem("zero_fill")
        groups = [range(0, 4), range(4, 10), range(10, 12), range(12, 14), range(14, 15), range(15, T)]
        gathered = [sem(f"gathered{n}") for n in range(len(groups))]
        stored = sem("stored")

        def layer_signals(i):
            m = Signals()
            m.ld_att = sem(f"ld_att_L{i}")
            m.ld_shared = sem(f"ld_shared_L{i}")
            m.st = sem(f"st_L{i}")
            m.mvr = sem(f"mvr_L{i}")
            m.ve_c = sem(f"ve_c_L{i}")
            m.rs = sem(f"rs_L{i}")
            m.xn = sem(f"xn_L{i}")
            m.xnT = sem(f"xnT_L{i}")
            m.xT = sem(f"xT_L{i}")
            m.ring_full = sem(f"ring_full_L{i}")
            m.proj_used = sem(f"proj_used_L{i}")
            m.scores_used = sem(f"scores_used_L{i}")
            m.cleared = sem(f"cleared_L{i}")
            m.nbc = sem(f"nbc_L{i}")
            m.nb = sem(f"nb_L{i}")
            m.rsc = sem(f"rsc_L{i}")
            m.e_norm = sem(f"e_norm_L{i}")
            m.eT_full = sem(f"eT_full_L{i}")
            m.eT_copied = sem(f"eT_copied_L{i}")
            m.pv = sem(f"pv_L{i}")
            m.o_copied = sem(f"o_copied_L{i}")
            m.outp = sem(f"outp_L{i}")
            m.resid = sem(f"resid_L{i}")
            m.st2 = sem(f"st2_L{i}")
            m.mv2r = sem(f"mv2r_L{i}")
            m.ve2_c = sem(f"ve2_c_L{i}")
            m.rs2 = sem(f"rs2_L{i}")
            m.xn2 = sem(f"xn2_L{i}")
            m.xn2T = sem(f"xn2T_L{i}")
            m.xT2 = sem(f"xT2_L{i}")
            m.router = sem(f"router_L{i}")
            m.logits = sem(f"logits_L{i}")
            m.xn_saved = sem(f"xn_saved_L{i}")
            m.xT_saved = sem(f"xT_saved_L{i}")
            m.r = sem(f"r_L{i}")
            m.r_exp = sem(f"r_exp_L{i}")
            m.oh_made = sem(f"oh_made_L{i}")
            m.rank = sem(f"rank_L{i}")
            m.slots = sem(f"slots_L{i}")
            m.tile_ids = sem(f"tile_ids_L{i}")
            m.scat = sem(f"scat_L{i}")
            m.gu_full = sem(f"gu_full_L{i}")
            m.silu = sem(f"silu_L{i}")
            m.gu_used = sem(f"gu_used_L{i}")
            m.d_full = sem(f"d_full_L{i}")
            m.d_used = sem(f"d_used_L{i}")
            m.xs0 = sem(f"xs0_L{i}")
            m.xs1 = sem(f"xs1_L{i}")
            m.w1_0 = sem(f"w1_0_L{i}")
            m.w1_1 = sem(f"w1_1_L{i}")
            m.w3_0 = sem(f"w3_0_L{i}")
            m.w3_1 = sem(f"w3_1_L{i}")
            m.w2_0 = sem(f"w2_0_L{i}")
            m.w2_1 = sem(f"w2_1_L{i}")
            m.xs_T = sem(f"xs_T_L{i}")
            m.xsT_made = sem(f"xsT_made_L{i}")
            m.gate_full = sem(f"gate_full_L{i}")
            m.h_full = sem(f"h_full_L{i}")
            m.silu2 = sem(f"silu2_L{i}")
            m.hg_made = sem(f"hg_made_L{i}")
            m.y_full = sem(f"y_full_L{i}")
            m.y_copied = sem(f"y_copied_L{i}")
            m.y_st0 = sem(f"y_st0_L{i}")
            m.y_st1 = sem(f"y_st1_L{i}")
            m.comb = sem(f"comb_L{i}")
            return m

        S = [layer_signals(0), layer_signals(1)]
        block = ctx.enter_context(nc.Block())

        def klen(c, s):
            return P if c.causal and s == 0 else N

        @block.sync
        def _(sp):
            sp.dma_start(xp, a["xp"]).then_inc(ld_x, 16)
            sp.dma_start(consts[:], a["consts"]).then_inc(ld_const, 16)
            for dst, name in ((pw, "proj_t"), (cw[:], "conv_w"), (cb[:], "conv_b"), (lnw, "ln_w"),
                              (lnb, "ln_b"), (pos_emb[:], "pos_emb"), (pb[:], "proj_b")):
                sp.dma_start(dst, a[name]).then_inc(ld_tok, 16)
            head_rows = P - NP
            sp.dma_start(H[NP:P, 0:T:2, :], a["txt"][:, 0:head_rows, :].rearrange("b p d -> p b d")).then_inc(ld_txt, 16)
            sp.dma_start(H[:, 1:T:2, :], a["txt"][:, head_rows:TXT, :].rearrange("b p d -> p b d")).then_inc(ld_txt, 16)

            def load_attention(i):
                c, m = L[i], S[i]
                for dst, name in ((wqk[:, :, 0:2 * c.width], "wqk"), (wv[:, :, 0:c.vwidth], "wv"),
                                  (wo[:, 0:c.chunks, :], "wo"), (bo[:], "bo"), (wr[:, :, 0:c.ew], "wr")):
                    sp.dma_start(dst, a[f"{name}{i}"]).then_inc(m.ld_att, 16)

            def load_shared(i):
                c, m = L[i], S[i]
                for dst, name in ((wg[:, :, 0:c.shared], "wg"), (wu[:, :, 0:c.shared], "wu"), (wd[:, 0:c.sch, :], "wd")):
                    sp.dma_start(dst, a[f"{name}{i}"]).then_inc(m.ld_shared, 16)

            def load_experts(i):
                c, m = L[i], S[i]
                sp.wait_ge(m.tile_ids, 2)

                def expert_of(j):
                    return sp.value_load(expert[i][0:1, ds(j, 1)], min_val=0, max_val=c.e - 1)

                def up_weights(j, u, first):
                    e = expert_of(j)
                    if not first:
                        sp.wait_ge(m.gate_full, j - 1)
                    sp.dma_start(w13[u][:, 0, :, 0:c.hidden], a[f"we_gate{i}"][ds(e, 1)].rearrange("e p k n -> p (e k) n")).then_inc((m.w1_0, m.w1_1)[u], 16)
                    if not first:
                        sp.wait_ge(m.h_full, j - 1)
                    sp.dma_start(w13[u][:, 1, :, 0:c.hidden], a[f"we_up{i}"][ds(e, 1)].rearrange("e p k n -> p (e k) n")).then_inc((m.w3_0, m.w3_1)[u], 16)

                def rows(j, u, first):
                    if not first:
                        sp.wait_ge(m.xs_T, j - 1)
                    sp.dma_start(xs[u][:], Xs[i][ds(j * SLOTS, SLOTS), :]).then_inc((m.xs0, m.xs1)[u], 16)

                pairs = sp.value_load(more_pairs[i][:, :], min_val=c.least_pairs - 2, max_val=c.nt // 2 - 2) + 2
                for u in range(2):
                    up_weights(u, u, True)
                sp.wait_ge(m.scat, 16 * 2 * T)
                for u in range(2):
                    rows(u, u, True)
                for u in range(2):
                    rows(2 + u, u, False)
                up_weights(2, 0, False)
                with sp.Fori(2, pairs) as k:
                    rows(2 * k, 0, False)
                    up_weights(2 * k - 1, 1, False)
                    rows(2 * k + 1, 1, False)
                    up_weights(2 * k, 0, False)
                up_weights(2 * pairs - 1, 1, False)

            load_attention(0)
            sp.wait_ge(tk_mm, 1)
            sp.wait_ge(tk, 1 + B + 9)
            load_shared(0)
            sp.wait_ge(const_made, 3)
            for part in (Xs[0], Xs[1], Ys[0][L[0].least_pairs * 2 * SLOTS:, :], Ys[1][L[1].least_pairs * 2 * SLOTS:, :]):
                flat = part.rearrange("(p n) d -> p (n d)", p=128)
                w = flat.shape[1]
                step = 6 * D
                for o in range(0, w, step):
                    n = min(step, w - o)
                    sp.dma_start(flat[:, o:o + n], zeros[:, 0:n]).then_inc(zero_fill, 16)
            sp.wait_ge(S[0].router, B)
            load_attention(1)
            load_experts(0)
            sp.wait_ge(S[0].d_full, T)
            load_shared(1)
            load_experts(1)
            for t, tiles_ in [(t, tiles_) for tiles_ in groups for t in tiles_]:
                sp.wait_ge(S[1].comb, tiles_[0] + len(tiles_) + t + 1)
                b, s = divmod(t, 2)
                sp.dma_start(out[b, s * P:(s + 1) * P, :], H[:, t, :]).then_inc(stored, 16)
            sp.wait_ge(stored, 16 * T)

        @block.tensor
        def _(pe):
            def mm(o, l, r, start=True, stop=True):
                return nc.tensor.matmul(o, l, r, start=start, stop=stop, skip_group_check=True)

            pe.wait_ge(const_made, 1)
            pe.wait_ge(tk_sum, 1)
            mm(ps[:, 0, 0:B], ones[:, :], psum1[:, :]).then_inc(tk_tot, 1)
            pe.wait_ge(tk_sq, B)
            mm(ps[:, 0, 16:16 + B], ones[:, :], sq[:, :]).then_inc(tk_tot, 1)
            pe.wait_ge(tk_fold, 1)
            for j in range(6):
                last_c = mm(ps[0:NP, 1, 0:D], cbr[:, j // 2, :], pw[:, j, :], start=(j == 0), stop=(j == 5))
            last_c.then_inc(tk_mm, 1)
            pe.wait_ge(tk_fold, 2)
            for b in range(B):
                for j in range(6):
                    last_c = mm(ps[0:NP, 2 + b // 2, (b % 2) * D:(b % 2 + 1) * D],
                                xp[:, b, j * NP:(j + 1) * NP], pf[:, j, :], start=(j == 0), stop=(j == 5))
                last_c.then_inc(tk_mm, 1)

            def attention(i):
                c, m = L[i], S[i]
                pq = c.per_chunk

                def turn_x(b):
                    pe.wait_ge(m.xn, 2 * b + 2)
                    for s in range(2):
                        for k in range(2):
                            t_ = nc.tensor.transpose(ps[0:KC, PSA, k * N + s * P:k * N + (s + 1) * P],
                                                     xn[:, s, k * KC:(k + 1) * KC], ident[0:P, 0:P])
                    t_.then_inc(m.xnT, 1)

                def ring(b, first, job):
                    if job < 4:
                        if not first:
                            pe.wait_ge(m.scores_used, 2 * PAIRS * b + job - 3)
                    elif job < c.proj_jobs + 4:
                        pe.wait_ge(m.proj_used, c.proj_jobs * b + job - 3)
                    else:
                        pe.wait_ge(m.scores_used, 2 * PAIRS * b + job - c.proj_jobs - 3)
                    return ps[:, RING + job % 4, :]

                def project(b, first):
                    pe.wait_ge(m.xT, b + 1)
                    for j in range(c.qk_jobs):
                        bank = ring(b, first, j)
                        for n in range(3):
                            col = (3 * j + n) * 128
                            mm(bank[:, n * N:(n + 1) * N], wqk[0:KC, 0, col:col + 128], xT[0:KC, 0, :], True, False)
                            x_ = mm(bank[:, n * N:(n + 1) * N], wqk[:, 1, col:col + 128], xT[:, 1, :], False, True)
                        x_.then_inc(m.ring_full, 1)
                    for s in range(2):
                        for q in range(c.v_parts):
                            bank = ring(b, first, c.qk_jobs + s * c.v_parts + q)
                            vw = c.v_cols
                            mm(bank[0:P, 0:vw], xT[0:KC, 0, s * P:(s + 1) * P], wv[0:KC, 0, q * vw:(q + 1) * vw], True, False)
                            mm(bank[0:P, 0:vw], xT[:, 1, s * P:(s + 1) * P], wv[:, 1, q * vw:(q + 1) * vw], False, True).then_inc(m.ring_full, 1)

                def scores(b, g, s, first):
                    if g == 0:
                        pe.wait_ge(m.proj_used, c.proj_jobs * (b + 1))
                    bank = ring(b, first, c.proj_jobs + 2 * g + s)
                    kl = klen(c, s)
                    if c.causal:
                        mm(bank[0:P, 0:G * kl], ident_b[:, :], mask_b[s][:, :, :], True, False)
                    for n in range(G):
                        q = c.order[G * g + n] // pq
                        x_ = mm(bank[0:P, n * kl:(n + 1) * kl], qT[:, G * g + n, s * P:(s + 1) * P],
                                kT[:, q, 0:kl], not c.causal, True)
                    x_.then_inc(m.ring_full, 1)

                def values(b, x, first, u):
                    pe.wait_ge(m.eT_copied, HEADS * b + x + 1)
                    per_bank = HEADS // c.o_banks
                    if x % per_bank == 0 and not (first and x == 0):
                        pe.wait_ge(m.o_copied, c.o_banks * b + x // per_bank)
                    h = c.order[x]
                    r, q = c.stride * (h % pq), (h // pq) % 3
                    o_ = ps[r:r + c.stride, PSO, q * N:(q + 1) * N]
                    mm(o_, V[u][:, 0, h * c.dh:h * c.dh + c.stride], ET[x % 2][:, 0, :], True, False)
                    if c.causal:
                        x_ = mm(o_[:, P:N], V[u][:, 1, h * c.dh:h * c.dh + c.stride], ET[x % 2][:, 1, 0:P], False, True)
                    else:
                        x_ = mm(o_, V[u][:, 1, h * c.dh:h * c.dh + c.stride], ET[x % 2][:, 1, :], False, True)
                    x_.then_inc(m.pv, 1)

                def turn_head(b, x, first):
                    g, n = x // G, x % G
                    if n == 0:
                        pe.wait_ge(m.e_norm, PAIRS * b + g + 1)
                    if not (first and x < 2):
                        pe.wait_ge(m.eT_copied, HEADS * b + x - 1)
                    bank = ps[0:P, PSE + x % 2, :]
                    for kc in range(2):
                        for s in range(2):
                            if c.causal and kc > s:
                                continue
                            at = kc * N + (0 if c.causal and kc else s * P)
                            x_ = nc.tensor.transpose(bank[:, at:at + P], Ex[g % 2][:, s, n, kc * P:(kc + 1) * P], ident[0:P, 0:P])
                    x_.then_inc(m.eT_full, 1)

                def pair(b, g, first, u, b_scores, g_scores, first_scores):
                    x = G * g
                    turn_head(b, x, first)
                    turn_head(b, x + 1, first)
                    if g_scores is not None:
                        scores(b_scores, g_scores, 0, first_scores)
                    values(b, x, first, u)
                    turn_head(b, x + 2, first)
                    values(b, x + 1, first, u)
                    if g_scores is not None:
                        scores(b_scores, g_scores, 1, first_scores)
                    values(b, x + 2, first, u)

                def out_project(b):
                    pe.wait_ge(m.o_copied, c.o_banks * (b + 1))
                    for s in range(2):
                        o_ = ps[0:P, PSA, s * D:(s + 1) * D]
                        mm(o_, ones[0:1, 0:P], bo[:, :], True, False)
                        for q in range(c.chunks):
                            x_ = mm(o_, OT[:, q, s * P:(s + 1) * P], wo[:, q, :], False, q == c.chunks - 1)
                    x_.then_inc(m.outp, 1)

                def turn_x2(b):
                    pe.wait_ge(m.xn2, 2 * b + 2)
                    for s in range(2):
                        for k in range(2):
                            t_ = nc.tensor.transpose(ps[0:KC, PSA, k * N + s * P:k * N + (s + 1) * P],
                                                     xn2[:, s, k * KC:(k + 1) * KC], ident[0:P, 0:P])
                    t_.then_inc(m.xn2T, 1)

                def route(b):
                    pe.wait_ge(m.xT2, b + 1)
                    for s in range(2):
                        o_ = ps[0:P, PSA, s * c.ew:(s + 1) * c.ew]
                        mm(o_, xT2[0:KC, 0, s * P:(s + 1) * P], wr[0:KC, 0, 0:c.ew], True, False)
                        x_ = mm(o_, xT2[:, 1, s * P:(s + 1) * P], wr[:, 1, 0:c.ew], False, True)
                    x_.then_inc(m.router, 1)

                def body(b, u, first, is_last):
                    if first:
                        for g in range(2):
                            for s in range(2):
                                scores(b, g, s, True)
                        turn_x(b + 1)
                    else:
                        pair(b - 1, 2, False, 1 - u, b, 0, False)
                        if not is_last:
                            turn_x(b + 1)
                        pair(b - 1, 3, False, 1 - u, b, 1, False)
                        out_project(b - 1)
                    pair(b, 0, first, u, b, 2, first)
                    pair(b, 1, first, u, b, 3, first)
                    if not first:
                        turn_x2(b - 1)
                    if not is_last:
                        project(b + 1, False)
                    if not first:
                        route(b - 1)

                def images():
                    pe.wait_ge(m.ld_att, 16 * 5)
                    if i:
                        pe.wait_ge(S[0].gu_used, L[0].s_jobs * B)
                    project(0, True)
                    if i:
                        pe.wait_ge(S[0].d_used, T)
                    body(0, 0, True, False)
                    with pe.Fori(0, (B - 2) // 2) as k:
                        body(2 * k + 1, 1, False, False)
                        body(2 * k + 2, 0, False, False)
                    body(B - 1, 1, False, True)
                    pair(B - 1, 2, False, 1, None, None, False)
                    pair(B - 1, 3, False, 1, None, None, False)
                    out_project(B - 1)
                    pe.wait_ge(m.ld_shared, 16 * 3)
                    pe.wait_ge(m.xT_saved, 1)
                    pe.wait_ge(m.scores_used, 2 * PAIRS * B)
                    shared_up(i, 0, 0, True, range(0, 2))
                    turn_x2(B - 1)
                    route(B - 1)

                return turn_x, images

            def shared_up(i, b, u, first, jobs):
                c, m = L[i], S[i]
                for j in jobs:
                    if not (first and j < 2):
                        pe.wait_ge(m.gu_used, c.s_jobs * b + j - 1)
                    p = (u * c.s_jobs + j) % 2
                    for w, bank in ((wg, p), (wu, 2 + p)):
                        for n in range(2):
                            col = (2 * j + n) * 128
                            for k in range(2):
                                x_ = mm(ps[:, bank, n * N:(n + 1) * N], w[:, k, col:col + 128],
                                        XT[:, k, b * N:(b + 1) * N], k == 0, k == 1)
                    x_.then_inc(m.gu_full, 1)

            def shared(i, half_, turn_x):
                c, m = L[i], S[i]

                def up(b, u, first):
                    shared_up(i, b, u, first, range(c.s_jobs))

                def down(b, u, first):
                    pe.wait_ge(m.gu_used, c.s_jobs * (b + 1))
                    for s in range(2):
                        if not first:
                            pe.wait_ge(m.d_used, 2 * b + s - 1)
                        for q in range(c.sch):
                            x_ = mm(ps[0:P, 4 + s, 0:D], gT[u][:, q, s * P:(s + 1) * P], wd[:, q, :], q == 0, q == c.sch - 1)
                        x_.then_inc(m.d_full, 1)

                if half_ == 0:
                    pe.wait_ge(m.xT_saved, B)
                    pe.wait_ge(m.logits, B)
                    shared_up(i, 0, 0, True, range(2, c.s_jobs))
                    pe.wait_ge(m.oh_made, 1)
                    mm(ps[0:P, 6, 0:T * c.e], consts[0:P, C_TRI:C_TRI + P], chosen[:, :, 0:c.e])
                    mm(ps[0:P, 7, 0:T * c.e], ones[0:P, 0:P], chosen[:, :, 0:c.e]).then_inc(m.rank, 1)
                else:
                    up(B // 2, 0, False)
                for b in range(half_ * B // 2 + 1, (half_ + 1) * B // 2):
                    up(b, b % 2, False)
                    down(b - 1, (b - 1) % 2, b == 1)
                if turn_x:
                    turn_x(0)
                down((half_ + 1) * B // 2 - 1, 1, False)

            def experts(i):
                c, m = L[i], S[i]

                def turn(j, u, k, first):
                    pe.wait_ge((m.xs0, m.xs1)[u], 16 * (k + 1))
                    if not first:
                        pe.wait_ge(m.xsT_made, j)
                    for n in range(2):
                        x_ = nc.tensor.transpose(ps[0:KC, 0, n * SLOTS:(n + 1) * SLOTS], xs[u][:, n * KC:(n + 1) * KC], ident)
                    x_.then_inc(m.xs_T, 1)

                def up(j, u, k, first):
                    pe.wait_ge(m.xsT_made, j + 1)
                    if not first:
                        pe.wait_ge(m.hg_made, j - 1)
                    for w in range(2):
                        pe.wait_ge(((m.w1_0, m.w1_1), (m.w3_0, m.w3_1))[w][u], 16 * (k + 1))
                        for n in range(c.nch):
                            for q in range(2):
                                x_ = mm(ps[0:c.mc, 1 + 2 * w + u, n * SLOTS:(n + 1) * SLOTS], w13[u][:, w, q, n * c.mc:(n + 1) * c.mc],
                                        xsT[u][:, q, :], q == 0, q == 1)
                        x_.then_inc((m.gate_full, m.h_full)[w], 1)

                def down(j, u, k, first):
                    pe.wait_ge((m.w2_0, m.w2_1)[u], 16 * (k + 1))
                    pe.wait_ge(m.hg_made, j + 1)
                    if not first:
                        pe.wait_ge(m.y_copied, j - 1)
                    for n in range(c.nch):
                        x_ = mm(ps[:, 5 + u, 0:D], hg[u][0:c.mc, n, :], w2[u][0:c.mc, n, :], n == 0, n == c.nch - 1)
                    x_.then_inc(m.y_full, 1)

                def two_tiles(k, first):
                    turn(2 * k, 0, k, False)
                    up(2 * k - 1, 1, k - 1, first)
                    down(2 * k - 2, 0, k - 1, first)
                    turn(2 * k + 1, 1, k, False)
                    up(2 * k, 0, k, False)
                    down(2 * k - 1, 1, k - 1, first)

                pairs = pe.value_load(more_pairs[i][:, :], min_val=c.least_pairs - 2, max_val=c.nt // 2 - 2) + 2
                pe.wait_ge(m.gu_used, c.s_jobs * B // 2)
                pe.wait_ge(m.d_used, B)
                turn(0, 0, 0, True)
                turn(1, 1, 0, False)
                up(0, 0, 0, True)
                two_tiles(1, True)
                with pe.Fori(2, pairs) as k:
                    two_tiles(k, False)
                up(2 * pairs - 1, 1, pairs - 1, False)
                down(2 * pairs - 2, 0, pairs - 1, False)
                down(2 * pairs - 1, 1, pairs - 1, False)
                pe.wait_ge(m.y_copied, 2 * pairs)

            pe.wait_ge(tk_done, 4)
            turn_x, images = attention(0)
            turn_x(0)
            for i in range(2):
                images()
                shared(i, 0, None)
                pe.wait_ge(S[i].tile_ids, 2)
                experts(i)
                if i == 0:
                    turn_x, images = attention(1)
                    shared(0, 1, turn_x)
                else:
                    shared(1, 1, None)

        @block.scalar
        def _(act):
            act.wait_ge(tk, 1 + B)
            for b in range(B):
                if b:
                    act.wait_ge(tk_sq, b)
                nc.scalar.activation(junk[:, :], xp[:, b, :], ACT.Square, accum_out=sq[:, b:b + 1]).then_inc(tk_sq, 1)

            def attention(i):
                c, m = L[i], S[i]

                def copy_xT(b):
                    act.wait_ge(m.xnT, b + 1)
                    nc.scalar.copy(xT[0:KC, :, :], ps[0:KC, PSA, 0:2 * N].rearrange("p (k n) -> p k n", k=2)).then_inc(m.xT, 1)

                def exps(b, g, halves=(0, 1)):
                    for s in halves:
                        j = c.proj_jobs + 2 * g + s
                        kl = klen(c, s)
                        act.wait_ge(m.nb, 2 * PAIRS * b + 2 * g + s + 1)
                        for n in range(G):
                            x_ = nc.scalar.activation(Ex[g % 2][:, s, n, 0:kl], ps[0:P, RING + j % 4, n * kl:(n + 1) * kl], ACT.Exp,
                                                      bias=nb[:, (2 * g + s) % 4, n:n + 1], scale=c.scale,
                                                      accum_out=sums[:, g % 2, s * G + n:s * G + n + 1])
                        x_.then_inc(m.scores_used, 1)

                def copy_head(b, h, first):
                    w = N + P if c.causal else 2 * N
                    act.wait_ge(m.eT_full, HEADS * b + h + 1)
                    if not (first and h < 2):
                        act.wait_ge(m.pv, HEADS * b + h - 1)
                    nc.scalar.copy(ET[h % 2][:, :, :].rearrange("p k n -> p (k n)")[:, 0:w], ps[0:P, PSE + h % 2, 0:w]).then_inc(m.eT_copied, 1)

                def copy_eT(b, g, first):
                    for n in range(G):
                        copy_head(b, G * g + n, first)

                def copy_eT_2(b, first):
                    copy_head(b, 6, False)
                    if c.o_banks == 2:
                        copy_out(b, 0, first)
                    copy_head(b, 7, False)
                    copy_head(b, 8, False)

                def copy_out(b, k, first):
                    act.wait_ge(m.pv, HEADS * b + (k + 1) * (HEADS // c.o_banks))
                    if not first:
                        act.wait_ge(m.outp, b)
                    nc.scalar.copy(OT[:, 3 * k:3 * k + 3, :], ps[:, PSO, 0:3 * N].rearrange("p (k n) -> p k n", k=3)).then_inc(m.o_copied, 1)

                def copy_xT2(b, first):
                    act.wait_ge(m.xn2T, b + 1)
                    if not first:
                        act.wait_ge(m.xT_saved, b)
                    nc.scalar.copy(xT2[0:KC, :, :], ps[0:KC, PSA, 0:2 * N].rearrange("p (k n) -> p k n", k=2)).then_inc(m.xT2, 1)

                def copy_logits(b):
                    act.wait_ge(m.router, b + 1)
                    nc.scalar.copy(LG[:, ds(2 * b, 2), 0:c.ew], ps[0:P, PSA, 0:2 * c.ew].rearrange("p (s e) -> p s e", s=2)).then_inc(m.logits, 1)

                def body(b, u, first, second, is_last):
                    if not first:
                        copy_eT_2(b - 1, second)
                    exps(b, 0, (0,))
                    if first:
                        exps(b, 0, (1,))
                    if not is_last:
                        copy_xT(b + 1)
                    if not first:
                        copy_eT(b - 1, 3, False)
                        exps(b, 0, (1,))
                        copy_out(b - 1, c.o_banks - 1, second)
                    exps(b, 1)
                    copy_eT(b, 0, first)
                    exps(b, 2)
                    copy_eT(b, 1, first)
                    if not first:
                        copy_xT2(b - 1, second)
                    exps(b, 3)
                    if not first:
                        copy_logits(b - 1)

                copy_xT(0)
                body(0, 0, True, False, False)
                body(1, 1, False, True, False)
                with act.Fori(1, B // 2 - 1) as k:
                    body(2 * k, 0, False, False, False)
                    body(2 * k + 1, 1, False, False, False)
                body(B - 2, 0, False, False, False)
                body(B - 1, 1, False, False, True)
                copy_eT_2(B - 1, False)
                copy_eT(B - 1, 3, False)
                copy_out(B - 1, c.o_banks - 1, False)
                copy_xT2(B - 1, False)
                copy_logits(B - 1)

            def route(i):
                c, m = L[i], S[i]
                act.wait_ge(m.r, 2)
                nc.scalar.activation(r_p[:, :, 0:c.e], r_q[:, :, 0:c.e], ACT.Exp).then_inc(m.r_exp, 1)
                if c.gate:
                    nc.scalar.activation(alpha[:, :], LG[:, :, c.e], ACT.Exp, scale=-1.0).then_inc(m.r_exp, 1)

            def shared(i, half_):
                c, m = L[i], S[i]

                def body(b, u):
                    for j in range(c.s_jobs):
                        p = (u * c.s_jobs + j) % 2
                        act.wait_ge(m.gu_full, c.s_jobs * b + j + 1)
                        nc.scalar.activation(sg[p][:, 0:2 * N], ps[:, p, 0:2 * N], ACT.Silu).then_inc(m.silu, 1)

                with act.Fori(half_ * B // 4, (half_ + 1) * B // 4) as k:
                    body(2 * k, 0)
                    body(2 * k + 1, 1)

            def experts(i):
                c, m = L[i], S[i]
                w = c.nch * SLOTS

                def copy_x(j, u, first):
                    act.wait_ge(m.xs_T, j + 1)
                    if not first:
                        act.wait_ge(m.h_full, j - 1)
                    nc.scalar.copy(xsT[u][:, :, :], ps[0:KC, 0, 0:2 * SLOTS].rearrange("p (k n) -> p k n", k=2)).then_inc(m.xsT_made, 1)

                def silu(j, u):
                    act.wait_ge(m.gate_full, j + 1)
                    nc.scalar.activation(sg[u][0:c.mc, 0:w], ps[0:c.mc, 1 + u, 0:w], ACT.Silu).then_inc(m.silu2, 1)

                def copy_y(j, u, k, first):
                    act.wait_ge(m.y_full, j + 1)
                    if not first:
                        act.wait_ge((m.y_st0, m.y_st1)[u], 16 * k)
                    nc.scalar.copy(ys[u][:, :], ps[:, 5 + u, 0:D]).then_inc(m.y_copied, 1)
                    act.wait_ge(m.y_copied, j + 1)
                    act.dma_start(Ys[i][ds(j * SLOTS, SLOTS), :], ys[u][:, :]).then_inc((m.y_st0, m.y_st1)[u], 16)

                def down_weights(j, u):
                    e = act.value_load(expert[i][0:1, ds(j, 1)], min_val=0, max_val=c.e - 1)
                    act.dma_start(w2[u][0:c.mc, 0:c.nch, :], a[f"we_down{i}"][ds(e, 1)].rearrange("e p k n -> p (e k) n")).then_inc((m.w2_0, m.w2_1)[u], 16)

                def two_tiles(k, first):
                    copy_x(2 * k, 0, False)
                    silu(2 * k - 1, 1)
                    copy_y(2 * k - 2, 0, k - 1, first)
                    down_weights(2 * k, 0)
                    copy_x(2 * k + 1, 1, False)
                    silu(2 * k, 0)
                    copy_y(2 * k - 1, 1, k - 1, first)
                    down_weights(2 * k + 1, 1)

                pairs = act.value_load(more_pairs[i][:, :], min_val=c.least_pairs - 2, max_val=c.nt // 2 - 2) + 2
                down_weights(0, 0)
                down_weights(1, 1)
                copy_x(0, 0, True)
                copy_x(1, 1, True)
                silu(0, 0)
                two_tiles(1, True)
                with act.Fori(2, pairs) as k:
                    two_tiles(k, False)
                silu(2 * pairs - 1, 1)
                copy_y(2 * pairs - 2, 0, pairs - 1, False)
                copy_y(2 * pairs - 1, 1, pairs - 1, False)

            for i in range(2):
                attention(i)
                route(i)
                shared(i, 0)
                act.wait_ge(S[i].tile_ids, 2)
                experts(i)
                shared(i, 1)

        @block.vector
        def _(dve):
            nc.vector.memset(ones[:, :], 1.0).then_inc(const_made, 1)
            nc.vector.memset(half[:, :], -0.5).then_inc(const_made, 1)
            nc.vector.memset(zeros[:, :], 0.0).then_inc(const_made, 1)
            nc.vector.memset(carrier[:, :], 0.0).then_inc(const_made, 1)
            nc.vector.memset(eps2[:, :], EPS).then_inc(const_made, 1)
            for t_ in (xT, xT2):
                nc.vector.memset(t_[KC:KC + 1, :, :], 1.0).then_inc(const_made, 1)
            for t_ in scan:
                nc.vector.memset(t_[:, :, :], 0.0).then_inc(const_made, 1)

            n_img = 6 * 128 * NP
            dve.wait_ge(ld_x, 16)
            nc.vector.tensor_reduce(psum1[:, :], xp[:, :, :], AX.X, ALU.add).then_inc(tk_sum, 1)
            dve.wait_ge(tk_tot, 1)
            nc.vector.tensor_scalar(mean[:, :], ps[:, 0, 0:B], 1.0 / n_img, None, ALU.mult).then_inc(tk, 1)
            dve.wait_ge(tk, 1)
            for b in range(B):
                nc.vector.tensor_scalar(xp[:, b, :], xp[:, b, :], mean[:, b:b + 1], None, ALU.subtract).then_inc(tk, 1)
            dve.wait_ge(ld_tok, 16 * 7)
            for o in range(3):
                nc.vector.tensor_scalar(cbr[:, o, :], ones[:, 0:NP], cb[:, o:o + 1], None, ALU.mult)
            nc.vector.memset(cmat[:, :], 0.0).then_inc(tk_fold, 1)
            for o in range(3):
                for ci in range(3):
                    dst = pf[:, 2 * ci:2 * ci + 2, :]
                    src = pw[:, 2 * o:2 * o + 2, :]
                    if o == 0:
                        nc.vector.tensor_scalar(dst, src, cw[:, 3 * o + ci:3 * o + ci + 1], None, ALU.mult).then_inc(tk, 1)
                    else:
                        dve.wait_ge(tk, 1 + B + 3 * (o - 1) + ci + 1)
                        nc.vector.scalar_tensor_tensor(out=dst, in0=src, scalar=cw[:, 3 * o + ci:3 * o + ci + 1], in1=dst,
                                                       op0=ALU.mult, op1=ALU.add).then_inc(tk, 1)
            dve.wait_ge(tk_tot, 2)
            nc.vector.tensor_scalar(vt[:, :], ps[:, 0, 16:16 + B], 1.0 / n_img, EPS, ALU.mult, ALU.add).then_inc(tk_rs, 1)
            dve.wait_ge(tk_rs, 2)
            for b in range(B):
                nc.vector.scalar_tensor_tensor(out=xp[:, b, :], in0=xp[:, b, :], scalar=rs[:, b:b + 1], in1=lnw[:, :],
                                               op0=ALU.mult, op1=ALU.mult).then_inc(tk, 1)
            for b in range(B):
                dve.wait_ge(tk, 1 + B + 9 + b + 1)
                x_ = nc.vector.tensor_tensor(xp[:, b, :], xp[:, b, :], lnb[:, :], ALU.add)
            x_.then_inc(tk_fold, 1)
            dve.wait_ge(tk_mm, 1)
            nc.vector.tensor_tensor(cmat[:, :], ps[0:NP, 1, 0:D], pos_emb[:, :], ALU.add).then_inc(tk, 1)
            dve.wait_ge(tk, 1 + 2 * B + 9 + 1)
            nc.vector.tensor_tensor(cmat[:, :], cmat[:, :], pb[:, :], ALU.add).then_inc(tk, 1)
            dve.wait_ge(tk, 1 + 2 * B + 9 + 2)
            for q in range(4):
                dve.wait_ge(tk_mm, 1 + 2 * (q + 1))
                nc.vector.tensor_tensor(H[0:NP, 4 * q:4 * q + 4:2, :], ps[0:NP, 2 + q, 0:2 * D].rearrange("p (b d) -> p b d", b=2),
                                        cmat[:, :].unsqueeze(1).to_broadcast([NP, 2, D]), ALU.add).then_inc(tk_done, 1)
            dve.wait_ge(ld_const, 16)
            nc.vector.tensor_copy(ident_b[:, :], ident[0:P, 0:P]).then_inc(const_made, 1)
            for s, (col, w) in enumerate(((C_M0, P), (C_M1, N))):
                nc.vector.tensor_copy(mask_b[s][:, :, :], consts[0:P, col:col + w].unsqueeze(1).to_broadcast([P, G, w])).then_inc(const_made, 1)
            dve.wait_ge(ld_txt, 32)
            dve.wait_ge(tk_done, 4)

            def carry_wait():
                nc.vector.tensor_copy(carrier[:, 1:2], carrier[:, 0:1])

            def attention(i):
                c, m = L[i], S[i]

                def norm_stats(b):
                    for s in range(2):
                        nc.vector.bn_stats(stats[:, s, :], H[:, ds(2 * b + s, 1), :].rearrange("p o d -> p (o d)")).then_inc(m.st, 1)
                    dve.wait_ge(m.st, 2 * b + 2)
                    carry_wait()
                    for s in range(2):
                        nc.vector.bn_aggr(mv[:, s, :], stats[:, s, :]).then_inc(m.mvr, 1)

                def norm_apply(b, first):
                    dve.wait_ge(m.rs, b + 1)
                    if not first:
                        dve.wait_ge(m.xnT, b)
                    for s in range(2):
                        nc.vector.tensor_scalar(xn[:, s, :], H[:, ds(2 * b + s, 1), :].rearrange("p o d -> p (o d)"), mv[:, s, 0:1], rstd[:, s:s + 1],
                                                ALU.subtract, ALU.mult).then_inc(m.xn, 1)

                def copy_proj(b, u):
                    half_ = c.qk_jobs // 2
                    def bank(j):
                        dve.wait_ge(m.ring_full, b * c.jobs + j + 1)
                        return ps[:, RING + j % 4, :]
                    for j in range(half_):
                        k_ = bank(j)
                        for r in range(c.per_chunk):
                            rows = slice(c.stride * r, c.stride * (r + 1))
                            g = 2 * j + r
                            x_ = nc.vector.tensor_copy(qT[rows, G * g:G * g + G, :], k_[rows, 0:3 * N].rearrange("p (k n) -> p k n", k=3))
                        x_.then_inc(m.proj_used, 1)
                    for j in range(half_):
                        nc.vector.tensor_copy(kT[:, 3 * j:3 * j + 3, :], bank(half_ + j)[:, 0:3 * N].rearrange("p (k n) -> p k n", k=3)).then_inc(m.proj_used, 1)
                    for s in range(2):
                        for q in range(c.v_parts):
                            nc.vector.tensor_copy(V[u][:, s, q * c.v_cols:(q + 1) * c.v_cols],
                                                  bank(c.qk_jobs + s * c.v_parts + q)[0:P, 0:c.v_cols]).then_inc(m.proj_used, 1)

                def maxima(b, g):
                    for s in range(2):
                        j = c.proj_jobs + 2 * g + s
                        r = (2 * g + s) % 4
                        kl = klen(c, s)
                        done = 2 * PAIRS * b + 2 * g + s + 1
                        dve.wait_ge(m.ring_full, b * c.jobs + j + 1)
                        nc.vector.tensor_reduce(top[:, r, :], ps[0:P, RING + j % 4, 0:G * kl].rearrange("p (h k) -> p h k", h=G), AX.X, ALU.max).then_inc(m.nbc, 1)
                        dve.wait_ge(m.nbc, done)
                        nc.vector.tensor_scalar(nb[:, r, :], top[:, r, :], -c.scale, None, ALU.mult).then_inc(m.nb, 1)

                def normalise(b, g):
                    dve.wait_ge(m.scores_used, 2 * PAIRS * b + 2 * g + 2)
                    nc.vector.reciprocal(rsum[:, g % 2, :], sums[:, g % 2, :]).then_inc(m.rsc, 1)
                    dve.wait_ge(m.rsc, PAIRS * b + g + 1)
                    if c.causal:
                        for s in range(2):
                            kl = klen(c, s)
                            e_ = Ex[g % 2][:, s, :, 0:kl]
                            x_ = nc.vector.tensor_tensor(e_, e_, rsum[:, g % 2, s * G:(s + 1) * G].unsqueeze(2).to_broadcast([P, G, kl]), ALU.mult)
                    else:
                        e_ = Ex[g % 2][:, :, :, :].rearrange("p s h k -> p (s h) k")
                        x_ = nc.vector.tensor_tensor(e_, e_, rsum[:, g % 2, :].unsqueeze(2).to_broadcast([P, 2 * G, N]), ALU.mult)
                    x_.then_inc(m.e_norm, 1)

                def residual(b):
                    dve.wait_ge(m.outp, b + 1)
                    h_ = H[:, ds(2 * b, 2), :]
                    nc.vector.tensor_tensor(h_, h_, ps[0:P, PSA, 0:2 * D].rearrange("p (s d) -> p s d", s=2), ALU.add).then_inc(m.resid, 1)
                    dve.wait_ge(m.resid, b + 1)
                    carry_wait()
                    for s in range(2):
                        nc.vector.bn_stats(stats2[:, s, :], H[:, ds(2 * b + s, 1), :].rearrange("p o d -> p (o d)")).then_inc(m.st2, 1)
                    dve.wait_ge(m.st2, 2 * b + 2)
                    carry_wait()
                    for s in range(2):
                        nc.vector.bn_aggr(mv2[:, s, :], stats2[:, s, :]).then_inc(m.mv2r, 1)

                def norm_apply2(b, first):
                    dve.wait_ge(m.rs2, b + 1)
                    if not first:
                        dve.wait_ge(m.xn2T, b)
                        dve.wait_ge(m.xn_saved, b)
                    for s in range(2):
                        nc.vector.tensor_scalar(xn2[:, s, :], H[:, ds(2 * b + s, 1), :].rearrange("p o d -> p (o d)"), mv2[:, s, 0:1], rstd2[:, s:s + 1],
                                                ALU.subtract, ALU.mult).then_inc(m.xn2, 1)

                def body(b, u, first, second, is_last, is_last2):
                    if not first:
                        normalise(b - 1, 3)
                    if not is_last:
                        norm_apply(b + 1, False)
                    maxima(b, 0)
                    maxima(b, 1)
                    normalise(b, 0)
                    normalise(b, 1)
                    if not first:
                        residual(b - 1)
                    maxima(b, 2)
                    if not first:
                        norm_apply2(b - 1, second)
                    if not is_last2:
                        norm_stats(b + 2)
                    maxima(b, 3)
                    normalise(b, 2)
                    if not is_last:
                        copy_proj(b + 1, 1 - u)

                def first_norms(part):
                    if part == 0:
                        if i:
                            dve.wait_ge(S[0].comb, 8)
                        norm_stats(0)
                        return
                    norm_apply(0, True)
                    norm_stats(1)
                    nc.vector.memset(qT[:, :, :], 0.0).then_inc(m.cleared, 1)
                    if c.dh < c.stride:
                        for v_ in V:
                            nc.vector.memset(v_[:, :, c.vwidth:c.vwidth + c.dh], 0.0).then_inc(m.cleared, 1)
                    dve.wait_ge(m.cleared, 3 if c.dh < c.stride else 1)

                def images():
                    copy_proj(0, 0)
                    body(0, 0, True, False, False, False)
                    body(1, 1, False, True, False, False)
                    with dve.Fori(1, B // 2 - 1) as k:
                        body(2 * k, 0, False, False, False, False)
                        body(2 * k + 1, 1, False, False, False, False)
                    body(B - 2, 0, False, False, False, True)
                    body(B - 1, 1, False, False, True, True)
                    normalise(B - 1, 3)
                    residual(B - 1)
                    norm_apply2(B - 1, False)

                return first_norms, images

            def route(i, product):
                c, m = L[i], S[i]
                E = c.e
                n = [0]

                def step(ins):
                    n[0] += 1
                    ins.then_inc(m.r, 1)

                def after():
                    dve.wait_ge(m.r, n[0])

                def over_e(x):
                    return x.unsqueeze(2).to_broadcast([P, T, E])

                dve.wait_ge(m.logits, B)
                lg = LG[:, :, 0:E]
                p, q = r_p[:, :, 0:E], r_q[:, :, 0:E]
                eq, v = r_eq[:, :, 0:E], r_v[:, :, 0:E]
                oh = [x[:, :, 0:E] for x in onehot]
                step(nc.vector.tensor_reduce(r_mx[:, :], lg, AX.X, ALU.max))
                after()
                step(nc.vector.tensor_tensor(q, lg, over_e(r_mx[:, :]), ALU.subtract))
                dve.wait_ge(m.r_exp, 2 if c.gate else 1)
                step(nc.vector.tensor_reduce(r_sm[:, :], p, AX.X, ALU.add))
                after()
                step(nc.vector.reciprocal(r_sm[:, :], r_sm[:, :]))
                after()
                step(nc.vector.tensor_tensor(p, p, over_e(r_sm[:, :]), ALU.mult))
                after()
                desc = consts[0:P, C_DESC[i]:C_DESC[i] + E].unsqueeze(1).to_broadcast([P, T, E])
                for k in range(2):
                    step(nc.vector.tensor_reduce(gate[k][:, :], p, AX.X, ALU.max))
                    after()
                    step(nc.vector.tensor_tensor(eq, p, over_e(gate[k][:, :]), ALU.is_equal))
                    after()
                    step(nc.vector.tensor_tensor(v, eq, desc, ALU.mult))
                    after()
                    step(nc.vector.tensor_reduce(r_vm[:, :], v, AX.X, ALU.max))
                    after()
                    step(nc.vector.tensor_tensor(oh[k], v, over_e(r_vm[:, :]), ALU.is_equal))
                    after()
                    if k == 0:
                        step(nc.vector.scalar_tensor_tensor(out=p, in0=oh[0], scalar=-2.0, in1=p, op0=ALU.mult, op1=ALU.add))
                        product(0)
                        product(1)
                        after()
                nc.vector.tensor_tensor(chosen[:, :, 0:E], oh[0], oh[1], ALU.add).then_inc(m.oh_made, 1)
                for j in range(2, c.s_jobs):
                    product(j)
                if c.gate:
                    step(nc.vector.tensor_scalar(alpha[:, :], alpha[:, :], 1.0, None, ALU.add))
                    after()
                    step(nc.vector.reciprocal(alpha[:, :], alpha[:, :]))
                    step(nc.vector.tensor_tensor(r_sm[:, :], gate[0][:, :], gate[1][:, :], ALU.add))
                    after()
                    step(nc.vector.reciprocal(r_sm[:, :], r_sm[:, :]))
                    step(nc.vector.tensor_scalar(r_vm[:, :], alpha[:, :], -1.0, 1.0, ALU.mult, ALU.add))
                    after()
                    step(nc.vector.tensor_tensor(r_sm[:, :], r_sm[:, :], r_vm[:, :], ALU.mult))
                    after()
                    for k in range(2):
                        step(nc.vector.tensor_tensor(gate[k][:, :], gate[k][:, :], r_sm[:, :], ALU.mult))
                    after()

                def assign_slots():
                    dve.wait_ge(m.rank, 1)
                    rank = ps[0:P, 6, 0:T * E].rearrange("p (t e) -> p t e", t=T)
                    total = ps[0:P, 7, 0:T * E].rearrange("p (t e) -> p t e", t=T)
                    z = 8
                    step(nc.vector.tensor_copy(scan[0][:, z + 1:z + 1 + T, 0:E], total))
                    after()
                    for k, sh in enumerate((1, 2, 4, 8)):
                        x, y = scan[k % 2], scan[(k + 1) % 2]
                        step(nc.vector.tensor_tensor(y[:, z:z + 1 + T, 0:E], x[:, z:z + 1 + T, 0:E], x[:, z - sh:z + 1 + T - sh, 0:E], ALU.add))
                        after()
                    before = scan[0]
                    step(nc.vector.tensor_tensor(r_cmp[:, 0:E, :], before[:, z + T, 0:E].unsqueeze(2).to_broadcast([P, E, ACCROSS]),
                                                 consts[0:P, C_STEP:C_STEP + ACCROSS].unsqueeze(1).to_broadcast([P, E, ACCROSS]), ALU.is_gt))
                    after()
                    step(nc.vector.tensor_reduce(tiles[:, 0:E], r_cmp[:, 0:E, :], AX.X, ALU.add))
                    after()
                    bef = r_bef[:, :, :].rearrange("p a b -> p (a b)")[:, 0:E * E].rearrange("p (a b) -> p a b", a=E)
                    step(nc.vector.tensor_tensor(bef, tiles[:, 0:E].unsqueeze(1).to_broadcast([P, E, E]),
                                                 consts[0:P, C_BEF[i]:C_BEF[i] + E * E].rearrange("p (a b) -> p a b", a=E), ALU.mult))
                    after()
                    step(nc.vector.tensor_reduce(base[:, 0:E], bef, AX.X, ALU.add))
                    after()
                    step(nc.vector.tensor_tensor(last[:, 0:E], base[:, 0:E], tiles[:, 0:E], ALU.add))
                    after()
                    step(nc.vector.tensor_tensor(r_id[:, 0:c.nt, 0:E], last[0:1, 0:E].unsqueeze(1).to_broadcast([1, c.nt, E]),
                                                 consts[0:1, C_TILE:C_TILE + c.nt].unsqueeze(2).to_broadcast([1, c.nt, E]), ALU.is_le))
                    after()
                    step(nc.vector.tensor_reduce(idf[:, 0:c.nt], r_id[:, 0:c.nt, 0:E], AX.X, ALU.add))
                    after()
                    nc.vector.tensor_scalar(expert[i][:, 0:c.nt], idf[:, 0:c.nt], float(E - 1), None, ALU.min).then_inc(m.tile_ids, 1)
                    step(nc.vector.tensor_scalar(r_np[:, 0:c.nt // 2], consts[0:1, C_TILE:C_TILE + c.nt // 2], 2.0, last[0:1, E - 1:E], ALU.mult, ALU.is_lt))
                    after()
                    step(nc.vector.tensor_reduce(npf[:, :], r_np[:, 0:c.nt // 2], AX.X, ALU.add))
                    after()
                    nc.vector.tensor_scalar(more_pairs[i][:, :], npf[:, :], -2.0, None, ALU.add).then_inc(m.tile_ids, 1)
                    step(nc.vector.tensor_scalar(base[:, 0:E], base[:, 0:E], float(SLOTS), None, ALU.mult))
                    ps_, pf_ = pos[:, :, 0:E], before[:, z:z + T, 0:E]
                    step(nc.vector.tensor_tensor(ps_, rank, pf_, ALU.add))
                    after()
                    step(nc.vector.tensor_tensor(ps_, ps_, base[:, 0:E].unsqueeze(1).to_broadcast([P, T, E]), ALU.add))
                    after()
                    for k in range(2):
                        step(nc.vector.tensor_tensor(r_v[:, :, 0:E], ps_, oh[k], ALU.mult))
                        after()
                        step(nc.vector.tensor_reduce(slotf[:, :], r_v[:, :, 0:E], AX.X, ALU.add))
                        after()
                        nc.vector.tensor_copy(slot[k][:, :], slotf[:, :]).then_inc(m.slots, 1)

                return assign_slots

            def shared(i, half_, first_norms):
                c, m = L[i], S[i]

                def product(b, u, j):
                    p = (u * c.s_jobs + j) % 2
                    dve.wait_ge(m.silu, c.s_jobs * b + j + 1)
                    nc.vector.tensor_tensor(gT[u][:, 2 * j:2 * j + 2, :], sg[p][:, 0:2 * N].rearrange("p (c n) -> p c n", c=2),
                                            ps[:, 2 + p, 0:2 * N].rearrange("p (c n) -> p c n", c=2), ALU.mult).then_inc(m.gu_used, 1)

                def products(b, u):
                    for j in range(c.s_jobs):
                        product(b, u, j)

                def add(b):
                    for s in range(2):
                        dve.wait_ge(m.d_full, 2 * b + s + 1)
                        h_ = H[:, ds(2 * b + s, 1), :].rearrange("p o d -> p (o d)")
                        if c.gate:
                            nc.vector.scalar_tensor_tensor(out=h_, in0=ps[0:P, 4 + s, 0:D], scalar=alpha[:, ds(2 * b + s, 1)], in1=h_,
                                                           op0=ALU.mult, op1=ALU.add).then_inc(m.d_used, 1)
                        else:
                            nc.vector.tensor_tensor(h_, ps[0:P, 4 + s, 0:D], h_, ALU.add).then_inc(m.d_used, 1)

                def combine(n):
                    dve.wait_ge(gathered[n], 32 * len(groups[n]) * (i + 1))
                    for k, t in [(k, t) for k in range(2) for t in groups[n]]:
                        if k:
                            dve.wait_ge(m.comb, groups[n][0] + t + 1)
                        else:
                            dve.wait_ge(m.d_used, t + 1)
                        nc.vector.scalar_tensor_tensor(out=H[:, t, :], in0=yg[t][:, k, :], scalar=gate[k][:, t:t + 1], in1=H[:, t, :],
                                                       op0=ALU.mult, op1=ALU.add).then_inc(m.comb, 1)

                if half_ == 0:
                    route(i, lambda j: product(0, 0, j))()
                    for b in range(1, B // 2):
                        products(b, b % 2)
                        add(b - 1)
                    add(B // 2 - 1)
                else:
                    products(4, 0)
                    products(5, 1)
                    add(4)
                    combine(0)
                    if first_norms:
                        first_norms(0)
                    products(6, 0)
                    add(5)
                    combine(1)
                    products(7, 1)
                    if first_norms:
                        first_norms(1)
                    add(6)
                    combine(2)
                    combine(3)
                    add(7)
                    combine(4)
                    combine(5)
                    dve.wait_ge(m.comb, 2 * T)

            def experts(i):
                c, m = L[i], S[i]
                w = c.nch * SLOTS

                def product(j, u):
                    dve.wait_ge(m.h_full, j + 1)
                    dve.wait_ge(m.silu2, j + 1)
                    nc.vector.tensor_tensor(hg[u][0:c.mc, 0:c.nch, :], sg[u][0:c.mc, 0:w].rearrange("p (c n) -> p c n", c=c.nch),
                                            ps[0:c.mc, 3 + u, 0:w].rearrange("p (c n) -> p c n", c=c.nch), ALU.mult).then_inc(m.hg_made, 1)

                pairs = dve.value_load(more_pairs[i][:, :], min_val=c.least_pairs - 2, max_val=c.nt // 2 - 2) + 2
                with dve.Fori(0, pairs) as k:
                    product(2 * k, 0)
                    product(2 * k + 1, 1)

            first_norms, images = attention(0)
            first_norms(0)
            first_norms(1)
            for i in range(2):
                images()
                shared(i, 0, None)
                dve.wait_ge(S[i].tile_ids, 2)
                experts(i)
                if i == 0:
                    first_norms, images = attention(1)
                    shared(0, 1, first_norms)
                else:
                    shared(1, 1, None)

        @block.gpsimd
        def _(pool):
            pool.wait_ge(const_made, 5)
            pool.wait_ge(tk_rs, 1)
            nc.gpsimd.tensor_tensor(rs[:, :], vt[:, :], half[:, 0:B], ALU.pow).then_inc(tk_rs, 1)

            def attention(i):
                c, m = L[i], S[i]

                def power(b, mv_, ve_, rstd_, ready, chain, done):
                    pool.wait_ge(ready, 2 * b + 2)
                    nc.gpsimd.tensor_tensor(ve_[:, :], mv_[:, :, 1], eps2[:, :], ALU.add).then_inc(chain, 1)
                    pool.wait_ge(chain, b + 1)
                    nc.gpsimd.tensor_tensor(rstd_[:, :], ve_[:, :], half[0:P, 0:2], ALU.pow).then_inc(done, 1)

                def save(b):
                    pool.wait_ge(m.xn2, 2 * b + 2)
                    nc.gpsimd.tensor_copy(XN[:, ds(2 * b, 2), :], xn2[:, :, :]).then_inc(m.xn_saved, 1)
                    pool.wait_ge(m.xT2, b + 1)
                    nc.gpsimd.tensor_copy(XT[:, :, ds(b * N, N)], xT2[0:KC, :, :]).then_inc(m.xT_saved, 1)

                power(0, mv, ve, rstd, m.mvr, m.ve_c, m.rs)
                power(1, mv, ve, rstd, m.mvr, m.ve_c, m.rs)
                with pool.Fori(0, B - 2) as b:
                    power(b + 2, mv, ve, rstd, m.mvr, m.ve_c, m.rs)
                    power(b, mv2, ve2, rstd2, m.mv2r, m.ve2_c, m.rs2)
                    save(b)
                for b in (B - 2, B - 1):
                    power(b, mv2, ve2, rstd2, m.mv2r, m.ve2_c, m.rs2)
                    save(b)

            def scatter(i):
                m = S[i]
                pool.wait_ge(zero_fill, 16 * sum((n + 5) // 6 for c in L for n in (c.nt, c.nt - 2 * c.least_pairs)))
                pool.wait_ge(m.slots, 2)
                pool.wait_ge(m.xn_saved, B)
                for t in range(T):
                    for k in range(2):
                        nc.gpsimd.indirect_dma_start(out=Xs[i], out_offset=bass.IndirectOffsetOnAxis(ap=slot[k][:, t:t + 1], axis=0),
                                                     in_=XN[:, t, :], in_offset=None).then_inc(m.scat, 16)

            def gather(i):
                c, m = L[i], S[i]
                pool.wait_ge(m.tile_ids, 2)
                pairs = pool.value_load(more_pairs[i][:, :], min_val=c.least_pairs - 2, max_val=c.nt // 2 - 2) + 2
                pool.wait_ge(m.y_st0, 16 * pairs)
                pool.wait_ge(m.y_st1, 16 * pairs)
                nc.gpsimd.tensor_tensor(carrier2[:, :], eps2[:, :], eps2[:, :], ALU.add)
                for n, t in [(n, t) for n, tiles_ in enumerate(groups) for t in tiles_]:
                    for k in range(2):
                        nc.gpsimd.indirect_dma_start(out=yg[t][:, k, :], out_offset=None, in_=Ys[i],
                                                     in_offset=bass.IndirectOffsetOnAxis(ap=slot[k][:, t:t + 1], axis=0)).then_inc(gathered[n], 16)

            for i in range(2):
                attention(i)
                scatter(i)
                gather(i)


def _layouts(np, z):
    f = np.float32
    out = {}
    out["xp"] = z["x"].reshape(B, 3, 6, 16, 6, 16).transpose(1, 3, 5, 0, 2, 4).reshape(6, 128, B, NP).transpose(1, 2, 0, 3).reshape(128, B, 6 * NP)
    for n, k in (("ln_w", "L0_tok_ln_w"), ("ln_b", "L0_tok_ln_b")):
        out[n] = z[k].reshape(3, 6, 16, 6, 16).transpose(0, 2, 4, 1, 3).reshape(6, 128, NP).transpose(1, 0, 2).reshape(128, 6 * NP)
    out["proj_t"] = z["L0_tok_proj_w"].T.reshape(6, 128, D).transpose(1, 0, 2)
    out["conv_w"] = np.broadcast_to(z["L0_tok_conv_w"].reshape(1, 9), (128, 9))
    out["conv_b"] = np.broadcast_to(z["L0_tok_conv_b"].reshape(1, 3), (128, 3))
    out["pos_emb"] = z["L0_tok_pos_emb"].reshape(NP, D)
    out["proj_b"] = np.broadcast_to(z["L0_tok_proj_b"].reshape(1, D), (NP, D))
    out["txt"] = z["txt"]

    def halves(w, bias):
        n = w.shape[1]
        r = np.zeros((KC + 1, 2, n), f)
        r[0:KC] = w.reshape(2, KC, n).transpose(1, 0, 2)
        r[KC, 1] = bias
        return r

    def spread(w):
        r = np.zeros((w.shape[0], HEADS, 32), f)
        r[:, :, 0:16] = w.reshape(w.shape[0], HEADS, 16)
        return r.reshape(w.shape[0], 384)

    w, bias = z["L0_attn_qkv_w"], z["L0_attn_qkv_b"]
    q, k = (halves(spread(w[n * D:(n + 1) * D].T), spread(bias[n * D:(n + 1) * D].reshape(1, D))[0]) for n in range(2))
    out["wqk0"] = np.concatenate([q, k], axis=2)
    out["wv0"] = halves(w[2 * D:].T, bias[2 * D:])
    out["wo0"] = spread(z["L0_attn_proj_w"]).T.reshape(3, 128, D).transpose(1, 0, 2)
    out["bo0"] = z["L0_attn_proj_b"].reshape(1, D)
    out["wr0"] = halves(z["L0_ffn_gate_w"].T, np.zeros(16, f))
    flat = lambda n: z[n].transpose(1, 0, 2).reshape(D, 768)
    out["wqk1"] = np.concatenate([halves(flat("L1_attn_W_Q"), z["L1_attn_b_Q"].reshape(768)), halves(flat("L1_attn_W_K"), z["L1_attn_b_K"].reshape(768))], axis=2)
    out["wv1"] = halves(flat("L1_attn_W_V"), z["L1_attn_b_V"].reshape(768))
    out["wo1"] = z["L1_attn_W_O"].reshape(6, 128, D).transpose(1, 0, 2)
    out["bo1"] = z["L1_attn_b_O"].reshape(1, D)
    out["wr1"] = np.concatenate([halves(z["L1_ffn_router_w"], np.zeros(8, f)), halves(z["L1_ffn_sg_w"], z["L1_ffn_sg_b"])], axis=2)
    rows = lambda w: w.reshape(2, KC, w.shape[1]).transpose(1, 0, 2)
    out["wg0"], out["wu0"] = rows(z["L0_ffn_sw1"].T), rows(z["L0_ffn_sw3"].T)
    out["wd0"] = z["L0_ffn_sw2"].T.reshape(8, 128, D).transpose(1, 0, 2)
    out["wg1"], out["wu1"] = rows(z["L1_ffn_ws_gate"]), rows(z["L1_ffn_ws_up"])
    out["wd1"] = z["L1_ffn_ws_down"].reshape(6, 128, D).transpose(1, 0, 2)
    for name, k in (("we_gate0", "L0_ffn_w1"), ("we_up0", "L0_ffn_w3")):
        out[name] = z[k].transpose(0, 2, 1).reshape(16, 2, KC, 512).transpose(0, 2, 1, 3)
    out["we_down0"] = z["L0_ffn_w2"].transpose(0, 2, 1).reshape(16, 4, 128, D).transpose(0, 2, 1, 3)
    for name, k in (("we_gate1", "L1_ffn_w_gate"), ("we_up1", "L1_ffn_w_up"), ("we_down1", "L1_ffn_w_down")):
        out[name] = z[k].reshape(8, 2, KC, D).transpose(0, 2, 1, 3)

    c = np.zeros((128, C_ALL), f)
    c[:, C_ID:C_ID + 128] = np.eye(128)
    c[0:P, C_TRI:C_TRI + P] = np.triu(np.ones((P, P)), 1)
    hidden = np.triu(np.ones((P, P)), 1) * -1e38
    c[0:P, C_M0:C_M0 + P] = hidden
    c[0:P, C_M1 + P:C_M1 + N] = hidden
    c[:, C_STEP:C_STEP + ACCROSS] = np.arange(ACCROSS) * SLOTS
    c[:, C_TILE:C_TILE + 36] = np.arange(36)
    for i, e in enumerate((16, 8)):
        c[:, C_DESC[i]:C_DESC[i] + e] = e - np.arange(e)
        c[:, C_BEF[i]:C_BEF[i] + e * e] = (np.arange(e)[:, None] > np.arange(e)[None, :]).reshape(e * e)
    out["consts"] = c
    return out


def kernel(**inputs):
    import numpy as _np
    import concourse.bacc as _bacc
    from concourse import mybir as _mybir
    from concourse.bass_utils import run_bass_kernel_spmd as _run

    nc = _bacc.Bacc("TRN2", target_bir_lowering=False, num_devices=1)
    arrays, args = {}, {}
    for name, v in _layouts(_np, {k: _np.asarray(v) for k, v in inputs.items()}).items():
        v = _np.ascontiguousarray(v)
        arrays[f"in_{name}"] = v
        args[name] = nc.dram_tensor(f"in_{name}", v.shape, _mybir.dt.from_np(v.dtype), kind="ExternalInput").ap()
    out = nc.dram_tensor("out_0_dram", (B, N, D), F32, kind="ExternalOutput").ap()
    build(nc, args, out)
    r = _run(nc, [arrays], core_ids=[0])
    return r.results[0]["out_0_dram"]
```

```python
from contextlib import ExitStack

import concourse.bass as bass
from concourse import mybir

ALU = mybir.AluOpType
ACT = mybir.ActivationFunctionType
AX = mybir.AxisListType
F32 = mybir.dt.float32
F32R = mybir.dt.float32r
BF16 = mybir.dt.bfloat16
I32 = mybir.dt.int32
U32 = mybir.dt.uint32
ds = bass.ds

B = 8
D = 192
KC = 96
NP = 36
TXT = 128
N = NP + TXT
P = N // 2
T = 2 * B
HEADS = 12
EPS = 1e-5
G = 3
PAIRS = HEADS // G
SLOTS = 128
ACCROSS = 11


class Shapes:
    pass


class Signals:
    pass


def layer_shapes(layer):
    s = Shapes()
    s.dh = (16, 64)[layer]
    s.stride = (32, 64)[layer]
    s.chunks = (3, 6)[layer]
    s.causal = (False, True)[layer]
    s.scale = s.dh ** -0.5
    s.e = (16, 8)[layer]
    s.hidden = (512, 192)[layer]
    s.mc = (128, 96)[layer]
    s.shared = (1024, 768)[layer]
    s.gate = (False, True)[layer]
    s.width = s.stride * HEADS
    s.vwidth = s.dh * HEADS
    s.per_chunk = 128 // s.stride
    s.qk_jobs = 2 * s.chunks // 3
    s.v_parts = (1, 2)[layer]
    s.v_cols = s.vwidth // s.v_parts
    s.proj_jobs = s.qk_jobs + 2 * s.v_parts
    s.jobs = s.proj_jobs + 2 * PAIRS
    s.o_banks = s.chunks // 3
    s.ew = s.e + (1 if s.gate else 0)
    if layer == 0:
        s.order = [g + 4 * n for g in range(PAIRS) for n in range(G)]
    else:
        s.order = [6 * (g // 2) + g % 2 + 2 * n for g in range(PAIRS) for n in range(G)]
    s.nch = s.hidden // s.mc
    s.sch = s.shared // 128
    s.s_jobs = s.sch * B // 2
    s.nt = (2 * B * N + s.e * (SLOTS - 1)) // SLOTS
    s.least_pairs = (2 * B * N + 2 * SLOTS - 1) // (2 * SLOTS)
    assert s.jobs % 4 == 0 and s.nt % 2 == 0
    return s


SPLITS = 8
ROW = D + 1
NO_ROW = 1 << 20
EMPTY_ROWS = 6 * N // ROW
BEFORE = 3 * B // 4


def fills(layers):
    return sum(-(-c.nt // EMPTY_ROWS) for c in layers)


C_ID = 0
C_TRI = C_ID + 128
C_MASK = C_TRI + P
C_STEP = C_MASK + P
C_TILE = C_STEP + ACCROSS
C_DESC = [C_TILE + 36, C_TILE + 36 + 16]
C_BEF = [C_DESC[1] + 8, C_DESC[1] + 8 + 256]
C_TOK = [C_BEF[1] + 64, C_BEF[1] + 64 + T]
C_ALL = C_TOK[1] + T


def build(nc, a, out):
    L = [layer_shapes(0), layer_shapes(1)]
    with ExitStack() as ctx:
        def sb(name, shape, dt=F32):
            return ctx.enter_context(nc.sbuf_tensor(name, shape, dt))

        def sem(name):
            return ctx.enter_context(nc.semaphore(name))

        ps = ctx.enter_context(nc.psum_tensor("ps", [128, 8, 512], F32))
        RING, PSE, PSO, PSA = 0, 4, 6, 7

        H = sb("H", [P, T, D])
        XN = sb("XN", [P, T, ROW])
        XTh = sb("XTh", [KC, 2, B * N], F32R)
        XTl = sb("XTl", [KC, 2, B * N], F32R)
        consts = sb("consts", [128, C_ALL])
        ident = consts[:, C_ID:C_ID + 128]
        ident_b = sb("ident_b", [P, P], BF16)
        mask_b = sb("mask_b", [P, G, P], BF16)
        ones = sb("ones", [128, 128])
        half = sb("half", [128, 16])
        eps2 = sb("eps2", [P, 2])
        carrier = sb("carrier", [P, 2])
        carrier2 = sb("carrier2", [P, 2, 2])
        wqk = sb("wqk", [KC + 1, 2, 2 * 768])
        wv = sb("wv", [KC + 1, 2, 768])
        wo = sb("wo", [128, 6, D])
        bo = sb("bo", [P, D])
        wr = sb("wr", [KC + 1, 2, 16])
        stats = sb("stats", [P, 2, 6])
        mv = sb("mv", [P, 2, 2])
        ve = sb("ve", [P, 2])
        rstd = sb("rstd", [P, 2])
        xn = sb("xn", [P, 2, D])
        xT = sb("xT", [KC + 1, 2, N])
        stats2 = sb("stats2", [P, 2, 6])
        mv2 = sb("mv2", [P, 2, 2])
        ve2 = sb("ve2", [P, 2])
        rstd2 = sb("rstd2", [P, 2])
        xn2 = sb("xn2", [P, 2, D])
        xT2 = sb("xT2", [KC + 1, 2, N])
        qT = sb("qT", [128, HEADS, N])
        kT = sb("kT", [128, 6, N])
        V = [sb(f"V{u}", [P, 2, 768]) for u in range(2)]
        top = sb("top", [P, 4, G])
        nb = sb("nb", [P, 4, G])
        sums = sb("sums", [P, 2, 2 * G])
        rsum = sb("rsum", [P, 2, 2 * G])
        Ex = [sb(f"Ex{i}", [P, 2, G, N]) for i in range(2)]
        ET = [sb(f"ET{i}", [P, 2, N]) for i in range(2)]
        OT = sb("OT", [128, 6, N])
        empty = OT[:, :, :].rearrange("p k n -> p (k n)")[:, 0:EMPTY_ROWS * ROW].rearrange("p (n d) -> p n d", d=ROW)
        LG = sb("LG", [P, T, 17])
        split = [[sb(f"w_{w}_{part}", [KC, 2 * 1024], F32R) for part in ("high", "low")] for w in ("gate", "up")]
        wd = sb("wd", [128, 8, D])
        sg = [sb(f"sg{i}", [128, 512]) for i in range(2)]
        gT = sb("gT", [128, 4, 2 * N])
        w13_whole = [sb(f"w13_{i}", [128, 2, 2, 512]) for i in range(2)]
        w13 = [[[x[0:KC, w, :, :].rearrange("p k n -> p (k n)")[:, 0:2 * c.hidden].rearrange("p (k n) -> p k n", k=2) for w in range(2)]
                for x in w13_whole] for c in L]
        whole = [x[0:KC, :, :, :].rearrange("p w k n -> p (w k n)") for x in w13_whole]
        w2 = [sb(f"w2_{i}", [128, 4, D]) for i in range(2)]
        xs = [sb(f"xs{i}", [SLOTS, D]) for i in range(2)]
        xsT = [sb(f"xsT{i}", [KC, 2, SLOTS]) for i in range(2)]
        hg = [sb(f"hg{i}", [128, 4, SLOTS]) for i in range(2)]
        ys = [sb(f"ys{i}", [SLOTS, D]) for i in range(2)]
        yg = [[XN[:, 8 * n:8 * n + 8, 0:D] for n in range(2)],
              [v_[:, :, :].rearrange("p s n -> p (s n)").rearrange("p (t d) -> p t d", d=D) for v_ in V]]
        row_of = [sb(f"row_of{i}", [SLOTS, 2]) for i in range(2)]
        E16 = 16
        r_mx = sb("r_mx", [P, T])
        r_p, r_q, r_eq, r_v, pos, r_bef = (qT[0:P, :, :].rearrange("p h n -> p (h n)")[:, n * T * E16:(n + 1) * T * E16].rearrange("p (t e) -> p t e", t=T)
                                           for n in range(6))
        r_cmp = qT[0:P, :, :].rearrange("p h n -> p (h n)")[:, 6 * T * E16:6 * T * E16 + E16 * ACCROSS].rearrange("p (e n) -> p e n", e=E16)
        r_sm = sb("r_sm", [P, T])
        r_vm = sb("r_vm", [P, T])
        onehot = [sb(f"onehot{i}", [P, T, E16]) for i in range(2)]
        chosen = sb("chosen", [P, T, E16])
        gate = [sb(f"gate{i}", [P, T]) for i in range(2)]
        scan = [sb(f"scan{i}", [P, 9 + T, E16]) for i in range(2)]
        count = sb("count", [P, E16])
        tiles = sb("tiles", [P, E16])
        base = sb("base", [P, E16])
        last = sb("last", [P, E16])
        r_id = kT[0:1, :, :].rearrange("p k n -> p (k n)")[:, 0:36 * E16].rearrange("p (j e) -> p j e", j=36)
        idf = sb("idf", [1, 36])
        expert = [sb(f"expert{i}", [1, 36], I32) for i in range(2)]
        r_np = sb("r_np", [1, 18])
        npf = sb("npf", [1, 1])
        more_pairs = [sb(f"more_pairs{i}", [1, 1], I32) for i in range(2)]
        slotf = sb("slotf", [P, T])
        slot = [sb(f"slot{i}", [P, T], U32) for i in range(2)]
        alpha = sb("alpha", [P, T])
        first, second = (x[:, :, :, :].rearrange("p w k n -> p (w k n)") for x in w13_whole)
        xp = first[:, 0:B * 6 * NP].rearrange("p (b n) -> p b n", b=B)
        pf = second[:, 0:6 * D].rearrange("p (j d) -> p j d", j=6)
        at = 6 * D
        lnw, lnb, junk = (second[:, at + n * 6 * NP:at + (n + 1) * 6 * NP] for n in range(3))
        at += 3 * 6 * NP
        cbr = second[:, at:at + 3 * NP].rearrange("p (o n) -> p o n", o=3)
        pw = wd[:, 0:6, :]
        tokT = kT[0:KC, :, :].rearrange("p k n -> p (k n)")[:, 0:2 * B * NP].rearrange("p (k n) -> p k n", k=2)
        cw = sb("cw", [128, 9])
        cb = sb("cb", [128, 3])
        pos_emb = sb("pos_emb", [NP, D])
        pb = sb("pb", [NP, D])
        psum1 = sb("psum1", [128, B])
        mean = sb("mean", [128, B])
        sq = sb("sq", [128, B])
        vt = sb("vt", [128, B])
        rs = sb("rs", [128, B])
        cmat = sb("cmat", [NP, D])

        Xs = [nc.dram_tensor(f"sorted_rows{i}", (L[i].nt * SLOTS, ROW), F32, kind="Internal").ap() for i in range(2)]
        Ys = [nc.dram_tensor(f"expert_out{i}", (2 * B * N, D), F32, kind="Internal").ap() for i in range(2)]

        ld_x = sem("ld_x"); ld_tok = sem("ld_tok"); ld_txt = sem("ld_txt"); ld_const = sem("ld_const")
        const_made = sem("const_made")
        tk = sem("tk"); tk_sum = sem("tk_sum"); tk_tot = sem("tk_tot"); tk_sq = sem("tk_sq")
        tk_rs = sem("tk_rs"); tk_fold = sem("tk_fold"); tk_mm = sem("tk_mm"); tk_done = sem("tk_done")
        written = sem("written")
        gathered = [sem(f"gathered{n}") for n in range(2)]

        def layer_signals(i):
            m = Signals()
            m.ld_att = sem(f"ld_att_L{i}")
            m.ld_shared = sem(f"ld_shared_L{i}")
            m.st = sem(f"st_L{i}")
            m.mvr = sem(f"mvr_L{i}")
            m.ve_c = sem(f"ve_c_L{i}")
            m.rs = sem(f"rs_L{i}")
            m.xn = sem(f"xn_L{i}")
            m.xnT = sem(f"xnT_L{i}")
            m.xT = sem(f"xT_L{i}")
            m.ring_full = sem(f"ring_full_L{i}")
            m.proj_used = sem(f"proj_used_L{i}")
            m.scores_used = sem(f"scores_used_L{i}")
            m.cleared = sem(f"cleared_L{i}")
            m.nbc = sem(f"nbc_L{i}")
            m.nb = sem(f"nb_L{i}")
            m.rsc = sem(f"rsc_L{i}")
            m.e_norm = sem(f"e_norm_L{i}")
            m.eT_full = sem(f"eT_full_L{i}")
            m.eT_copied = sem(f"eT_copied_L{i}")
            m.pv = sem(f"pv_L{i}")
            m.o_copied = sem(f"o_copied_L{i}")
            m.outp = sem(f"outp_L{i}")
            m.resid = sem(f"resid_L{i}")
            m.st2 = sem(f"st2_L{i}")
            m.mv2r = sem(f"mv2r_L{i}")
            m.rs2 = sem(f"rs2_L{i}")
            m.xn2 = sem(f"xn2_L{i}")
            m.xn2T = sem(f"xn2T_L{i}")
            m.xT2 = sem(f"xT2_L{i}")
            m.router = sem(f"router_L{i}")
            m.logits = sem(f"logits_L{i}")
            m.xn_saved = sem(f"xn_saved_L{i}")
            m.xT_saved = sem(f"xT_saved_L{i}")
            m.r = sem(f"r_L{i}")
            m.r_exp = sem(f"r_exp_L{i}")
            m.oh_made = sem(f"oh_made_L{i}")
            m.rank = sem(f"rank_L{i}")
            m.slots = sem(f"slots_L{i}")
            m.tile_ids = sem(f"tile_ids_L{i}")
            m.scat = sem(f"scat_L{i}")
            m.gu_full = sem(f"gu_full_L{i}")
            m.silu = sem(f"silu_L{i}")
            m.gu_used = sem(f"gu_used_L{i}")
            m.d_full = sem(f"d_full_L{i}")
            m.d_used = sem(f"d_used_L{i}")
            m.xs0 = sem(f"xs0_L{i}")
            m.xs1 = sem(f"xs1_L{i}")
            m.w1_0 = sem(f"w1_0_L{i}")
            m.w1_1 = sem(f"w1_1_L{i}")
            m.w3_0 = sem(f"w3_0_L{i}")
            m.w3_1 = sem(f"w3_1_L{i}")
            m.w2_0 = sem(f"w2_0_L{i}")
            m.w2_1 = sem(f"w2_1_L{i}")
            m.xs_T = sem(f"xs_T_L{i}")
            m.xsT_made = sem(f"xsT_made_L{i}")
            m.gate_full = sem(f"gate_full_L{i}")
            m.h_full = sem(f"h_full_L{i}")
            m.silu2 = sem(f"silu2_L{i}")
            m.hg_made = sem(f"hg_made_L{i}")
            m.y_full = sem(f"y_full_L{i}")
            m.w_split = sem(f"w_split_L{i}")
            m.xT_high = sem(f"xT_high_L{i}")
            m.gT_used = sem(f"gT_used_L{i}")
            m.y_copied = sem(f"y_copied_L{i}")
            m.y_st0 = sem(f"y_st0_L{i}")
            m.y_st1 = sem(f"y_st1_L{i}")
            m.rows_in0 = sem(f"rows_in0_L{i}")
            m.rows_in1 = sem(f"rows_in1_L{i}")
            m.carried = sem(f"carried_L{i}")
            m.comb = sem(f"comb_L{i}")
            return m

        S = [layer_signals(0), layer_signals(1)]
        block = ctx.enter_context(nc.Block())

        def klen(c, s):
            return P if c.causal and s == 0 else N

        @block.sync
        def _(sp):
            sp.dma_start(xp, a["xp"]).then_inc(ld_x, 16)
            sp.dma_start(consts[:], a["consts"]).then_inc(ld_const, 16)
            for dst, name in ((pw, "proj_t"), (cw[:], "conv_w"), (cb[:], "conv_b"), (lnw, "ln_w"),
                              (lnb, "ln_b"), (pos_emb[:], "pos_emb"), (pb[:], "proj_b")):
                sp.dma_start(dst, a[name]).then_inc(ld_tok, 16)
            head_rows = P - NP
            sp.dma_start(H[NP:P, 0:T:2, :], a["txt"][:, 0:head_rows, :].rearrange("b p d -> p b d")).then_inc(ld_txt, 16)
            sp.dma_start(H[:, 1:T:2, :], a["txt"][:, head_rows:TXT, :].rearrange("b p d -> p b d")).then_inc(ld_txt, 16)

            def load_attention(i):
                c, m = L[i], S[i]
                for dst, name in ((wqk[:, :, 0:2 * c.width], "wqk"), (wv[:, :, 0:c.vwidth], "wv"),
                                  (wo[:, 0:c.chunks, :], "wo"), (bo[:], "bo"), (wr[:, :, 0:c.ew], "wr")):
                    sp.dma_start(dst, a[f"{name}{i}"]).then_inc(m.ld_att, 16)

            def load_shared(i):
                c, m = L[i], S[i]
                for dst, name in ((whole[0][:, 0:2 * c.shared], "wg"), (whole[1][:, 0:2 * c.shared], "wu")):
                    sp.dma_start(dst, a[f"{name}{i}"].rearrange("p k n -> p (k n)")).then_inc(m.ld_shared, 16)
                sp.dma_start(wd[:, 0:c.sch, :], a[f"wd{i}"]).then_inc(m.ld_shared, 16)

            def load_experts(i):
                c, m = L[i], S[i]
                sp.wait_ge(m.tile_ids, 2)
                sp.wait_ge(m.w_split, 4 * SPLITS)

                def expert_of(j):
                    return sp.value_load(expert[i][0:1, ds(j, 1)], min_val=0, max_val=c.e - 1)

                def up_weights(j, u, first):
                    e = expert_of(j)
                    if not first:
                        sp.wait_ge(m.gate_full, j - 1)
                    sp.dma_start(w13[i][u][0], a[f"we_gate{i}"][ds(e, 1)].rearrange("e p k n -> p (e k) n")).then_inc((m.w1_0, m.w1_1)[u], 16)
                    if not first:
                        sp.wait_ge(m.h_full, j - 1)
                    sp.dma_start(w13[i][u][1], a[f"we_up{i}"][ds(e, 1)].rearrange("e p k n -> p (e k) n")).then_inc((m.w3_0, m.w3_1)[u], 16)

                def rows(j, u, first):
                    if not first:
                        sp.wait_ge(m.xs_T, j - 1)
                    sp.dma_start(xs[u][:], Xs[i][ds(j * SLOTS, SLOTS), 0:D]).then_inc((m.xs0, m.xs1)[u], 16)

                pairs = sp.value_load(more_pairs[i][:, :], min_val=c.least_pairs - 2, max_val=c.nt // 2 - 2) + 2
                for u in range(2):
                    up_weights(u, u, True)
                sp.wait_ge(m.scat, 16 * 2 * T)
                for u in range(2):
                    rows(u, u, True)
                for u in range(2):
                    rows(2 + u, u, False)
                up_weights(2, 0, False)
                with sp.Fori(2, pairs) as k:
                    rows(2 * k, 0, False)
                    up_weights(2 * k - 1, 1, False)
                    rows(2 * k + 1, 1, False)
                    up_weights(2 * k, 0, False)
                up_weights(2 * pairs - 1, 1, False)
                sp.wait_ge(m.y_st0, 16 * pairs)
                sp.wait_ge(m.y_st1, 16 * pairs)
                for n in range(2):
                    for k in range(2):
                        at = k * B * N + 8 * n * P
                        sp.dma_start(yg[k][n], Ys[i][at:at + 8 * P, :].rearrange("(t p) d -> p t d", p=P)).then_inc(gathered[n], 16)

            load_attention(0)
            sp.wait_ge(const_made, 4)
            for c, rows_ in zip(L, Xs):
                by_partition = rows_.rearrange("(p n) d -> p n d", p=128)
                for o in range(0, c.nt, EMPTY_ROWS):
                    n = min(EMPTY_ROWS, c.nt - o)
                    sp.dma_start(by_partition[:, o:o + n, :], empty[:, 0:n, :]).then_inc(written, 16)
            sp.wait_ge(tk_mm, 3)
            sp.wait_ge(tk, 1 + 2 * B + 9 + 2)
            load_shared(0)
            sp.wait_ge(S[0].router, B)
            load_attention(1)
            load_experts(0)
            sp.wait_ge(S[0].gT_used, L[0].s_jobs)
            load_shared(1)
            load_experts(1)
            for t in range(T):
                if t < T - 4:
                    sp.wait_ge(S[1].comb, 8 * (t // 8) + 8 + t + 1)
                else:
                    sp.wait_ge(S[1].d_used, t + 1)
                b, s = divmod(t, 2)
                sp.dma_start(out[b, s * P:(s + 1) * P, :], H[:, t, :]).then_inc(written, 16)
            sp.wait_ge(written, 16 * (fills(L) + T))

        @block.tensor
        def _(pe):
            def mm(o, l, r, start=True, stop=True):
                return nc.tensor.matmul(o, l, r, start=start, stop=stop, skip_group_check=True)

            pe.wait_ge(const_made, 1)
            pe.wait_ge(tk_sum, 1)
            mm(ps[:, 0, 0:B], ones[:, :], psum1[:, :]).then_inc(tk_tot, 1)
            pe.wait_ge(tk_sq, B)
            mm(ps[:, 0, 16:16 + B], ones[:, :], sq[:, :]).then_inc(tk_tot, 1)
            pe.wait_ge(tk_fold, 1)
            for j in range(6):
                last_c = mm(ps[0:NP, 1, 0:D], cbr[:, j // 2, :], pw[:, j, :], start=(j == 0), stop=(j == 5))
            last_c.then_inc(tk_mm, 1)
            for g in range(2):
                pe.wait_ge(tk_fold, 2 + g)
                for k in range(2):
                    for j in range(6):
                        last_c = mm(ps[0:KC, 2 + 2 * g + k, 0:4 * NP].rearrange("p (b n) -> p b n", b=4), pf[:, j, k * KC:(k + 1) * KC],
                                    xp[:, 4 * g:4 * g + 4, j * NP:(j + 1) * NP], start=(j == 0), stop=(j == 5))
                last_c.then_inc(tk_mm, 1)
            pe.wait_ge(tk, 1 + 2 * B + 9 + 1)
            for q in range(4):
                pe.wait_ge(tk_sq, B + 1 + q // 2)
                for b in (2 * q, 2 * q + 1):
                    for k in range(2):
                        last_c = nc.tensor.transpose(ps[0:NP, (6, 7, 0, 1)[q], (b % 2) * D + k * KC:(b % 2) * D + (k + 1) * KC],
                                                     tokT[:, k, b * NP:(b + 1) * NP], ident[0:KC, 0:KC])
                last_c.then_inc(tk_mm, 1)

            def attention(i):
                c, m = L[i], S[i]
                pq = c.per_chunk

                def turn_x(b):
                    pe.wait_ge(m.xn, 2 * b + 2)
                    for s in range(2):
                        for k in range(2):
                            t_ = nc.tensor.transpose(ps[0:KC, PSA, k * N + s * P:k * N + (s + 1) * P],
                                                     xn[:, s, k * KC:(k + 1) * KC], ident[0:P, 0:P])
                    t_.then_inc(m.xnT, 1)

                def ring(b, first, job):
                    if job < 4:
                        if not first:
                            pe.wait_ge(m.scores_used, 2 * PAIRS * b + job - 3)
                    elif job < c.proj_jobs + 4:
                        pe.wait_ge(m.proj_used, c.proj_jobs * b + job - 3)
                    else:
                        pe.wait_ge(m.scores_used, 2 * PAIRS * b + job - c.proj_jobs - 3)
                    return ps[:, RING + job % 4, :]

                def project(b, first):
                    pe.wait_ge(m.xT, b + 1)
                    for j in range(c.qk_jobs):
                        bank = ring(b, first, j)
                        for n in range(3):
                            col = (3 * j + n) * 128
                            mm(bank[:, n * N:(n + 1) * N], wqk[0:KC, 0, col:col + 128], xT[0:KC, 0, :], True, False)
                            x_ = mm(bank[:, n * N:(n + 1) * N], wqk[:, 1, col:col + 128], xT[:, 1, :], False, True)
                        x_.then_inc(m.ring_full, 1)
                    for s in range(2):
                        for q in range(c.v_parts):
                            bank = ring(b, first, c.qk_jobs + s * c.v_parts + q)
                            vw = c.v_cols
                            mm(bank[0:P, 0:vw], xT[0:KC, 0, s * P:(s + 1) * P], wv[0:KC, 0, q * vw:(q + 1) * vw], True, False)
                            mm(bank[0:P, 0:vw], xT[:, 1, s * P:(s + 1) * P], wv[:, 1, q * vw:(q + 1) * vw], False, True).then_inc(m.ring_full, 1)

                def scores(b, g, s, first):
                    if g == 0:
                        pe.wait_ge(m.proj_used, c.proj_jobs * (b + 1))
                    bank = ring(b, first, c.proj_jobs + 2 * g + s)
                    kl = klen(c, s)
                    if c.causal:
                        own = bank[0:P, 0:G * kl].rearrange("p (h k) -> p h k", h=G)[:, :, kl - P:kl]
                        mm(own, ident_b[:, :], mask_b[:, :, :], True, False)
                    for n in range(G):
                        q = c.order[G * g + n] // pq
                        x_ = mm(bank[0:P, n * kl:(n + 1) * kl], qT[:, G * g + n, s * P:(s + 1) * P],
                                kT[:, q, 0:kl], not c.causal, True)
                    x_.then_inc(m.ring_full, 1)

                def values(b, x, first, u):
                    pe.wait_ge(m.eT_copied, HEADS * b + x + 1)
                    per_bank = HEADS // c.o_banks
                    if x % per_bank == 0 and not (first and x == 0):
                        pe.wait_ge(m.o_copied, c.o_banks * b + x // per_bank)
                    h = c.order[x]
                    r, q = c.stride * (h % pq), (h // pq) % 3
                    o_ = ps[r:r + c.stride, PSO, q * N:(q + 1) * N]
                    mm(o_, V[u][:, 0, h * c.dh:h * c.dh + c.stride], ET[x % 2][:, 0, :], True, False)
                    if c.causal:
                        x_ = mm(o_[:, P:N], V[u][:, 1, h * c.dh:h * c.dh + c.stride], ET[x % 2][:, 1, 0:P], False, True)
                    else:
                        x_ = mm(o_, V[u][:, 1, h * c.dh:h * c.dh + c.stride], ET[x % 2][:, 1, :], False, True)
                    x_.then_inc(m.pv, 1)

                def turn_head(b, x, first):
                    g, n = x // G, x % G
                    if n == 0:
                        pe.wait_ge(m.e_norm, PAIRS * b + g + 1)
                    if not (first and x < 2):
                        pe.wait_ge(m.eT_copied, HEADS * b + x - 1)
                    bank = ps[0:P, PSE + x % 2, :]
                    for kc in range(2):
                        for s in range(2):
                            if c.causal and kc > s:
                                continue
                            at = kc * N + (0 if c.causal and kc else s * P)
                            x_ = nc.tensor.transpose(bank[:, at:at + P], Ex[g % 2][:, s, n, kc * P:(kc + 1) * P], ident[0:P, 0:P])
                    x_.then_inc(m.eT_full, 1)

                def pair(b, g, first, u, b_scores, g_scores, first_scores):
                    x = G * g
                    turn_head(b, x, first)
                    turn_head(b, x + 1, first)
                    if g_scores is not None:
                        scores(b_scores, g_scores, 0, first_scores)
                    values(b, x, first, u)
                    turn_head(b, x + 2, first)
                    values(b, x + 1, first, u)
                    if g == PAIRS - 1:
                        values(b, x + 2, first, u)
                    if g_scores is not None:
                        scores(b_scores, g_scores, 1, first_scores)
                    if g < PAIRS - 1:
                        values(b, x + 2, first, u)

                def out_project(b):
                    pe.wait_ge(m.o_copied, c.o_banks * (b + 1))
                    for s in range(2):
                        o_ = ps[0:P, PSA, s * D:(s + 1) * D]
                        for q in range(c.chunks):
                            x_ = mm(o_, OT[:, q, s * P:(s + 1) * P], wo[:, q, :], q == 0, q == c.chunks - 1)
                    x_.then_inc(m.outp, 1)

                def turn_x2(b):
                    pe.wait_ge(m.xn2, 2 * b + 2)
                    for s in range(2):
                        for k in range(2):
                            t_ = nc.tensor.transpose(ps[0:KC, PSA, k * N + s * P:k * N + (s + 1) * P],
                                                     xn2[:, s, k * KC:(k + 1) * KC], ident[0:P, 0:P])
                    t_.then_inc(m.xn2T, 1)

                def route(b):
                    pe.wait_ge(m.xT2, b + 1)
                    for s in range(2):
                        o_ = ps[0:P, PSA, s * c.ew:(s + 1) * c.ew]
                        mm(o_, xT2[0:KC, 0, s * P:(s + 1) * P], wr[0:KC, 0, 0:c.ew], True, False)
                        x_ = mm(o_, xT2[:, 1, s * P:(s + 1) * P], wr[:, 1, 0:c.ew], False, True)
                    x_.then_inc(m.router, 1)

                def body(b, u, first, is_last):
                    if first:
                        for g in range(2):
                            for s in range(2):
                                scores(b, g, s, True)
                        turn_x(b + 1)
                    else:
                        pair(b - 1, 2, False, 1 - u, b, 0, False)
                        if not is_last:
                            turn_x(b + 1)
                        pair(b - 1, 3, False, 1 - u, b, 1, False)
                        out_project(b - 1)
                    pair(b, 0, first, u, b, 2, first)
                    pair(b, 1, first, u, b, 3, first)
                    if not first:
                        turn_x2(b - 1)
                    if not is_last:
                        project(b + 1, False)
                    if not first:
                        route(b - 1)

                def images():
                    pe.wait_ge(m.ld_att, 16 * 5)
                    if i:
                        pe.wait_ge(S[0].gu_used, L[0].s_jobs)
                    project(0, True)
                    if i:
                        pe.wait_ge(S[0].d_used, T)
                    body(0, 0, True, False)
                    with pe.Fori(0, (B - 2) // 2) as k:
                        body(2 * k + 1, 1, False, False)
                        body(2 * k + 2, 0, False, False)
                    body(B - 1, 1, False, True)
                    pair(B - 1, 2, False, 1, None, None, False)
                    pair(B - 1, 3, False, 1, None, None, False)
                    out_project(B - 1)
                    pe.wait_ge(m.ld_shared, 16 * 3)
                    pe.wait_ge(m.w_split, 4 * SPLITS)
                    pe.wait_ge(m.xT_saved, 2)
                    pe.wait_ge(m.scores_used, 2 * PAIRS * B)
                    shared_up(i, 0)
                    shared_up(i, 1)
                    turn_x2(B - 1)
                    route(B - 1)

                return turn_x, images

            def shared_up(i, job):
                c, m = L[i], S[i]
                two, q = divmod(job, c.sch)
                if job >= 2:
                    pe.wait_ge(m.gu_used, job - 1)
                for w, bank in ((0, job % 2), (1, 2 + job % 2)):
                    n = 0
                    for k in range(2):
                        at = k * c.shared + q * 128
                        high, low = (x[:, at:at + 128] for x in split[w])
                        for l, r in ((low, XTh), (high, XTh), (high, XTl)):
                            x_ = mm(ps[:, bank, 0:2 * N], l, r[:, k, 2 * two * N:2 * (two + 1) * N], n == 0, n == 5)
                            n += 1
                x_.then_inc(m.gu_full, 1)

            def shared(i, half_, turn_x):
                c, m = L[i], S[i]

                def down(job):
                    two, q = divmod(job, c.sch)
                    pe.wait_ge(m.gu_used, job + 1)
                    if q == 0 and two:
                        pe.wait_ge(m.d_used, 4 * two)
                    for t in range(4):
                        x_ = mm(ps[0:P, 4 + t // 2, (t % 2) * D:(t % 2 + 1) * D], gT[:, job % 4, t * P:(t + 1) * P], wd[:, q, :],
                                q == 0 and t % 2 == 0, q == c.sch - 1)
                        if q == c.sch - 1 and t == 1:
                            x_.then_inc(m.d_full, 1)
                    x_.then_inc(m.gT_used, 1)

                first, end = ((0, BEFORE // 2 * c.sch), (BEFORE // 2 * c.sch, c.s_jobs))[half_]
                if half_ == 0:
                    pe.wait_ge(m.logits, B)
                else:
                    shared_up(i, first)
                    shared_up(i, first + 1)
                for job in range(first + 2, end):
                    if job == c.sch:
                        pe.wait_ge(m.xT_saved, B)
                    shared_up(i, job)
                    down(job - 2)
                    if job == 5:
                        pe.wait_ge(m.oh_made, 1)
                        mm(ps[0:P, 6, 0:T * c.e], consts[0:P, C_TRI:C_TRI + P], chosen[:, :, 0:c.e])
                        mm(ps[0:P, 7, 0:T * c.e], ones[0:P, 0:P], chosen[:, :, 0:c.e]).then_inc(m.rank, 1)
                if turn_x:
                    turn_x(0)
                down(end - 2)
                down(end - 1)

            def experts(i):
                c, m = L[i], S[i]

                def turn(j, u, k, first):
                    pe.wait_ge((m.xs0, m.xs1)[u], 16 * (k + 1))
                    if not first:
                        pe.wait_ge(m.xsT_made, j)
                    for n in range(2):
                        x_ = nc.tensor.transpose(ps[0:KC, 0, n * SLOTS:(n + 1) * SLOTS], xs[u][:, n * KC:(n + 1) * KC], ident)
                    x_.then_inc(m.xs_T, 1)

                def up(j, u, k, first):
                    pe.wait_ge(m.xsT_made, j + 1)
                    if not first:
                        pe.wait_ge(m.hg_made, j - 1)
                    for w in range(2):
                        pe.wait_ge(((m.w1_0, m.w1_1), (m.w3_0, m.w3_1))[w][u], 16 * (k + 1))
                        for n in range(c.nch):
                            for q in range(2):
                                x_ = mm(ps[0:c.mc, 1 + 2 * w + u, n * SLOTS:(n + 1) * SLOTS], w13[i][u][w][:, q, n * c.mc:(n + 1) * c.mc],
                                        xsT[u][:, q, :], q == 0, q == 1)
                        x_.then_inc((m.gate_full, m.h_full)[w], 1)

                def down(j, u, k, first):
                    pe.wait_ge((m.w2_0, m.w2_1)[u], 16 * (k + 1))
                    pe.wait_ge(m.hg_made, j + 1)
                    if not first:
                        pe.wait_ge(m.y_copied, j - 1)
                    for n in range(c.nch):
                        x_ = mm(ps[:, 5 + u, 0:D], hg[u][0:c.mc, n, :], w2[u][0:c.mc, n, :], n == 0, n == c.nch - 1)
                    x_.then_inc(m.y_full, 1)

                def two_tiles(k, first):
                    turn(2 * k, 0, k, False)
                    up(2 * k - 1, 1, k - 1, first)
                    down(2 * k - 2, 0, k - 1, first)
                    turn(2 * k + 1, 1, k, False)
                    up(2 * k, 0, k, False)
                    down(2 * k - 1, 1, k - 1, first)

                pairs = pe.value_load(more_pairs[i][:, :], min_val=c.least_pairs - 2, max_val=c.nt // 2 - 2) + 2
                pe.wait_ge(m.gu_used, BEFORE // 2 * c.sch)
                pe.wait_ge(m.d_used, 2 * BEFORE)
                turn(0, 0, 0, True)
                turn(1, 1, 0, False)
                up(0, 0, 0, True)
                two_tiles(1, True)
                with pe.Fori(2, pairs) as k:
                    two_tiles(k, False)
                up(2 * pairs - 1, 1, pairs - 1, False)
                down(2 * pairs - 2, 0, pairs - 1, False)
                down(2 * pairs - 1, 1, pairs - 1, False)
                pe.wait_ge(m.y_copied, 2 * pairs)

            pe.wait_ge(tk_done, 4)
            turn_x, images = attention(0)
            turn_x(0)
            for i in range(2):
                images()
                shared(i, 0, None)
                pe.wait_ge(S[i].tile_ids, 2)
                experts(i)
                if i == 0:
                    turn_x, images = attention(1)
                    shared(0, 1, turn_x)
                else:
                    shared(1, 1, None)

        @block.scalar
        def _(act):
            act.wait_ge(tk, 1 + B)
            for b in range(B):
                if b:
                    act.wait_ge(tk_sq, b)
                nc.scalar.activation(junk[:, :], xp[:, b, :], ACT.Square, accum_out=sq[:, b:b + 1]).then_inc(tk_sq, 1)
            for g in range(2):
                act.wait_ge(tk_mm, 2 + g)
                for k in range(2):
                    x_ = nc.scalar.copy(tokT[:, k, 4 * g * NP:4 * (g + 1) * NP], ps[0:KC, 2 + 2 * g + k, 0:4 * NP])
                x_.then_inc(tk_sq, 1)

            def attention(i):
                c, m = L[i], S[i]

                def copy_xT(b):
                    act.wait_ge(m.xnT, b + 1)
                    nc.scalar.copy(xT[0:KC, :, :], ps[0:KC, PSA, 0:2 * N].rearrange("p (k n) -> p k n", k=2)).then_inc(m.xT, 1)

                def exps(b, g, halves=(0, 1), heads=range(G)):
                    for s in halves:
                        j = c.proj_jobs + 2 * g + s
                        kl = klen(c, s)
                        act.wait_ge(m.nb, 2 * PAIRS * b + 2 * g + s + 1)
                        for n in heads:
                            x_ = nc.scalar.activation(Ex[g % 2][:, s, n, 0:kl], ps[0:P, RING + j % 4, n * kl:(n + 1) * kl], ACT.Exp,
                                                      bias=nb[:, (2 * g + s) % 4, n:n + 1], scale=c.scale,
                                                      accum_out=sums[:, g % 2, s * G + n:s * G + n + 1])
                        if G - 1 in heads:
                            x_.then_inc(m.scores_used, 1)

                def copy_head(b, h, first):
                    w = N + P if c.causal else 2 * N
                    act.wait_ge(m.eT_full, HEADS * b + h + 1)
                    if not (first and h < 2):
                        act.wait_ge(m.pv, HEADS * b + h - 1)
                    nc.scalar.copy(ET[h % 2][:, :, :].rearrange("p k n -> p (k n)")[:, 0:w], ps[0:P, PSE + h % 2, 0:w]).then_inc(m.eT_copied, 1)

                def copy_eT(b, g, first):
                    for n in range(G):
                        copy_head(b, G * g + n, first)

                def copy_eT_2(b, first):
                    copy_head(b, 6, False)
                    if c.o_banks == 2:
                        copy_out(b, 0, first)
                    copy_head(b, 7, False)
                    copy_head(b, 8, False)

                def copy_out(b, k, first):
                    if first and i == 0:
                        act.wait_ge(written, 16 * fills(L))
                    act.wait_ge(m.pv, HEADS * b + (k + 1) * (HEADS // c.o_banks))
                    if not first:
                        act.wait_ge(m.outp, b)
                    nc.scalar.copy(OT[:, 3 * k:3 * k + 3, :], ps[:, PSO, 0:3 * N].rearrange("p (k n) -> p k n", k=3)).then_inc(m.o_copied, 1)

                def copy_xT2(b, first):
                    act.wait_ge(m.xn2T, b + 1)
                    if not first:
                        act.wait_ge(m.xT_saved, b)
                    nc.scalar.copy(xT2[0:KC, :, :], ps[0:KC, PSA, 0:2 * N].rearrange("p (k n) -> p k n", k=2)).then_inc(m.xT2, 1)

                def copy_logits(b):
                    act.wait_ge(m.router, b + 1)
                    nc.scalar.copy(LG[:, ds(2 * b, 2), 0:c.ew], ps[0:P, PSA, 0:2 * c.ew].rearrange("p (s e) -> p s e", s=2)).then_inc(m.logits, 1)

                def body(b, u, first, second, is_last):
                    if not first:
                        copy_eT_2(b - 1, second)
                    if first or c.causal:
                        exps(b, 0, (0,))
                    if first:
                        exps(b, 0, (1,))
                    if not is_last:
                        copy_xT(b + 1)
                    if not first:
                        copy_head(b - 1, 9, False)
                        copy_head(b - 1, 10, False)
                        if not c.causal:
                            exps(b, 0, (0,), (0, 1))
                        copy_head(b - 1, 11, False)
                        copy_out(b - 1, c.o_banks - 1, second)
                        if not c.causal:
                            exps(b, 0, (0,), (2,))
                        exps(b, 0, (1,))
                    exps(b, 1)
                    copy_eT(b, 0, first)
                    exps(b, 2, (0,))
                    copy_head(b, G, first)
                    copy_head(b, G + 1, first)
                    exps(b, 2, (1,))
                    copy_head(b, G + 2, first)
                    if not first:
                        copy_xT2(b - 1, second)
                    exps(b, 3)
                    if not first:
                        copy_logits(b - 1)

                copy_xT(0)
                body(0, 0, True, False, False)
                body(1, 1, False, True, False)
                with act.Fori(1, B // 2 - 1) as k:
                    body(2 * k, 0, False, False, False)
                    body(2 * k + 1, 1, False, False, False)
                body(B - 2, 0, False, False, False)
                body(B - 1, 1, False, False, True)
                copy_eT_2(B - 1, False)
                copy_eT(B - 1, 3, False)
                copy_out(B - 1, c.o_banks - 1, False)
                shared_silu(i, 0, 0)
                shared_silu(i, 1, 1)
                copy_xT2(B - 1, False)
                copy_logits(B - 1)

            def route(i):
                c, m = L[i], S[i]
                act.wait_ge(m.r, 2)
                nc.scalar.activation(r_p[:, :, 0:c.e], r_q[:, :, 0:c.e], ACT.Exp).then_inc(m.r_exp, 1)
                if c.gate:
                    nc.scalar.activation(alpha[:, :], LG[:, :, c.e], ACT.Exp, scale=-1.0).then_inc(m.r_exp, 1)

            def shared_silu(i, job, u):
                act.wait_ge(S[i].gu_full, job + 1)
                nc.scalar.activation(sg[u][:, 0:2 * N], ps[:, u, 0:2 * N], ACT.Silu).then_inc(S[i].silu, 1)

            def shared(i, half_):
                before = BEFORE // 4 * L[i].sch + (BEFORE // 2 % 2) * L[i].sch // 2
                with act.Fori(before if half_ else 1, L[i].s_jobs // 2 if half_ else before) as k:
                    for u in range(2):
                        shared_silu(i, 2 * k + u, u)

            def experts(i):
                c, m = L[i], S[i]
                w = c.nch * SLOTS

                def copy_x(j, u, first):
                    act.wait_ge(m.xs_T, j + 1)
                    if not first:
                        act.wait_ge(m.h_full, j - 1)
                    nc.scalar.copy(xsT[u][:, :, :], ps[0:KC, 0, 0:2 * SLOTS].rearrange("p (k n) -> p k n", k=2)).then_inc(m.xsT_made, 1)

                def silu(j, u):
                    act.wait_ge(m.gate_full, j + 1)
                    nc.scalar.activation(sg[u][0:c.mc, 0:w], ps[0:c.mc, 1 + u, 0:w], ACT.Silu).then_inc(m.silu2, 1)

                def copy_y(j, u, k, first):
                    if not first:
                        act.wait_ge((m.y_st0, m.y_st1)[u], 16 * k)
                    act.dma_start(row_of[u][:, :], Xs[i][ds(j * SLOTS, SLOTS), ROW - 2:ROW]).then_inc((m.rows_in0, m.rows_in1)[u], 16)
                    act.wait_ge(m.y_full, j + 1)
                    nc.scalar.copy(ys[u][:, :], ps[:, 5 + u, 0:D]).then_inc(m.y_copied, 1)

                def down_weights(j, u):
                    e = act.value_load(expert[i][0:1, ds(j, 1)], min_val=0, max_val=c.e - 1)
                    act.dma_start(w2[u][0:c.mc, 0:c.nch, :], a[f"we_down{i}"][ds(e, 1)].rearrange("e p k n -> p (e k) n")).then_inc((m.w2_0, m.w2_1)[u], 16)

                def two_tiles(k, first):
                    copy_x(2 * k, 0, False)
                    silu(2 * k - 1, 1)
                    copy_y(2 * k - 2, 0, k - 1, first)
                    down_weights(2 * k, 0)
                    copy_x(2 * k + 1, 1, False)
                    silu(2 * k, 0)
                    copy_y(2 * k - 1, 1, k - 1, first)
                    down_weights(2 * k + 1, 1)

                pairs = act.value_load(more_pairs[i][:, :], min_val=c.least_pairs - 2, max_val=c.nt // 2 - 2) + 2
                down_weights(0, 0)
                down_weights(1, 1)
                copy_x(0, 0, True)
                copy_x(1, 1, True)
                silu(0, 0)
                two_tiles(1, True)
                with act.Fori(2, pairs) as k:
                    two_tiles(k, False)
                silu(2 * pairs - 1, 1)
                copy_y(2 * pairs - 2, 0, pairs - 1, False)
                copy_y(2 * pairs - 1, 1, pairs - 1, False)

            for i in range(2):
                attention(i)
                route(i)
                shared(i, 0)
                act.wait_ge(S[i].tile_ids, 2)
                experts(i)
                shared(i, 1)

        @block.vector
        def _(dve):
            nc.vector.memset(ones[:, :], 1.0).then_inc(const_made, 1)
            nc.vector.memset(half[:, :], -0.5).then_inc(const_made, 1)
            nc.vector.memset(empty, 0.0).then_inc(const_made, 1)
            dve.wait_ge(const_made, 3)
            nc.vector.memset(empty.bitcast(U32)[:, :, D:ROW], NO_ROW).then_inc(const_made, 1)
            nc.vector.memset(carrier[:, :], 0.0).then_inc(const_made, 1)
            nc.vector.memset(eps2[:, :], EPS).then_inc(const_made, 1)
            for t_ in (xT, xT2):
                nc.vector.memset(t_[KC:KC + 1, :, :], 1.0).then_inc(const_made, 1)
            for t_ in scan:
                nc.vector.memset(t_[:, :, :], 0.0).then_inc(const_made, 1)

            n_img = 6 * 128 * NP
            dve.wait_ge(ld_x, 16)
            nc.vector.tensor_reduce(psum1[:, :], xp[:, :, :], AX.X, ALU.add).then_inc(tk_sum, 1)
            dve.wait_ge(tk_tot, 1)
            nc.vector.tensor_scalar(mean[:, :], ps[:, 0, 0:B], 1.0 / n_img, None, ALU.mult).then_inc(tk, 1)
            dve.wait_ge(tk, 1)
            for b in range(B):
                nc.vector.tensor_scalar(xp[:, b, :], xp[:, b, :], mean[:, b:b + 1], None, ALU.subtract).then_inc(tk, 1)
            dve.wait_ge(ld_tok, 16 * 7)
            for o in range(3):
                nc.vector.tensor_scalar(cbr[:, o, :], ones[:, 0:NP], cb[:, o:o + 1], None, ALU.mult)
            nc.vector.memset(cmat[:, :], 0.0).then_inc(tk_fold, 1)
            for o in range(3):
                if o == 2:
                    dve.wait_ge(tk_tot, 2)
                    nc.vector.tensor_scalar(vt[:, :], ps[:, 0, 16:16 + B], 1.0 / n_img, EPS, ALU.mult, ALU.add).then_inc(tk_rs, 1)
                for ci in range(3):
                    dst = pf[:, 2 * ci:2 * ci + 2, :]
                    src = pw[:, 2 * o:2 * o + 2, :]
                    if o == 0:
                        nc.vector.tensor_scalar(dst, src, cw[:, 3 * o + ci:3 * o + ci + 1], None, ALU.mult).then_inc(tk, 1)
                    else:
                        dve.wait_ge(tk, 1 + B + 3 * (o - 1) + ci + 1)
                        nc.vector.scalar_tensor_tensor(out=dst, in0=src, scalar=cw[:, 3 * o + ci:3 * o + ci + 1], in1=dst,
                                                       op0=ALU.mult, op1=ALU.add).then_inc(tk, 1)
            dve.wait_ge(tk_rs, 2)
            for g in range(2):
                for b in range(4 * g, 4 * g + 4):
                    nc.vector.scalar_tensor_tensor(out=xp[:, b, :], in0=xp[:, b, :], scalar=rs[:, b:b + 1], in1=lnw[:, :],
                                                   op0=ALU.mult, op1=ALU.mult).then_inc(tk, 1)
                for b in range(4 * g, 4 * g + 4):
                    dve.wait_ge(tk, 1 + B + 9 + b + 1)
                    x_ = nc.vector.tensor_tensor(xp[:, b, :], xp[:, b, :], lnb[:, :], ALU.add)
                x_.then_inc(tk_fold, 1)
            dve.wait_ge(tk_mm, 1)
            nc.vector.tensor_tensor(cmat[:, :], ps[0:NP, 1, 0:D], pos_emb[:, :], ALU.add).then_inc(tk, 1)
            dve.wait_ge(tk, 1 + 2 * B + 9 + 1)
            nc.vector.tensor_tensor(cmat[:, :], cmat[:, :], pb[:, :], ALU.add).then_inc(tk, 1)
            dve.wait_ge(tk, 1 + 2 * B + 9 + 2)
            dve.wait_ge(ld_const, 16)
            nc.vector.tensor_copy(ident_b[:, :], ident[0:P, 0:P]).then_inc(const_made, 1)
            nc.vector.tensor_copy(mask_b[:, :, :], consts[0:P, C_MASK:C_MASK + P].unsqueeze(1).to_broadcast([P, G, P])).then_inc(const_made, 1)
            def add_tokens(q):
                dve.wait_ge(tk_mm, 4 + q)
                nc.vector.tensor_tensor(H[0:NP, 4 * q:4 * q + 4:2, :], ps[0:NP, (6, 7, 0, 1)[q], 0:2 * D].rearrange("p (b d) -> p b d", b=2),
                                        cmat[:, :].unsqueeze(1).to_broadcast([NP, 2, D]), ALU.add).then_inc(tk_done, 1)

            def clear(i):
                c, m = L[i], S[i]
                nc.vector.memset(qT[:, :, :], 0.0).then_inc(m.cleared, 1)
                if c.dh < c.stride:
                    for v_ in V:
                        nc.vector.memset(v_[:, :, c.vwidth:c.vwidth + c.dh], 0.0).then_inc(m.cleared, 1)

            def carry_wait():
                nc.vector.tensor_copy(carrier[:, 1:2], carrier[:, 0:1])

            def attention(i):
                c, m = L[i], S[i]

                def norm_stats(b):
                    for s in range(2):
                        nc.vector.bn_stats(stats[:, s, :], H[:, ds(2 * b + s, 1), :].rearrange("p o d -> p (o d)")).then_inc(m.st, 1)
                    dve.wait_ge(m.st, 2 * b + 2)
                    carry_wait()
                    for s in range(2):
                        nc.vector.bn_aggr(mv[:, s, :], stats[:, s, :]).then_inc(m.mvr, 1)

                def add_bias(b):
                    h_ = H[:, ds(2 * b, 2), :]
                    nc.vector.tensor_tensor(h_, h_, bo[:, :].unsqueeze(1).to_broadcast([P, 2, D]), ALU.add).then_inc(m.resid, 1)

                def norm_apply(b, first):
                    dve.wait_ge(m.rs, b + 1)
                    if not first:
                        dve.wait_ge(m.xnT, b)
                    for s in range(2):
                        nc.vector.tensor_scalar(xn[:, s, :], H[:, ds(2 * b + s, 1), :].rearrange("p o d -> p (o d)"), mv[:, s, 0:1], rstd[:, s:s + 1],
                                                ALU.subtract, ALU.mult).then_inc(m.xn, 1)

                def copy_proj(b, u):
                    half_ = c.qk_jobs // 2
                    def bank(j):
                        dve.wait_ge(m.ring_full, b * c.jobs + j + 1)
                        return ps[:, RING + j % 4, :]
                    for j in range(half_):
                        k_ = bank(j)
                        for r in range(c.per_chunk):
                            rows = slice(c.stride * r, c.stride * (r + 1))
                            g = 2 * j + r
                            x_ = nc.vector.tensor_copy(qT[rows, G * g:G * g + G, :], k_[rows, 0:3 * N].rearrange("p (k n) -> p k n", k=3))
                        x_.then_inc(m.proj_used, 1)
                    for j in range(half_):
                        nc.vector.tensor_copy(kT[:, 3 * j:3 * j + 3, :], bank(half_ + j)[:, 0:3 * N].rearrange("p (k n) -> p k n", k=3)).then_inc(m.proj_used, 1)
                    for s in range(2):
                        for q in range(c.v_parts):
                            nc.vector.tensor_copy(V[u][:, s, q * c.v_cols:(q + 1) * c.v_cols],
                                                  bank(c.qk_jobs + s * c.v_parts + q)[0:P, 0:c.v_cols]).then_inc(m.proj_used, 1)

                def maxima(b, g):
                    for s in range(2):
                        j = c.proj_jobs + 2 * g + s
                        r = (2 * g + s) % 4
                        kl = klen(c, s)
                        done = 2 * PAIRS * b + 2 * g + s + 1
                        dve.wait_ge(m.ring_full, b * c.jobs + j + 1)
                        nc.vector.tensor_reduce(top[:, r, :], ps[0:P, RING + j % 4, 0:G * kl].rearrange("p (h k) -> p h k", h=G), AX.X, ALU.max).then_inc(m.nbc, 1)
                        dve.wait_ge(m.nbc, done)
                        nc.vector.tensor_scalar(nb[:, r, :], top[:, r, :], -c.scale, None, ALU.mult).then_inc(m.nb, 1)

                def normalise(b, g):
                    dve.wait_ge(m.scores_used, 2 * PAIRS * b + 2 * g + 2)
                    nc.vector.reciprocal(rsum[:, g % 2, :], sums[:, g % 2, :]).then_inc(m.rsc, 1)
                    dve.wait_ge(m.rsc, PAIRS * b + g + 1)
                    if c.causal:
                        for s in range(2):
                            kl = klen(c, s)
                            e_ = Ex[g % 2][:, s, :, 0:kl]
                            x_ = nc.vector.tensor_tensor(e_, e_, rsum[:, g % 2, s * G:(s + 1) * G].unsqueeze(2).to_broadcast([P, G, kl]), ALU.mult)
                    else:
                        e_ = Ex[g % 2][:, :, :, :].rearrange("p s h k -> p (s h) k")
                        x_ = nc.vector.tensor_tensor(e_, e_, rsum[:, g % 2, :].unsqueeze(2).to_broadcast([P, 2 * G, N]), ALU.mult)
                    x_.then_inc(m.e_norm, 1)

                def residual(b, missing):
                    dve.wait_ge(m.outp, b + 1)
                    dve.wait_ge(m.resid, 2 * b + 3 - missing)
                    h_ = H[:, ds(2 * b, 2), :]
                    nc.vector.tensor_tensor(h_, h_, ps[0:P, PSA, 0:2 * D].rearrange("p (s d) -> p s d", s=2), ALU.add).then_inc(m.resid, 1)
                    dve.wait_ge(m.resid, 2 * b + 4 - missing)
                    carry_wait()
                    for s in range(2):
                        nc.vector.bn_stats(stats2[:, s, :], H[:, ds(2 * b + s, 1), :].rearrange("p o d -> p (o d)")).then_inc(m.st2, 1)
                    dve.wait_ge(m.st2, 2 * b + 2)
                    carry_wait()
                    for s in range(2):
                        nc.vector.bn_aggr(mv2[:, s, :], stats2[:, s, :]).then_inc(m.mv2r, 1)

                def norm_apply2(b, first):
                    dve.wait_ge(m.rs2, b + 1)
                    if not first:
                        dve.wait_ge(m.xn2T, b)
                        dve.wait_ge(m.xn_saved, b)
                    for s in range(2):
                        nc.vector.tensor_scalar(xn2[:, s, :], H[:, ds(2 * b + s, 1), :].rearrange("p o d -> p (o d)"), mv2[:, s, 0:1], rstd2[:, s:s + 1],
                                                ALU.subtract, ALU.mult).then_inc(m.xn2, 1)

                def body(b, u, first, second, is_last, is_last2):
                    if not first:
                        normalise(b - 1, 3)
                    if not is_last:
                        norm_apply(b + 1, False)
                    maxima(b, 0)
                    if not is_last:
                        add_bias(b + 1)
                    maxima(b, 1)
                    normalise(b, 0)
                    normalise(b, 1)
                    if not first:
                        residual(b - 1, 1 if is_last else 0)
                    maxima(b, 2)
                    if not first:
                        norm_apply2(b - 1, second)
                    if not is_last2:
                        norm_stats(b + 2)
                    maxima(b, 3)
                    normalise(b, 2)
                    if not is_last:
                        copy_proj(b + 1, 1 - u)

                def first_norms(part):
                    if part == 0:
                        if i:
                            dve.wait_ge(S[0].comb, 16)
                        norm_stats(0)
                        return
                    norm_apply(0, True)
                    norm_stats(1)

                def images():
                    dve.wait_ge(m.cleared, 3 if c.dh < c.stride else 1)
                    dve.wait_ge(m.ld_att, 16 * 5)
                    if i:
                        dve.wait_ge(S[0].comb, 2 * T)
                    add_bias(0)
                    copy_proj(0, 0)
                    body(0, 0, True, False, False, False)
                    body(1, 1, False, True, False, False)
                    with dve.Fori(1, B // 2 - 1) as k:
                        body(2 * k, 0, False, False, False, False)
                        body(2 * k + 1, 1, False, False, False, False)
                    body(B - 2, 0, False, False, False, True)
                    body(B - 1, 1, False, False, True, True)
                    normalise(B - 1, 3)
                    residual(B - 1, 2)
                    norm_apply2(B - 1, False)

                return first_norms, images

            def route(i, shared_job):
                c, m = L[i], S[i]
                E = c.e
                n = [0]

                def step(ins):
                    n[0] += 1
                    ins.then_inc(m.r, 1)

                def after():
                    dve.wait_ge(m.r, n[0])

                def over_e(x):
                    return x.unsqueeze(2).to_broadcast([P, T, E])

                dve.wait_ge(m.logits, B)
                nc.vector.tensor_copy(XN[:, :, :].bitcast(U32)[:, :, D], consts[0:P, C_TOK[0]:C_TOK[0] + T])
                lg = LG[:, :, 0:E]
                p, q = r_p[:, :, 0:E], r_q[:, :, 0:E]
                eq, v = r_eq[:, :, 0:E], r_v[:, :, 0:E]
                oh = [x[:, :, 0:E] for x in onehot]
                step(nc.vector.tensor_reduce(r_mx[:, :], lg, AX.X, ALU.max))
                after()
                step(nc.vector.tensor_tensor(q, lg, over_e(r_mx[:, :]), ALU.subtract))
                shared_job(2)
                dve.wait_ge(m.r_exp, 2 if c.gate else 1)
                step(nc.vector.tensor_reduce(r_sm[:, :], p, AX.X, ALU.add))
                after()
                step(nc.vector.reciprocal(r_sm[:, :], r_sm[:, :]))
                after()
                step(nc.vector.tensor_tensor(p, p, over_e(r_sm[:, :]), ALU.mult))
                shared_job(3)
                after()
                desc = consts[0:P, C_DESC[i]:C_DESC[i] + E].unsqueeze(1).to_broadcast([P, T, E])
                for k in range(2):
                    step(nc.vector.tensor_reduce(gate[k][:, :], p, AX.X, ALU.max))
                    after()
                    step(nc.vector.tensor_tensor(eq, p, over_e(gate[k][:, :]), ALU.is_equal))
                    after()
                    step(nc.vector.tensor_tensor(v, eq, desc, ALU.mult))
                    after()
                    step(nc.vector.tensor_reduce(r_vm[:, :], v, AX.X, ALU.max))
                    after()
                    step(nc.vector.tensor_tensor(oh[k], v, over_e(r_vm[:, :]), ALU.is_equal))
                    after()
                    if k == 0:
                        step(nc.vector.scalar_tensor_tensor(out=p, in0=oh[0], scalar=-2.0, in1=p, op0=ALU.mult, op1=ALU.add))
                        shared_job(4)
                        after()
                nc.vector.tensor_tensor(chosen[:, :, 0:E], oh[0], oh[1], ALU.add).then_inc(m.oh_made, 1)
                shared_job(5)

                def mix_gates():
                    step(nc.vector.tensor_scalar(alpha[:, :], alpha[:, :], 1.0, None, ALU.add))
                    after()
                    step(nc.vector.reciprocal(alpha[:, :], alpha[:, :]))
                    step(nc.vector.tensor_tensor(r_sm[:, :], gate[0][:, :], gate[1][:, :], ALU.add))
                    after()
                    step(nc.vector.reciprocal(r_sm[:, :], r_sm[:, :]))
                    step(nc.vector.tensor_scalar(r_vm[:, :], alpha[:, :], -1.0, 1.0, ALU.mult, ALU.add))
                    after()
                    step(nc.vector.tensor_tensor(r_sm[:, :], r_sm[:, :], r_vm[:, :], ALU.mult))
                    after()
                    for k in range(2):
                        step(nc.vector.tensor_tensor(gate[k][:, :], gate[k][:, :], r_sm[:, :], ALU.mult))
                    after()

                def assign_slots():
                    dve.wait_ge(m.rank, 1)
                    rank = ps[0:P, 6, 0:T * E].rearrange("p (t e) -> p t e", t=T)
                    total = ps[0:P, 7, 0:T * E].rearrange("p (t e) -> p t e", t=T)
                    z = 8
                    step(nc.vector.tensor_copy(scan[0][:, z + 1:z + 1 + T, 0:E], total))
                    after()
                    for k, sh in enumerate((1, 2, 4, 8)):
                        x, y = scan[k % 2], scan[(k + 1) % 2]
                        step(nc.vector.tensor_tensor(y[:, z:z + 1 + T, 0:E], x[:, z:z + 1 + T, 0:E], x[:, z - sh:z + 1 + T - sh, 0:E], ALU.add))
                        after()
                    shared_job(6)
                    before = scan[0]
                    step(nc.vector.tensor_tensor(r_cmp[:, 0:E, :], before[:, z + T, 0:E].unsqueeze(2).to_broadcast([P, E, ACCROSS]),
                                                 consts[0:P, C_STEP:C_STEP + ACCROSS].unsqueeze(1).to_broadcast([P, E, ACCROSS]), ALU.is_gt))
                    after()
                    step(nc.vector.tensor_reduce(tiles[:, 0:E], r_cmp[:, 0:E, :], AX.X, ALU.add))
                    after()
                    bef = r_bef[:, :, :].rearrange("p a b -> p (a b)")[:, 0:E * E].rearrange("p (a b) -> p a b", a=E)
                    step(nc.vector.tensor_tensor(bef, tiles[:, 0:E].unsqueeze(1).to_broadcast([P, E, E]),
                                                 consts[0:P, C_BEF[i]:C_BEF[i] + E * E].rearrange("p (a b) -> p a b", a=E), ALU.mult))
                    after()
                    step(nc.vector.tensor_reduce(base[:, 0:E], bef, AX.X, ALU.add))
                    after()
                    step(nc.vector.tensor_scalar(count[:, 0:E], base[:, 0:E], float(SLOTS), None, ALU.mult))
                    ps_, pf_ = pos[:, :, 0:E], before[:, z:z + T, 0:E]
                    step(nc.vector.tensor_tensor(ps_, rank, pf_, ALU.add))
                    after()
                    step(nc.vector.tensor_tensor(ps_, ps_, count[:, 0:E].unsqueeze(1).to_broadcast([P, T, E]), ALU.add))
                    after()
                    for k in range(2):
                        step(nc.vector.tensor_tensor(r_v[:, :, 0:E], ps_, oh[k], ALU.mult))
                        after()
                        step(nc.vector.tensor_reduce(slotf[:, :], r_v[:, :, 0:E], AX.X, ALU.add))
                        after()
                        nc.vector.tensor_copy(slot[k][:, :], slotf[:, :]).then_inc(m.slots, 1)
                    if c.gate:
                        mix_gates()
                    for job in range(7, 10):
                        shared_job(job)
                    step(nc.vector.tensor_tensor(last[:, 0:E], base[:, 0:E], tiles[:, 0:E], ALU.add))
                    after()
                    step(nc.vector.tensor_tensor(r_id[:, 0:c.nt, 0:E], last[0:1, 0:E].unsqueeze(1).to_broadcast([1, c.nt, E]),
                                                 consts[0:1, C_TILE:C_TILE + c.nt].unsqueeze(2).to_broadcast([1, c.nt, E]), ALU.is_le))
                    after()
                    step(nc.vector.tensor_reduce(idf[:, 0:c.nt], r_id[:, 0:c.nt, 0:E], AX.X, ALU.add))
                    after()
                    nc.vector.tensor_scalar(expert[i][:, 0:c.nt], idf[:, 0:c.nt], float(E - 1), None, ALU.min).then_inc(m.tile_ids, 1)
                    step(nc.vector.tensor_scalar(r_np[:, 0:c.nt // 2], consts[0:1, C_TILE:C_TILE + c.nt // 2], 2.0, last[0:1, E - 1:E], ALU.mult, ALU.is_lt))
                    after()
                    step(nc.vector.tensor_reduce(npf[:, :], r_np[:, 0:c.nt // 2], AX.X, ALU.add))
                    after()
                    nc.vector.tensor_scalar(more_pairs[i][:, :], npf[:, :], -2.0, None, ALU.add).then_inc(m.tile_ids, 1)

                return assign_slots

            def shared_job(i, job):
                c, m = L[i], S[i]
                u = job % 2
                dve.wait_ge(m.silu, job + 1)
                if job >= 4:
                    dve.wait_ge(m.gT_used, job - 3)
                nc.vector.tensor_tensor(gT[:, job % 4, :], sg[u][:, 0:2 * N], ps[:, 2 + u, 0:2 * N], ALU.mult).then_inc(m.gu_used, 1)
                two, q = divmod(job, c.sch)
                if q == 1 and two in (1, 2):
                    add(i, two - 1)

            def add(i, two):
                c, m = L[i], S[i]
                for s in range(2):
                    if s == 0:
                        dve.wait_ge(m.d_full, two + 1)
                    else:
                        dve.wait_ge(m.gT_used, c.sch * (two + 1))
                    t = 4 * two + 2 * s
                    sums_ = ps[0:P, 4 + s, 0:2 * D].rearrange("p (s d) -> p s d", s=2)
                    if c.gate:
                        for n in range(2):
                            nc.vector.scalar_tensor_tensor(out=H[:, t + n, :], in0=sums_[:, n, :], scalar=alpha[:, t + n:t + n + 1],
                                                           in1=H[:, t + n, :], op0=ALU.mult, op1=ALU.add).then_inc(m.d_used, 1)
                    else:
                        nc.vector.tensor_tensor(H[:, t:t + 2, :], sums_, H[:, t:t + 2, :], ALU.add).then_inc(m.d_used, 2)

            def combine(i, n, k):
                m = S[i]
                dve.wait_ge(gathered[n], 32 * (i + 1))
                for t in range(8 * n, 8 * n + 8):
                    if k:
                        dve.wait_ge(m.comb, 8 * n + t + 1)
                    elif t < 2 * BEFORE:
                        dve.wait_ge(m.d_used, t + 1)
                    nc.vector.scalar_tensor_tensor(out=H[:, t, :], in0=yg[k][n][:, t % 8, :], scalar=gate[k][:, t:t + 1], in1=H[:, t, :],
                                                   op0=ALU.mult, op1=ALU.add).then_inc(m.comb, 1)

            def shared(i, half_, first_norms):
                c, m = L[i], S[i]
                last = BEFORE // 2 * c.sch
                if half_ == 0:
                    route(i, lambda job: shared_job(i, job))()
                    if i == 0:
                        dve.wait_ge(m.slots, 2)
                        clear(1)
                    for job in range(10, last):
                        shared_job(i, job)
                    add(i, 2)
                    return
                for job in range(last, c.s_jobs):
                    shared_job(i, job)
                    if job == last + 2:
                        combine(i, 0, 0)
                    if job == last + 3:
                        combine(i, 0, 1)
                        if first_norms:
                            first_norms(0)
                    if job == last + 4:
                        combine(i, 1, 0)
                    if job == last + 5:
                        if first_norms:
                            first_norms(1)
                combine(i, 1, 1)
                dve.wait_ge(S[i].comb, 2 * T)
                add(i, 3)

            def experts(i):
                c, m = L[i], S[i]
                w = c.nch * SLOTS

                def product(j, u):
                    dve.wait_ge(m.h_full, j + 1)
                    dve.wait_ge(m.silu2, j + 1)
                    nc.vector.tensor_tensor(hg[u][0:c.mc, 0:c.nch, :], sg[u][0:c.mc, 0:w].rearrange("p (c n) -> p c n", c=c.nch),
                                            ps[0:c.mc, 3 + u, 0:w].rearrange("p (c n) -> p c n", c=c.nch), ALU.mult).then_inc(m.hg_made, 1)

                pairs = dve.value_load(more_pairs[i][:, :], min_val=c.least_pairs - 2, max_val=c.nt // 2 - 2) + 2
                with dve.Fori(0, pairs) as k:
                    product(2 * k, 0)
                    product(2 * k + 1, 1)

            first_norms, images = attention(0)
            clear(0)
            add_tokens(0)
            dve.wait_ge(ld_txt, 32)
            dve.wait_ge(tk_done, 1)
            first_norms(0)
            for q in range(1, 4):
                add_tokens(q)
            dve.wait_ge(tk_done, 4)
            first_norms(1)
            for i in range(2):
                images()
                shared_job(i, 0)
                shared_job(i, 1)
                shared(i, 0, None)
                dve.wait_ge(S[i].tile_ids, 2)
                experts(i)
                if i == 0:
                    first_norms, images = attention(1)
                    shared(0, 1, first_norms)
                else:
                    shared(1, 1, None)

        @block.gpsimd
        def _(pool):
            pool.wait_ge(const_made, 6)
            pool.wait_ge(tk_rs, 1)
            nc.gpsimd.tensor_tensor(rs[:, :], vt[:, :], half[:, 0:B], ALU.pow).then_inc(tk_rs, 1)

            def attention(i):
                c, m = L[i], S[i]

                def power(b, n, mv_, ve_, rstd_, ready, done):
                    pool.wait_ge(ready, 2 * b + 2)
                    nc.gpsimd.tensor_tensor(ve_[:, :], mv_[:, :, 1], eps2[:, :], ALU.add).then_inc(m.ve_c, 1)
                    pool.wait_ge(m.ve_c, n)
                    nc.gpsimd.tensor_tensor(rstd_[:, :], ve_[:, :], half[0:P, 0:2], ALU.pow).then_inc(done, 1)

                def save(b):
                    pool.wait_ge(m.xn2, 2 * b + 2)
                    nc.gpsimd.tensor_copy(XN[:, ds(2 * b, 2), 0:D], xn2[:, :, :]).then_inc(m.xn_saved, 1)
                    pool.wait_ge(m.xT2, b + 1)
                    nc.gpsimd.tensor_copy(XTh[:, :, ds(b * N, N)], xT2[0:KC, :, :]).then_inc(m.xT_high, 1)
                    pool.wait_ge(m.xT_high, b + 1)
                    nc.gpsimd.tensor_tensor(XTl[:, :, ds(b * N, N)], xT2[0:KC, :, :], XTh[:, :, :].bitcast(F32)[:, :, ds(b * N, N)],
                                            ALU.subtract).then_inc(m.xT_saved, 1)

                def split_weights(piece):
                    n = 2 * c.shared // SPLITS
                    at = ds(piece * n, n)
                    pool.wait_ge(m.ld_shared, 16 * 3)
                    for w in range(2):
                        nc.gpsimd.tensor_copy(split[w][0][:, at], whole[w][:, at]).then_inc(m.w_split, 1)
                    pool.wait_ge(m.w_split, 4 * piece + 2)
                    for w in range(2):
                        nc.gpsimd.tensor_tensor(split[w][1][:, at], whole[w][:, at], split[w][0][:, :].bitcast(F32)[:, at],
                                                ALU.subtract).then_inc(m.w_split, 1)

                power(0, 1, mv, ve, rstd, m.mvr, m.rs)
                power(1, 2, mv, ve, rstd, m.mvr, m.rs)
                with pool.Fori(0, B - 2) as b:
                    power(b + 2, 2 * b + 3, mv, ve, rstd, m.mvr, m.rs)
                    power(b, 2 * b + 4, mv2, ve2, rstd2, m.mv2r, m.rs2)
                    save(b)
                    split_weights(b)
                for piece in range(B - 2, SPLITS):
                    split_weights(piece)
                for b in (B - 2, B - 1):
                    power(b, B + b + 1, mv2, ve2, rstd2, m.mv2r, m.rs2)
                    save(b)

            def scatter(i):
                m = S[i]
                pool.wait_ge(written, 16 * fills(L))
                pool.wait_ge(m.xn_saved, B)
                for k in range(2):
                    pool.wait_ge(m.slots, k + 1)
                    if k:
                        pool.wait_ge(m.scat, 16 * T)
                        nc.gpsimd.tensor_copy(XN[:, :, :].bitcast(U32)[:, :, D], consts[0:P, C_TOK[1]:C_TOK[1] + T]).then_inc(m.xn_saved, 1)
                        pool.wait_ge(m.xn_saved, B + 1)
                    for t in range(T):
                        nc.gpsimd.indirect_dma_start(out=Xs[i], out_offset=bass.IndirectOffsetOnAxis(ap=slot[k][:, t:t + 1], axis=0),
                                                     in_=XN[:, t, :], in_offset=None).then_inc(m.scat, 16)

            def carry_waits(i, n):
                nc.gpsimd.tensor_tensor(carrier2[:, n, :], eps2[:, :], eps2[:, :], ALU.add).then_inc(S[i].carried, 1)

            def results(i):
                c, m = L[i], S[i]

                def store(j, u, k, first):
                    if not first and u == 0:
                        pool.wait_ge(m.carried, 2 * k)
                    pool.wait_ge(m.y_copied, j + 1)
                    pool.wait_ge((m.rows_in0, m.rows_in1)[u], 16 * (k + 1))
                    carry_waits(i, u)
                    nc.gpsimd.indirect_dma_start(out=Ys[i], out_offset=bass.IndirectOffsetOnAxis(ap=row_of[u][:, :].bitcast(U32)[:, 1:2], axis=0),
                                                 in_=ys[u][:, :], in_offset=None, bounds_check=2 * B * N - 1,
                                                 oob_is_err=False).then_inc((m.y_st0, m.y_st1)[u], 16)

                pool.wait_ge(m.tile_ids, 2)
                pairs = pool.value_load(more_pairs[i][:, :], min_val=c.least_pairs - 2, max_val=c.nt // 2 - 2) + 2
                for u in range(2):
                    store(u, u, 0, True)
                with pool.Fori(1, pairs) as k:
                    for u in range(2):
                        store(2 * k + u, u, k, False)

            for i in range(2):
                attention(i)
                scatter(i)
                results(i)


def _layouts(np, z):
    f = np.float32
    out = {}
    out["xp"] = z["x"].reshape(B, 3, 6, 16, 6, 16).transpose(1, 3, 5, 0, 2, 4).reshape(6, 128, B, NP).transpose(1, 2, 0, 3).reshape(128, B, 6 * NP)
    for n, k in (("ln_w", "L0_tok_ln_w"), ("ln_b", "L0_tok_ln_b")):
        out[n] = z[k].reshape(3, 6, 16, 6, 16).transpose(0, 2, 4, 1, 3).reshape(6, 128, NP).transpose(1, 0, 2).reshape(128, 6 * NP)
    out["proj_t"] = z["L0_tok_proj_w"].T.reshape(6, 128, D).transpose(1, 0, 2)
    out["conv_w"] = np.broadcast_to(z["L0_tok_conv_w"].reshape(1, 9), (128, 9))
    out["conv_b"] = np.broadcast_to(z["L0_tok_conv_b"].reshape(1, 3), (128, 3))
    out["pos_emb"] = z["L0_tok_pos_emb"].reshape(NP, D)
    out["proj_b"] = np.broadcast_to(z["L0_tok_proj_b"].reshape(1, D), (NP, D))
    out["txt"] = z["txt"]

    def halves(w, bias):
        n = w.shape[1]
        r = np.zeros((KC + 1, 2, n), f)
        r[0:KC] = w.reshape(2, KC, n).transpose(1, 0, 2)
        r[KC, 1] = bias
        return r

    def spread(w):
        r = np.zeros((w.shape[0], HEADS, 32), f)
        r[:, :, 0:16] = w.reshape(w.shape[0], HEADS, 16)
        return r.reshape(w.shape[0], 384)

    w, bias = z["L0_attn_qkv_w"], z["L0_attn_qkv_b"]
    q, k = (halves(spread(w[n * D:(n + 1) * D].T), spread(bias[n * D:(n + 1) * D].reshape(1, D))[0]) for n in range(2))
    out["wqk0"] = np.concatenate([q, k], axis=2)
    out["wv0"] = halves(w[2 * D:].T, bias[2 * D:])
    out["wo0"] = spread(z["L0_attn_proj_w"]).T.reshape(3, 128, D).transpose(1, 0, 2)
    out["bo0"] = np.broadcast_to(z["L0_attn_proj_b"].reshape(1, D), (P, D))
    out["wr0"] = halves(z["L0_ffn_gate_w"].T, np.zeros(16, f))
    flat = lambda n: z[n].transpose(1, 0, 2).reshape(D, 768)
    out["wqk1"] = np.concatenate([halves(flat("L1_attn_W_Q"), z["L1_attn_b_Q"].reshape(768)), halves(flat("L1_attn_W_K"), z["L1_attn_b_K"].reshape(768))], axis=2)
    out["wv1"] = halves(flat("L1_attn_W_V"), z["L1_attn_b_V"].reshape(768))
    out["wo1"] = z["L1_attn_W_O"].reshape(6, 128, D).transpose(1, 0, 2)
    out["bo1"] = np.broadcast_to(z["L1_attn_b_O"].reshape(1, D), (P, D))
    out["wr1"] = np.concatenate([halves(z["L1_ffn_router_w"], np.zeros(8, f)), halves(z["L1_ffn_sg_w"], z["L1_ffn_sg_b"])], axis=2)
    rows = lambda w: w.reshape(2, KC, w.shape[1]).transpose(1, 0, 2)
    out["wg0"], out["wu0"] = rows(z["L0_ffn_sw1"].T), rows(z["L0_ffn_sw3"].T)
    out["wd0"] = z["L0_ffn_sw2"].T.reshape(8, 128, D).transpose(1, 0, 2)
    out["wg1"], out["wu1"] = rows(z["L1_ffn_ws_gate"]), rows(z["L1_ffn_ws_up"])
    out["wd1"] = z["L1_ffn_ws_down"].reshape(6, 128, D).transpose(1, 0, 2)
    for name, k in (("we_gate0", "L0_ffn_w1"), ("we_up0", "L0_ffn_w3")):
        out[name] = z[k].transpose(0, 2, 1).reshape(16, 2, KC, 512).transpose(0, 2, 1, 3)
    out["we_down0"] = z["L0_ffn_w2"].transpose(0, 2, 1).reshape(16, 4, 128, D).transpose(0, 2, 1, 3)
    for name, k in (("we_gate1", "L1_ffn_w_gate"), ("we_up1", "L1_ffn_w_up"), ("we_down1", "L1_ffn_w_down")):
        out[name] = z[k].reshape(8, 2, KC, D).transpose(0, 2, 1, 3)

    c = np.zeros((128, C_ALL), f)
    c[:, C_ID:C_ID + 128] = np.eye(128)
    c[0:P, C_TRI:C_TRI + P] = np.triu(np.ones((P, P)), 1)
    hidden = np.triu(np.ones((P, P)), 1) * -1e38
    c[0:P, C_MASK:C_MASK + P] = hidden
    c[:, C_STEP:C_STEP + ACCROSS] = np.arange(ACCROSS) * SLOTS
    c[:, C_TILE:C_TILE + 36] = np.arange(36)
    for i, e in enumerate((16, 8)):
        c[:, C_DESC[i]:C_DESC[i] + e] = e - np.arange(e)
        c[:, C_BEF[i]:C_BEF[i] + e * e] = (np.arange(e)[:, None] > np.arange(e)[None, :]).reshape(e * e)
        c[0:P, C_TOK[i]:C_TOK[i] + T] = i * B * N + P * np.arange(T)[None, :] + np.arange(P)[:, None]
    out["consts"] = c
    return out


def kernel(**inputs):
    import numpy as _np
    import concourse.bacc as _bacc
    from concourse import mybir as _mybir
    from concourse.bass_utils import run_bass_kernel_spmd as _run

    nc = _bacc.Bacc("TRN2", target_bir_lowering=False, num_devices=1)
    arrays, args = {}, {}
    for name, v in _layouts(_np, {k: _np.asarray(v) for k, v in inputs.items()}).items():
        v = _np.ascontiguousarray(v)
        arrays[f"in_{name}"] = v
        args[name] = nc.dram_tensor(f"in_{name}", v.shape, _mybir.dt.from_np(v.dtype), kind="ExternalInput").ap()
    out = nc.dram_tensor("out_0_dram", (B, N, D), F32, kind="ExternalOutput").ap()
    build(nc, args, out)
    r = _run(nc, [arrays], core_ids=[0])
    return r.results[0]["out_0_dram"]
```
